# Optimizing a Trainium2 kernel written in Bass

```python
import numpy as np
import jax
import jax.numpy as jnp

def _softmax(x, axis=-1):
    return jax.nn.softmax(x, axis=axis)

def _gelu(x):
    return jax.nn.gelu(x, approximate=True)

def _silu(x):
    return jax.nn.silu(x)

def _sigmoid(x):
    return jax.nn.sigmoid(x)

def _layernorm(x, axis=-1, eps=1e-05):
    m = jnp.mean(x, axis=axis, keepdims=True)
    v = jnp.var(x, axis=axis, keepdims=True)
    return (x - m) / jnp.sqrt(v + eps)

def _scatter_add(tgt, idx, src, axis=0):
    return tgt.at[idx].add(src)

def _segment_sum(src, seg, n):
    return jax.ops.segment_sum(src, seg, n)
kernel_name = 'mk_xattn_ffn_d2_seqx_r2_33b522'

def setup_inputs(seed: int=0):
    np.random.seed(seed)
    _w = jnp.asarray

    def _rec_inputs():
        import jax
        import jax.numpy as jnp
        _rk = jax.random.key(seed)
        x = 7.22e-05 + 1 * jax.random.normal(jax.random.fold_in(_rk, 1), (2, 1024, 512), jnp.float32)
        _lenS = 1024 - jax.random.randint(jax.random.fold_in(_rk, 7), (2,), 0, max(1, 1024 // 4) + 1, jnp.int32)
        _lenS2 = 2048 - jax.random.randint(jax.random.fold_in(_rk, 8), (2,), 0, max(1, 2048 // 4) + 1, jnp.int32)
        _ctx_1024P = jax.random.normal(jax.random.fold_in(_rk, 11), (2, 16, 512), jnp.float32)
        _ctx_1024c = jax.random.dirichlet(jax.random.fold_in(_rk, 511), 0.3 * jnp.ones((16,), jnp.float32), (2, 2048))
        _ctx_1024t = jnp.einsum('bsk,bkd->bsd', _ctx_1024c, _ctx_1024P)
        _ctx_1024t = _ctx_1024t * jax.lax.rsqrt(jnp.mean(jnp.square(_ctx_1024t)) + 1e-12) * 0.953939
        ctx_1024 = 4.13588e-05 + 0.999923 * (_ctx_1024t + 0.3 * jax.random.normal(jax.random.fold_in(_rk, 611), (2, 2048, 512), jnp.float32))
        _validS = jnp.arange(1024)[None, :] < _lenS[:, None]
        _validS2 = jnp.arange(2048)[None, :] < _lenS2[:, None]
        _causal = jnp.tril(jnp.ones((1024, 1024), dtype=bool))
        mask_BxS2_if0 = jnp.where(jnp.ones((2, 2048), dtype=bool), 0, 1).astype(jnp.int32)
        return (x, ctx_1024, mask_BxS2_if0)
    x, ctx_1024, mask_BxS2_if0 = _rec_inputs()

    def _L0_xattn_setup():
        import jax, jax.numpy as jnp
        import numpy as np
        D_MODEL = 512
        NUM_HEADS = 16
        HEAD_DIM = D_MODEL // NUM_HEADS
        key = jax.random.key(seed)
        ks = jax.random.split(key, 10)
        B, SQ, SKV = (4, 1024, 1024)
        s = 1.0 / np.sqrt(D_MODEL)
        return {'query': jax.random.normal(ks[0], (B, SQ, D_MODEL), jnp.float32), 'key_value': jax.random.normal(ks[1], (B, SKV, D_MODEL), jnp.float32), 'Wq': jax.random.normal(ks[2], (D_MODEL, D_MODEL), jnp.float32) * s, 'bq': jnp.zeros((D_MODEL,), jnp.float32), 'Wk': jax.random.normal(ks[3], (D_MODEL, D_MODEL), jnp.float32) * s, 'bk': jnp.zeros((D_MODEL,), jnp.float32), 'Wv': jax.random.normal(ks[4], (D_MODEL, D_MODEL), jnp.float32) * s, 'bv': jnp.zeros((D_MODEL,), jnp.float32), 'Wo': jax.random.normal(ks[5], (D_MODEL, D_MODEL), jnp.float32) * s, 'bo': jnp.zeros((D_MODEL,), jnp.float32)}
    _L0_xattn_all = _L0_xattn_setup()
    _L0_xattn_in = {k: v for k, v in _L0_xattn_all.items() if k in ('Wq', 'bq', 'Wk', 'bk', 'Wv', 'bv', 'Wo', 'bo')}
    del _L0_xattn_all

    def _L0_ffn_setup():
        import jax, jax.numpy as jnp
        import numpy as np
        NUM_HEADS = 16
        TOP_K = 2
        key = jax.random.key(seed)
        ks = jax.random.split(key, 5)
        B, S, D, E = (4, 1024, 512, 8)
        scale = 0.02
        return {'x': jax.random.normal(ks[0], (B, S, D), dtype=jnp.float32), 'W_qkv': jax.random.normal(ks[1], (D, 3 * D), dtype=jnp.float32) * scale, 'b_qkv': jnp.zeros((3 * D,), dtype=jnp.float32), 'W_gate': jax.random.normal(ks[2], (D, E), dtype=jnp.float32) * scale, 'b_gate': jnp.zeros((E,), dtype=jnp.float32), 'W_experts': jax.random.normal(ks[3], (E, D, D), dtype=jnp.float32) * scale, 'b_experts': jnp.zeros((E, D), dtype=jnp.float32)}
    _L0_ffn_all = _L0_ffn_setup()
    _L0_ffn_in = {k: v for k, v in _L0_ffn_all.items() if k in ('W_qkv', 'b_qkv', 'W_gate', 'b_gate', 'W_experts', 'b_experts')}
    del _L0_ffn_all

    def _L1_xattn_setup():
        import jax, jax.numpy as jnp
        import numpy as np
        import math
        B, M, D, H, NK = (4, 1024, 512, 16, 5)
        HD = D // H

        def _gather_pad0(x, idx):
            Bx, Hx, W, hd = x.shape
            valid = (idx >= 0) & (idx < W)
            idxc = jnp.clip(idx, 0, W - 1).reshape(Bx, Hx, -1)
            g = jnp.take_along_axis(x, idxc[..., None], axis=2)
            g = g.reshape(idx.shape + (hd,))
            return g * valid[..., None].astype(x.dtype)
        key = jax.random.key(seed)
        ks = jax.random.split(key, 9)
        w = lambda k, shape: jax.random.normal(k, shape, jnp.float32) * 0.02
        return {'k': jax.random.normal(ks[0], (B, M, D), jnp.float32), 'v': jax.random.normal(ks[1], (B, M, D), jnp.float32), 'q': jax.random.normal(ks[2], (B, M, D), jnp.float32), 'mask': jnp.zeros((B, M), jnp.int32), 'Wk': w(ks[3], (D, D)), 'bk': jnp.zeros((D,), jnp.float32), 'Wv': w(ks[4], (D, D)), 'bv': jnp.zeros((D,), jnp.float32), 'Wq': w(ks[5], (D, D)), 'bq': jnp.zeros((D,), jnp.float32), 'Woff': w(ks[6], (H * NK, D)), 'boff': jnp.zeros((H * NK,), jnp.float32), 'Wo': w(ks[7], (D, D)), 'bo': jnp.zeros((D,), jnp.float32)}
    _L1_xattn_all = _L1_xattn_setup()
    _L1_xattn_in = {k: v for k, v in _L1_xattn_all.items() if k in ('Wk', 'bk', 'Wv', 'bv', 'Wq', 'bq', 'Woff', 'boff', 'Wo', 'bo')}
    del _L1_xattn_all

    def _L1_ffn_setup():
        import jax, jax.numpy as jnp
        import numpy as np
        B, S, D, H, M, E, K = (8, 1024, 512, 1024, 64, 8, 2)
        EH = H // 2

        def _layernorm(x, g, b, eps=1e-05):
            mu = jnp.mean(x, axis=-1, keepdims=True)
            var = jnp.var(x, axis=-1, keepdims=True)
            return (x - mu) * jax.lax.rsqrt(var + eps) * g + b
        key = jax.random.key(seed)
        ks = jax.random.split(key, 16)
        sc = lambda *shape: 1.0 / np.sqrt(shape[0])
        return {'inputs_embeds': jax.random.normal(ks[0], (B, S, D), jnp.float32), 'W_enc': jax.random.normal(ks[1], (D, H), jnp.float32) * sc(D), 'b_enc': jnp.zeros((H,), jnp.float32), 'W_s2c': jax.random.normal(ks[2], (H, M), jnp.float32) * sc(H), 'b_s2c': jnp.zeros((M,), jnp.float32), 'Wr': jax.random.normal(ks[3], (M, E), jnp.float32) * sc(M), 'br': jnp.zeros((E,), jnp.float32), 'W1': jax.random.normal(ks[4], (E, M, EH), jnp.float32) * sc(M), 'b1': jnp.zeros((E, EH), jnp.float32), 'W2': jax.random.normal(ks[5], (E, EH, M), jnp.float32) * sc(EH), 'b2': jnp.zeros((E, M), jnp.float32), 'W_c2s': jax.random.normal(ks[6], (M, H), jnp.float32) * sc(M), 'b_c2s': jnp.zeros((H,), jnp.float32), 'W_dec': jax.random.normal(ks[7], (H, D), jnp.float32) * sc(H), 'b_dec': jnp.zeros((D,), jnp.float32), 'ln_g': jnp.ones((D,), jnp.float32), 'ln_b': jnp.zeros((D,), jnp.float32)}
    _L1_ffn_all = _L1_ffn_setup()
    _L1_ffn_in = {k: v for k, v in _L1_ffn_all.items() if k in ('W_enc', 'b_enc', 'W_s2c', 'b_s2c', 'Wr', 'br', 'W1', 'b1', 'W2', 'b2', 'W_c2s', 'b_c2s', 'W_dec', 'b_dec', 'ln_g', 'ln_b')}
    del _L1_ffn_all
    return {'x': x, 'ctx_1024': ctx_1024, 'mask_BxS2_if0': mask_BxS2_if0, 'L0_xattn_Wq': _L0_xattn_in['Wq'], 'L0_xattn_bq': _L0_xattn_in['bq'], 'L0_xattn_Wk': _L0_xattn_in['Wk'], 'L0_xattn_bk': _L0_xattn_in['bk'], 'L0_xattn_Wv': _L0_xattn_in['Wv'], 'L0_xattn_bv': _L0_xattn_in['bv'], 'L0_xattn_Wo': _L0_xattn_in['Wo'], 'L0_xattn_bo': _L0_xattn_in['bo'], 'L0_ffn_W_qkv': _L0_ffn_in['W_qkv'], 'L0_ffn_b_qkv': _L0_ffn_in['b_qkv'], 'L0_ffn_W_gate': _L0_ffn_in['W_gate'], 'L0_ffn_b_gate': _L0_ffn_in['b_gate'], 'L0_ffn_W_experts': _L0_ffn_in['W_experts'], 'L0_ffn_b_experts': _L0_ffn_in['b_experts'], 'L1_xattn_Wk': _L1_xattn_in['Wk'], 'L1_xattn_bk': _L1_xattn_in['bk'], 'L1_xattn_Wv': _L1_xattn_in['Wv'], 'L1_xattn_bv': _L1_xattn_in['bv'], 'L1_xattn_Wq': _L1_xattn_in['Wq'], 'L1_xattn_bq': _L1_xattn_in['bq'], 'L1_xattn_Woff': _L1_xattn_in['Woff'], 'L1_xattn_boff': _L1_xattn_in['boff'], 'L1_xattn_Wo': _L1_xattn_in['Wo'], 'L1_xattn_bo': _L1_xattn_in['bo'], 'L1_ffn_W_enc': _L1_ffn_in['W_enc'], 'L1_ffn_b_enc': _L1_ffn_in['b_enc'], 'L1_ffn_W_s2c': _L1_ffn_in['W_s2c'], 'L1_ffn_b_s2c': _L1_ffn_in['b_s2c'], 'L1_ffn_Wr': _L1_ffn_in['Wr'], 'L1_ffn_br': _L1_ffn_in['br'], 'L1_ffn_W1': _L1_ffn_in['W1'], 'L1_ffn_b1': _L1_ffn_in['b1'], 'L1_ffn_W2': _L1_ffn_in['W2'], 'L1_ffn_b2': _L1_ffn_in['b2'], 'L1_ffn_W_c2s': _L1_ffn_in['W_c2s'], 'L1_ffn_b_c2s': _L1_ffn_in['b_c2s'], 'L1_ffn_W_dec': _L1_ffn_in['W_dec'], 'L1_ffn_b_dec': _L1_ffn_in['b_dec'], 'L1_ffn_ln_g': _L1_ffn_in['ln_g'], 'L1_ffn_ln_b': _L1_ffn_in['ln_b']}

def reference(x, ctx_1024, mask_BxS2_if0, L0_xattn_Wq, L0_xattn_bq, L0_xattn_Wk, L0_xattn_bk, L0_xattn_Wv, L0_xattn_bv, L0_xattn_Wo, L0_xattn_bo, L0_ffn_W_qkv, L0_ffn_b_qkv, L0_ffn_W_gate, L0_ffn_b_gate, L0_ffn_W_experts, L0_ffn_b_experts, L1_xattn_Wk, L1_xattn_bk, L1_xattn_Wv, L1_xattn_bv, L1_xattn_Wq, L1_xattn_bq, L1_xattn_Woff, L1_xattn_boff, L1_xattn_Wo, L1_xattn_bo, L1_ffn_W_enc, L1_ffn_b_enc, L1_ffn_W_s2c, L1_ffn_b_s2c, L1_ffn_Wr, L1_ffn_br, L1_ffn_W1, L1_ffn_b1, L1_ffn_W2, L1_ffn_b2, L1_ffn_W_c2s, L1_ffn_b_c2s, L1_ffn_W_dec, L1_ffn_b_dec, L1_ffn_ln_g, L1_ffn_ln_b):
    import jax
    import jax.numpy as jnp

    def _L0_xattn_ref(query, key_value, Wq, bq, Wk, bk, Wv, bv, Wo, bo):
        import jax, jax.numpy as jnp
        import numpy as np
        D_MODEL = 512
        NUM_HEADS = 16
        HEAD_DIM = D_MODEL // NUM_HEADS
        B, SQ, _ = query.shape
        SKV = key_value.shape[1]
        H, Dh = (NUM_HEADS, HEAD_DIM)
        Q = (query @ Wq.T + bq).reshape(B, SQ, H, Dh).transpose(0, 2, 1, 3)
        K = (key_value @ Wk.T + bk).reshape(B, SKV, H, Dh).transpose(0, 2, 1, 3)
        V = (key_value @ Wv.T + bv).reshape(B, SKV, H, Dh).transpose(0, 2, 1, 3)
        scale = jnp.asarray(np.sqrt(Dh), query.dtype)
        scores = jnp.einsum('bhqd,bhkd->bhqk', Q, K) / scale
        weights = jax.nn.softmax(scores, axis=-1)
        attn = jnp.einsum('bhqk,bhkd->bhqd', weights, V)
        attn = attn.transpose(0, 2, 1, 3).reshape(B, SQ, H * Dh)
        return attn @ Wo.T + bo

    def _L0_ffn_ref(x, W_qkv, b_qkv, W_gate, b_gate, W_experts, b_experts):
        import jax, jax.numpy as jnp
        import numpy as np
        NUM_HEADS = 16
        TOP_K = 2
        B, S, D = x.shape
        H = NUM_HEADS
        hd = D // H
        E = W_gate.shape[-1]
        qkv = (x @ W_qkv + b_qkv).reshape(B, S, 3, H, hd)
        q, k, v = (qkv[:, :, 0], qkv[:, :, 1], qkv[:, :, 2])
        attn = jnp.einsum('bqhd,bkhd->bhqk', q, k) / jnp.sqrt(jnp.asarray(hd, x.dtype))
        attn = jax.nn.softmax(attn, axis=-1)
        attn_out = jnp.einsum('bhqk,bkhd->bqhd', attn, v).reshape(B, S, D)
        gate = jax.nn.softmax(x @ W_gate + b_gate, axis=-1)
        top_g, top_i = jax.lax.top_k(gate, TOP_K)
        combine = jnp.sum(jax.nn.one_hot(top_i, E, dtype=x.dtype) * top_g[..., None], axis=2)
        expert_out = jnp.einsum('bsd,edf->bsef', x, W_experts) + b_experts
        moe_out = jnp.einsum('bsef,bse->bsf', expert_out, combine)
        return attn_out + moe_out

    def _L1_xattn_ref(k, v, q, mask, Wk, bk, Wv, bv, Wq, bq, Woff, boff, Wo, bo):
        import jax, jax.numpy as jnp
        import numpy as np
        import math
        B, M, D, H, NK = (4, 1024, 512, 16, 5)
        HD = D // H

        def _gather_pad0(x, idx):
            Bx, Hx, W, hd = x.shape
            valid = (idx >= 0) & (idx < W)
            idxc = jnp.clip(idx, 0, W - 1).reshape(Bx, Hx, -1)
            g = jnp.take_along_axis(x, idxc[..., None], axis=2)
            g = g.reshape(idx.shape + (hd,))
            return g * valid[..., None].astype(x.dtype)
        Bq, Q, _ = q.shape
        key_len = k.shape[1]
        K = jnp.einsum('bmd,ed->bme', k, Wk) + bk
        V = jnp.einsum('bmd,ed->bme', v, Wv) + bv
        Qp = jnp.einsum('bqd,ed->bqe', q, Wq) + bq
        off = jnp.einsum('bqd,ed->bqe', Qp, Woff) + boff
        off = off.reshape(Bq, Q, H, NK).transpose(0, 2, 1, 3)
        Kh = K.reshape(Bq, key_len, H, HD).transpose(0, 2, 1, 3)
        Vh = V.reshape(Bq, key_len, H, HD).transpose(0, 2, 1, 3)
        Qh = Qp.reshape(Bq, Q, H, HD).transpose(0, 2, 1, 3)
        loc = jnp.arange(Q, dtype=jnp.float32)[:, None]
        left = -NK // 2
        ref = jnp.arange(left, NK + left, dtype=jnp.float32)
        sign_lens = (1 - mask).sum(-1).astype(jnp.float32) - 1.0
        loc_x = jnp.mod(ref + off + loc, sign_lens[:, None, None, None])
        xg = loc_x / (key_len - 1) * 2.0 - 1.0
        ix = ((xg + 1.0) * key_len - 1.0) / 2.0
        x0 = jnp.floor(ix)
        dx = ix - x0
        i0 = x0.astype(jnp.int32)
        i1 = i0 + 1
        w0 = (1.0 - dx)[..., None]
        w1 = dx[..., None]
        sk = 0.5 * (w0 * _gather_pad0(Kh, i0) + w1 * _gather_pad0(Kh, i1))
        sv = 0.5 * (w0 * _gather_pad0(Vh, i0) + w1 * _gather_pad0(Vh, i1))
        scores = jnp.einsum('bhqd,bhqkd->bhqk', Qh / math.sqrt(HD), sk)
        attn = jax.nn.softmax(scores, axis=-1)
        ctx = jnp.einsum('bhqk,bhqkd->bhqd', attn, sv)
        ctx = ctx.transpose(0, 2, 1, 3).reshape(Bq, Q, H * HD)
        return jnp.einsum('bqd,ed->bqe', ctx, Wo) + bo

    def _L1_ffn_ref(inputs_embeds, W_enc, b_enc, W_s2c, b_s2c, Wr, br, W1, b1, W2, b2, W_c2s, b_c2s, W_dec, b_dec, ln_g, ln_b):
        import jax, jax.numpy as jnp
        import numpy as np
        B, S, D, H, M, E, K = (8, 1024, 512, 1024, 64, 8, 2)
        EH = H // 2

        def _layernorm(x, g, b, eps=1e-05):
            mu = jnp.mean(x, axis=-1, keepdims=True)
            var = jnp.var(x, axis=-1, keepdims=True)
            return (x - mu) * jax.lax.rsqrt(var + eps) * g + b
        b, s, d = inputs_embeds.shape
        spikes_enc = jax.nn.sigmoid(inputs_embeds @ W_enc + b_enc)
        flat = spikes_enc.reshape(b * s, -1)
        cont = flat @ W_s2c + b_s2c
        probs = jax.nn.softmax(cont @ Wr + br, axis=-1)
        topk_w, topk_idx = jax.lax.top_k(probs, K)
        topk_w = topk_w / jnp.sum(topk_w, axis=-1, keepdims=True)
        gate = jnp.sum(jax.nn.one_hot(topk_idx, E, dtype=cont.dtype) * topk_w[..., None], axis=1)
        h = jax.nn.relu(jnp.einsum('tm,emh->eth', cont, W1) + b1[:, None, :])
        y = jnp.einsum('eth,ehm->etm', h, W2) + b2[:, None, :]
        expert_out = jnp.einsum('etm,te->tm', y, gate)
        spikes_moe = jax.nn.sigmoid(expert_out @ W_c2s + b_c2s)
        spikes_moe = spikes_moe.reshape(b, s, -1)
        decoded = spikes_moe @ W_dec + b_dec
        return _layernorm(decoded, ln_g, ln_b)
    x = x + _L0_xattn_ref(_layernorm(x, axis=-1), ctx_1024, L0_xattn_Wq, L0_xattn_bq, L0_xattn_Wk, L0_xattn_bk, L0_xattn_Wv, L0_xattn_bv, L0_xattn_Wo, L0_xattn_bo)
    x = x + _L0_ffn_ref(_layernorm(x, axis=-1), L0_ffn_W_qkv, L0_ffn_b_qkv, L0_ffn_W_gate, L0_ffn_b_gate, L0_ffn_W_experts, L0_ffn_b_experts)
    x = x + _L1_xattn_ref(ctx_1024, ctx_1024, _layernorm(x, axis=-1), mask_BxS2_if0, L1_xattn_Wk, L1_xattn_bk, L1_xattn_Wv, L1_xattn_bv, L1_xattn_Wq, L1_xattn_bq, L1_xattn_Woff, L1_xattn_boff, L1_xattn_Wo, L1_xattn_bo)
    x = x + _L1_ffn_ref(_layernorm(x, axis=-1), L1_ffn_W_enc, L1_ffn_b_enc, L1_ffn_W_s2c, L1_ffn_b_s2c, L1_ffn_Wr, L1_ffn_br, L1_ffn_W1, L1_ffn_b1, L1_ffn_W2, L1_ffn_b2, L1_ffn_W_c2s, L1_ffn_b_c2s, L1_ffn_W_dec, L1_ffn_b_dec, L1_ffn_ln_g, L1_ffn_ln_b)
    return x

_drawn_inputs = setup_inputs


def setup_inputs(seed=0):
    import zlib

    import numpy as np

    out = dict(_drawn_inputs(seed))
    spreads = {'L0_xattn_bq': (0.0, 0.457),
     'L0_xattn_bk': (0.0, 0.8),
     'L0_xattn_bv': (0.0, 0.1),
     'L0_xattn_bo': (0.0, 0.1),
     'L0_ffn_b_qkv': (0.0, 0.1),
     'L0_ffn_b_gate': (0.0, 0.308),
     'L0_ffn_b_experts': (0.0, 0.409),
     'L1_xattn_bk': (0.0, 0.8),
     'L1_xattn_bv': (0.0, 0.453),
     'L1_xattn_bq': (0.0, 0.8),
     'L1_xattn_boff': (0.0, 0.8),
     'L1_xattn_bo': (0.0, 0.1),
     'L1_ffn_b_enc': (0.0, 0.61),
     'L1_ffn_b_s2c': (0.0, 0.1),
     'L1_ffn_br': (0.0, 0.1),
     'L1_ffn_b1': (0.0, 0.567),
     'L1_ffn_b2': (0.0, 0.355),
     'L1_ffn_b_c2s': (0.0, 0.272),
     'L1_ffn_b_dec': (0.0, 0.1),
     'L1_ffn_ln_g': (1.0, 0.2),
     'L1_ffn_ln_b': (0.0, 0.1)}
    factors = {'L1_xattn_Wk': 8.0, 'L1_xattn_Wq': 7.857, 'L1_xattn_Woff': 7.97}
    for name, (base, spread) in spreads.items():
        noise = np.random.default_rng([zlib.crc32(name.encode()), seed]).standard_normal(out[name].shape)
        drawn = base * np.exp(spread * noise) if base else spread * noise
        out[name] = jnp.asarray(drawn.astype(out[name].dtype))
    for name, factor in factors.items():
        out[name] = (out[name] * factor).astype(out[name].dtype)
    return out
```

```python
from contextlib import ExitStack

import concourse.bass as bass
from concourse import mybir

F32 = mybir.dt.float32
F32R = mybir.dt.float32r
BF16 = mybir.dt.bfloat16
I32 = mybir.dt.int32
ALU = mybir.AluOpType
ACT = mybir.ActivationFunctionType
X = mybir.AxisListType.X

P = 128
B, S, T, D = 2, 1024, 2048, 512
H, HD = 16, 32
C = D // P
G = 512
TT = G // P
NK5 = 5
NS = H * NK5
ROWS = T + 4
PAIR = 2 * HD
E0 = 8
HID, MM, EH, E1 = 1024, 64, 512, 8
V1 = HD + 1
EPS = 1e-5
SCALE = float(HD) ** -0.5


class Steps:

    def __init__(self, eng, sem, per):
        self.eng, self.sem, self.per = eng, sem, per

    def begin(self, it):
        self.it, self.k = it, 0

    def did(self, ins):
        ins.then_inc(self.sem, 1)
        self.k += 1
        return ins

    def settle(self):
        self.eng.wait_ge(self.sem, self.it * self.per + self.k)

    def end(self):
        assert self.k == self.per, f"{self.k} steps, not {self.per}"


class Tools:
    def __init__(self, nc, ctx, tag):
        self.nc, self.ctx, self.tag, self.own = nc, ctx, tag, []

    def sb(self, name, shape, dt=F32):
        return self.ctx.enter_context(self.nc.sbuf_tensor(f"{self.tag}_{name}", shape, dt))

    def ps(self, name, shape, dt=F32):
        return self.ctx.enter_context(self.nc.psum_tensor(f"{self.tag}_{name}", shape, dt))

    def sem(self, name):
        self.own.append(self.nc.alloc_semaphore(f"{self.tag}_{name}"))
        return self.own[-1]

    def sems(self, name, n):
        return [self.sem(f"{name}{i}") for i in range(n)]


    def block(self):
        self.ctx.callback(self.retire)
        return self.ctx.enter_context(self.nc.Block())

    def retire(self):
        self.nc.clear_and_free_semaphores(self.own)
        self.nc.all_engine_barrier()


def row_of(vec, n):
    return bass.AP(vec.tensor, vec.offset, [[0, P], [1, n]])


def layer_norm(steps, eng, passed, x, out, stats, mv, rstd):
    var, half, y, sq = (rstd[:, i, :] for i in range(4))
    for t in range(TT):
        steps.did(eng.bn_stats(stats[:, t, :], x[:, t, :]))
    steps.settle()
    eng.sem_inc(passed, 1)
    for t in range(TT):
        steps.did(eng.bn_aggr(mv[:, t, :], stats[:, t, :]))
    steps.settle()
    steps.did(eng.tensor_scalar(var, mv[:, :, 1], EPS, None, ALU.add))
    steps.settle()
    steps.did(eng.tensor_scalar(y.bitcast(I32), var.bitcast(I32), 1, None, ALU.logical_shift_right))
    steps.did(eng.tensor_scalar(half, var, -0.5, None, ALU.mult))
    steps.settle()
    steps.did(eng.tensor_scalar(y.bitcast(I32), y.bitcast(I32), -1.0, float(0x5F3759DF), ALU.mult, ALU.add))
    steps.settle()
    for _ in range(3):
        steps.did(eng.tensor_tensor(sq, y, y, ALU.mult))
        steps.settle()
        steps.did(eng.tensor_tensor(sq, sq, half, ALU.mult))
        steps.settle()
        steps.did(eng.scalar_tensor_tensor(out=y, in0=sq, scalar=1.5, in1=y, op0=ALU.add, op1=ALU.mult))
        steps.settle()
    for t in range(TT):
        steps.did(eng.tensor_scalar(out[:, t, :], x[:, t, :], mv[:, t, 0:1], y[:, t:t + 1],
                                    ALU.subtract, ALU.mult))
    steps.settle()


def constants(nc, ident, identb, ahead):
    with ExitStack() as ctx:
        t = Tools(nc, ctx, "const")
        made = t.sem("made")
        passed = t.sems("passed", 4)
        block = t.block()

        @block.gpsimd
        def _(pool):
            pool.memset(ident[:, :], 0.0).then_inc(made, 1)
            pool.memset(identb[:, :], 0.0).then_inc(made, 1)
            pool.memset(ahead[:, :, :], 0.0).then_inc(made, 1)
            pool.wait_ge(made, 3)
            for m in (ident, identb):
                pool.affine_select(out=m[:, :], in_=m[:, :], compare_op=ALU.not_equal, fill=1.0, base=0,
                                   pattern=[[-1, P]], channel_multiplier=1).then_inc(made, 1)
            pool.affine_select(out=ahead[:, :, :], in_=ahead[:, :, :], compare_op=ALU.is_ge, fill=1.0, base=0,
                               pattern=[[-1, E0], [1, E0]], channel_multiplier=0).then_inc(made, 1)
            pool.wait_ge(made, 6)


def project_context(nc, ctxT, wkT0, bk0, wvT0, bv0, wkT1, bk1, wvT1, bv1, k_hi, k_lo, v_ones, tables):
    NG = B * T // G
    with ExitStack() as ctx:
        t = Tools(nc, ctx, "ctx")
        w = [t.sb(f"w{i}", [P, C, D]) for i in range(4)]
        bk0_c = t.sb("bk0_c", [P, C])
        rows = t.sb("rows", [P, 3, D])
        x = t.sb("x", [P, 2, C, G])
        kh = t.sb("kh", [P, 2, C, G], F32R)
        kl = t.sb("kl", [P, 2, C, G], F32R)
        vo = t.sb("vo", [P, 2, TT, H, V1])
        kv = t.sb("kv", [P, 2, TT, H, 2, HD])
        zero = t.sb("zero", [H, 2 * PAIR])
        R = 8
        bank = [t.ps(f"bank{i}", [P, G]) for i in range(R)]
        w_in = t.sem("w_in")
        x_in, x_used = t.sems("x_in", 2), t.sems("x_used", 2)
        full, free = t.sems("full", R), t.sems("free", R)
        hi_done, out_ready = t.sem("hi_done"), t.sem("out_ready")
        stored, preset, zeroed, zeros_out = t.sems("stored", 2), t.sem("preset"), t.sem("zeroed"), t.sem("zeros_out")
        ND = 2 + 1 + TT
        N = 4 * TT
        passed = t.sems("passed", 4)
        block = t.block()

        @block.sync
        def _(sp):
            for i, src in enumerate((wkT0, wvT0, wkT1, wvT1)):
                sp.dma_start(w[i][:, :, :], src.rearrange("(c p) n -> p c n", p=P)).then_inc(w_in, 16)
            sp.dma_start(bk0_c[:, :], bk0.rearrange("(c p) -> p c", p=P), allow_slow_non_contiguous=True).then_inc(w_in, 16)
            for i, src in enumerate((bv0, bk1, bv1)):
                sp.dma_start(rows[:, i, :], row_of(src, D)).then_inc(w_in, 16)
            xs = ctxT.rearrange("(c p) t -> p c t", p=P)
            with sp.Fori(0, NG // 2) as j:
                for u in range(2):
                    sp.wait_ge(x_used[u], j)
                    sp.sem_inc(passed[0], 1)
                    sp.dma_start(x[:, u, :, :], xs[:, :, bass.ds((2 * j + u) * G, G)]).then_inc(x_in[u], 16)

        @block.tensor
        def _(pe):
            pe.wait_ge(w_in, 16 * 8)
            with pe.Fori(0, NG // 2) as j:
                for u in range(2):
                    pe.wait_ge(x_in[u], 16 * j + 16)
                    for k in range(N):
                        kind, o = divmod(k, TT)
                        pe.wait_ge(free[k % R], (2 * j + u) * (N // R) + k // R)
                        for c in range(C):
                            if kind == 0:
                                mm = pe.matmul(bank[k % R][:, :], w[0][:, c, o * P:(o + 1) * P], x[:, u, c, :],
                                               start=(c == 0), stop=(c == C - 1))
                            else:
                                mm = pe.matmul(bank[k % R][:, :], x[:, u, c, o * P:(o + 1) * P], w[kind][:, c, :],
                                               start=(c == 0), stop=(c == C - 1))
                        mm.then_inc(full[k % R], 1)
                    pe.wait_ge(full[(N - 1) % R], (2 * j + u + 1) * (N // R))
                    pe.sem_inc(x_used[u], 1)

        @block.scalar
        def _(act):
            act.wait_ge(w_in, 16 * 8)
            with act.Fori(0, NG // 2) as j:
                for u in range(2):
                    act.wait_ge(stored[u], 16 * ND * j)
                    for o in range(C):
                        act.wait_ge(full[o % R], (2 * j + u) * (N // R) + o // R + 1)
                        act.activation(kh[:, u, o, :], bank[o % R][:, :], ACT.Identity,
                                       bias=bk0_c[:, o:o + 1]).then_inc(hi_done, 1)

        @block.vector
        def _(dve):
            dve.memset(vo[:, :, :, :, HD:V1], 1.0).then_inc(preset, 1)
            dve.wait_ge(preset, 1)
            dve.wait_ge(w_in, 16 * 8)
            with dve.Fori(0, NG // 2) as j:
                for u in range(2):
                    dve.wait_ge(stored[u], 16 * ND * j)
                    for k in range(N):
                        kind, o = divmod(k, TT)
                        dve.wait_ge(full[k % R], (2 * j + u) * (N // R) + k // R + 1)
                        if kind == 0:
                            dve.wait_ge(hi_done, (2 * j + u) * C + o + 1)
                            ins = dve.scalar_tensor_tensor(out=kl[:, u, o, :], in0=bank[k % R][:, :],
                                                           scalar=bk0_c[:, o:o + 1], in1=kh[:, u, o, :].bitcast(F32),
                                                           op0=ALU.add, op1=ALU.subtract)
                        else:
                            src = bank[k % R][:, :].rearrange("p (h d) -> p h d", h=H)
                            add = rows[:, kind - 1, :].rearrange("p (h d) -> p h d", h=H)
                            dst = vo[:, u, o, :, 0:HD] if kind == 1 else kv[:, u, o, :, kind - 2, :]
                            ins = dve.tensor_tensor(dst, src, add, ALU.add)
                        ins.then_inc(free[k % R], 1)
                    dve.wait_ge(free[(N - 1) % R], (2 * j + u + 1) * (N // R))
                    dve.sem_inc(out_ready, 1)

        @block.gpsimd
        def _(pool):
            pool.memset(zero[:, :], 0.0).then_inc(zeroed, 1)
            pool.wait_ge(zeroed, 1)
            for tab in tables:
                rv = tab.rearrange("(h r d) -> h r d", h=H, r=ROWS)
                pool.dma_start(rv[:, 0:2, :], zero[:, :].rearrange("h (r d) -> h r d", r=2)).then_inc(zeros_out, 16)
                pool.dma_start(rv[:, T + 2:ROWS, :], zero[:, :].rearrange("h (r d) -> h r d", r=2)).then_inc(zeros_out, 16)
            for b in range(B):
                tab = tables[b].rearrange("(h r d) -> r h d", h=H, r=ROWS)
                with pool.Fori(0, NG // B // 2) as j:
                    for u in range(2):
                        g = (NG // B) * b + 2 * j + u
                        pool.wait_ge(out_ready, g + 1)
                        pool.sem_inc(passed[1], 1)
                        done = stored[u]
                        hi = k_hi.rearrange("(g c p) t -> g p c t", c=C, p=P)
                        lo = k_lo.rearrange("(g c p) t -> g p c t", c=C, p=P)
                        pool.dma_start(hi[bass.ds(g, 1), :, :, :].rearrange("a p c t -> (a p) c t").bitcast(F32),
                                       kh[:, u, :, :].bitcast(F32)).then_inc(done, 16)
                        pool.dma_start(lo[bass.ds(g, 1), :, :, :].rearrange("a p c t -> (a p) c t").bitcast(F32),
                                       kl[:, u, :, :].bitcast(F32)).then_inc(done, 16)
                        vd = v_ones.rearrange("(n p) f -> p n f", p=P)
                        pool.dma_start(vd[:, bass.ds(g * TT, TT), :],
                                       vo[:, u, :, :, :].rearrange("p n h d -> p n (h d)")).then_inc(done, 16)
                        for o in range(TT):
                            pool.dma_start(tab[bass.ds((2 * j + u) * G + (o * P + 2), P), :, :],
                                           kv[:, u, o, :, :, :].rearrange("p h a d -> p h (a d)")).then_inc(done, 16)
            for u in range(2):
                pool.wait_ge(stored[u], 16 * ND * (NG // 2))
            pool.wait_ge(zeros_out, 16 * 2 * B)


def project_query(nc, x_dram, wqT, bq, ident, q_hi, q_lo):
    NG = B * S // G
    with ExitStack() as ctx:
        t = Tools(nc, ctx, "qry")
        w = t.sb("w", [P, C, D])
        bq_c = t.sb("bq_c", [P, C])
        x = t.sb("x", [P, 2, TT, D])
        ln = t.sb("ln", [P, 2, TT, D])
        lnT = t.sb("lnT", [P, 2, C, G])
        stats, mv, rstd = t.sb("stats", [P, TT, 6]), t.sb("mv", [P, TT, 2]), t.sb("rstd", [P, 4, TT])
        qh = t.sb("qh", [P, 2, C, G], F32R)
        ql = t.sb("ql", [P, 2, C, G], F32R)
        tb = [t.ps(f"tb{i}", [P, G]) for i in range(4)]
        qb = [t.ps(f"qb{i}", [P, G]) for i in range(4)]
        w_in, x_in, x_used = t.sem("w_in"), t.sems("x_in", 2), t.sem("x_used")
        dsem, ln_done, t_full, t_out = t.sem("dve_steps"), t.sem("ln_done"), t.sem("t_full"), t.sem("t_out")
        q_full, hi_done, lo_done = t.sem("q_full"), t.sem("hi_done"), t.sem("lo_done")
        stored = t.sems("stored", 2)
        passed = t.sems("passed", 4)
        block = t.block()

        @block.sync
        def _(sp):
            sp.dma_start(w[:, :, :], wqT.rearrange("(c p) n -> p c n", p=P)).then_inc(w_in, 16)
            sp.dma_start(bq_c[:, :], bq.rearrange("(c p) -> p c", p=P), allow_slow_non_contiguous=True).then_inc(w_in, 16)
            xs = x_dram.rearrange("(n p) d -> p n d", p=P)
            with sp.Fori(0, NG // 2) as j:
                for u in range(2):
                    sp.wait_ge(ln_done, 2 * j)
                    sp.sem_inc(passed[0], 1)
                    sp.dma_start(x[:, u, :, :], xs[:, bass.ds((2 * j + u) * TT, TT), :]).then_inc(x_in[u], 16)

        @block.vector
        def _(dve):
            steps = Steps(dve, dsem, 25)
            dve.wait_ge(w_in, 32)
            with dve.Fori(0, NG // 2) as j:
                for u in range(2):
                    g = 2 * j + u
                    steps.begin(g)
                    dve.wait_ge(x_in[u], 16 * j + 16)
                    dve.wait_ge(t_full, 2 * C * j)
                    layer_norm(steps, dve, passed[3], x[:, u, :, :], ln[:, u, :, :], stats, mv, rstd)
                    steps.end()
                    dve.sem_inc(ln_done, 1)
                    dve.wait_ge(stored[u], 32 * j)
                    for o in range(C):
                        dve.wait_ge(q_full, g * C + o + 1)
                        dve.wait_ge(hi_done, g * C + o + 1)
                        dve.scalar_tensor_tensor(out=ql[:, u, o, :], in0=qb[o][:, :], scalar=bq_c[:, o:o + 1],
                                                 in1=qh[:, u, o, :].bitcast(F32), op0=ALU.add,
                                                 op1=ALU.subtract).then_inc(lo_done, 1)

        @block.tensor
        def _(pe):
            pe.wait_ge(w_in, 32)
            with pe.Fori(0, NG // 2) as j:
                for u in range(2):
                    g = 2 * j + u
                    pe.wait_ge(ln_done, g + 1)
                    pe.wait_ge(t_out, g * C)
                    for c in range(C):
                        for n in range(TT):
                            mm = pe.transpose(tb[c][:, n * P:(n + 1) * P], ln[:, u, n, c * P:(c + 1) * P], ident[:, :])
                        mm.then_inc(t_full, 1)
                    pe.wait_ge(t_out, g * C + C)
                    pe.wait_ge(lo_done, g * C)
                    for o in range(C):
                        for c in range(C):
                            mm = pe.matmul(qb[o][:, :], w[:, c, o * P:(o + 1) * P], lnT[:, u, c, :],
                                           start=(c == 0), stop=(c == C - 1))
                        mm.then_inc(q_full, 1)

        @block.scalar
        def _(act):
            act.wait_ge(w_in, 32)
            with act.Fori(0, NG // 2) as j:
                for u in range(2):
                    g = 2 * j + u
                    act.wait_ge(q_full, 2 * C * j)
                    for c in range(C):
                        act.wait_ge(t_full, g * C + c + 1)
                        act.copy(lnT[:, u, c, :], tb[c][:, :]).then_inc(t_out, 1)
                    act.wait_ge(stored[u], 32 * j)
                    for o in range(C):
                        act.wait_ge(q_full, g * C + o + 1)
                        act.activation(qh[:, u, o, :], qb[o][:, :], ACT.Identity,
                                       bias=bq_c[:, o:o + 1]).then_inc(hi_done, 1)

        @block.gpsimd
        def _(pool):
            hi = q_hi.rearrange("(g c p) t -> g p c t", c=C, p=P)
            lo = q_lo.rearrange("(g c p) t -> g p c t", c=C, p=P)
            with pool.Fori(0, NG // 2) as j:
                for u in range(2):
                    g = 2 * j + u
                    pool.wait_ge(lo_done, g * C + C)
                    pool.sem_inc(passed[1], 1)
                    for dst, src in ((hi, qh), (lo, ql)):
                        pool.dma_start(dst[bass.ds(g, 1), :, :, :].rearrange("a p c t -> (a p) c t").bitcast(F32),
                                       src[:, u, :, :].bitcast(F32)).then_inc(stored[u], 16)
            for u in range(2):
                pool.wait_ge(stored[u], 32 * (NG // 2))


def attention(nc, tag, TK, q_hi, q_lo, k_hi, k_lo, v_ones, ident, identb, out):
    NK = TK // P
    QG, KG = S // G, TK // G
    WA = 1024
    NKC = TK // WA
    NA = (S // P) * NKC
    NQ = S // P
    HALF = S // 2
    HU = 4
    NH = B * H
    PR = 4
    R = 4
    EARLY = 3
    assert NA == NK
    units = [[(1, s + EARLY)] if s + EARLY <= NA else [(2, s + EARLY - NA - 1)] for s in range(NK)]
    units[NK - 1].append((2, EARLY - 1))
    assert units[NK - 2] == [(2, 0)] and units[NK - 1] == [(2, 1), (2, 2)]
    with ExitStack() as ctx:
        t = Tools(nc, ctx, tag)
        kst = [t.sb(f"kst{i}", [P, TK], F32R) for i in range(HU)]
        qst = [t.sb(f"qst{i}", [P, S], F32R) for i in range(HU)]
        v = [t.sb(f"v{i}", [P, NK, V1]) for i in range(HU)]
        p = [t.sb(f"p{i}", [P, S]) for i in range(PR)]
        oT = [t.sb(f"oT{i}", [P, HALF]) for i in range(2)]
        o = [t.sb(f"o{i}", [P, NQ, HD]) for i in range(2)]
        inv = [t.sb(f"inv{i}", [P, NQ // 2, 2, 1]) for i in range(2)]
        mx = t.sb("mx", [P, NA])
        negm = t.sb("negm", [P, NQ], BF16)
        ps_a = t.ps("ps_a", [P, WA])
        ps_b = [t.ps(f"ps_b{i}", [P, S]) for i in range(2)]
        ps_o = [t.ps(f"ps_o{i}", [P, HALF]) for i in range(2)]
        preset, loaded, head_used = t.sem("preset"), t.sems("loaded", HU), t.sems("head_used", HU)
        a_full, a_free, negm_done = t.sem("a_full"), t.sem("a_free"), t.sem("negm_done")
        b_full, exp_done, p_used = t.sems("b_full", 2), t.sems("exp_done", 2), t.sems("p_used", PR)
        o_full, oT_done, turned = t.sems("o_full", 2), t.sems("oT_done", 2), t.sems("turned", 2)
        o_done, o_free, o_out, inv_done = t.sems("o_done", 2), t.sems("o_free", 2), t.sems("o_out", 2), t.sem("inv_done")
        stored = t.sems("stored", 2)
        LOADS = 7
        passed = t.sems("passed", 4)
        block = t.block()

        @block.sync
        def _(sp):
            for u in range(HU):
                sp.sem_inc(head_used[u], 1)
            qh = q_hi.rearrange("(b g r) t -> b r g t", b=B, g=QG)
            ql = q_lo.rearrange("(b g r) t -> b r g t", b=B, g=QG)
            kh = k_hi.rearrange("(b g r) t -> b r g t", b=B, g=KG)
            kl = k_lo.rearrange("(b g r) t -> b r g t", b=B, g=KG)
            vs = v_ones.rearrange("(b n p) f -> b p n f", b=B, p=P)
            for b in range(B):
                with sp.Fori(0, H // HU) as j:
                    for u in range(HU):
                        sp.wait_ge(head_used[u], j + (b * (H // HU) + 1))
                        sp.sem_inc(passed[0], 1)
                        h = j * HU + u
                        for i, (part, full) in enumerate(((qh, qst), (qh, qst), (ql, qst), (kh, kst), (kl, kst), (kh, kst))):
                            r = HD * (i % 3)
                            dst = full[u][r:r + HD, :].rearrange("r (g t) -> r g t", t=G)
                            sp.dma_start(dst.bitcast(F32), part[b, bass.ds(h * HD, HD), :, :].bitcast(F32)).then_inc(loaded[u], 16)
                        sp.dma_start(v[u][:, :, :], vs[b, :, :, bass.ds(h * V1, V1)]).then_inc(loaded[u], 16)

        def turns(j, u, left, step, end):
            for s in range(R, NK):
                step(j, u, s, left)
            if left != 0:
                nj, nu = (j, u + 1) if u + 1 < HU else (j + 1, 0)
                for s in range(R):
                    step(nj, nu, s, None if left is None else left - 1)
            else:
                step(j, u, NK, 0)
            end(j, u)

        def all_turns(eng, step, end):
            for s in range(R):
                step(0, 0, s, None)
            with eng.Fori(0, NH // HU - 1) as j:
                for u in range(HU):
                    turns(j, u, None, step, end)
            for u in range(HU):
                turns(NH // HU - 1, u, HU - 1 - u, step, end)

        @block.tensor
        def _(pe):

            def unit(j, u, a):
                if u >= HU:
                    j, u = j + 1, u - HU
                at = (j * HU + u) * (NA + 1) + a
                if a == NA:
                    pe.wait_ge(negm_done, j * HU + u + 1)
                    for qt in range(NQ):
                        mm = pe.matmul(ps_a[0:1, qt * P:(qt + 1) * P], negm[:, qt:qt + 1], identb[:, :], start=True, stop=True)
                else:
                    if a == 0:
                        pe.wait_ge(loaded[u], 16 * LOADS * j + 16 * LOADS)
                    if not isinstance(at, int) or at > 0:
                        pe.wait_ge(a_free, at)
                    qt, kc = divmod(a, NKC)
                    for i in range(WA // 512):
                        mm = pe.matmul(ps_a[:, i * 512:(i + 1) * 512], qst[u][0:96, qt * P:(qt + 1) * P],
                                       kst[u][0:96, kc * WA + i * 512:kc * WA + (i + 1) * 512], start=True, stop=True)
                mm.then_inc(a_full, 1)

            def with_v(j, u, s):
                pe.wait_ge(exp_done[s % 2], (j * HU + u) * (NK // 2) + (s // 2 + 1))
                if s == 0:
                    pe.wait_ge(o_free[u % 2], j * 2 + (u // 2 + 1))
                for i in range(2):
                    mm = pe.matmul(ps_o[u % 2][64 * i:64 * i + V1, :], v[u][:, s, :], p[s % PR][:, i * HALF:(i + 1) * HALF],
                                   start=(s == 0), stop=(s == NK - 1), skip_group_check=True)
                mm.then_inc(p_used[s % PR], 1)

            def step(j, u, s, left):
                n = j * HU + u
                if s == 0:
                    pe.wait_ge(a_free, n * (NA + 1) + (NA + 1))
                if s < NK:
                    if s >= 2 or not isinstance(n, int) or n > 0:
                        pe.wait_ge(exp_done[s % 2], n * (NK // 2) + s // 2)
                    for i in range(2):
                        mm = pe.matmul(ps_b[s % 2][:, i * 512:(i + 1) * 512], kst[u][0:97, s * P:(s + 1) * P],
                                       qst[u][0:97, i * 512:(i + 1) * 512], start=True, stop=True)
                    mm.then_inc(b_full[s % 2], 1)
                    for ahead, a in units[s][:1]:
                        if left is None or ahead <= left:
                            unit(j, u + ahead, a)
                if s > 0:
                    with_v(j, u, s - 1)
                elif not isinstance(n, int) or n > 0:
                    with_v(*((j, u - 1) if u > 0 else (j - 1, HU - 1)), NK - 1)
                if s < NK:
                    for ahead, a in units[s][1:]:
                        if left is None or ahead <= left:
                            unit(j, u + ahead, a)
                if s == 0 and not (isinstance(n, int) and n == 0) or s == NK:
                    pj, pu = (j, u) if s == NK else (j, u - 1) if u > 0 else (j - 1, HU - 1)
                    pe.wait_ge(p_used[(NK - 1) % PR], (pj * HU + pu) * (NK // PR) + NK // PR)
                    pe.sem_inc(o_full[pu % 2], 1)
                    pe.sem_inc(head_used[pu], 1)

            def end(j, u):
                i = u % 2
                pe.wait_ge(oT_done[i], j * 4 + (2 * (u // 2) + 2))
                for q in range(HALF // P):
                    mm = pe.transpose(ps_o[i][:, q * P:q * P + 97], oT[i][0:97, q * P:(q + 1) * P], ident[0:97, 0:97])
                mm.then_inc(turned[i], 1)

            pe.wait_ge(preset, HU + 2)
            for a in range(NA + 1):
                unit(0, 0, a)
            for a in range(EARLY):
                unit(0, 1, a)
            all_turns(pe, step, end)

        @block.scalar
        def _(act):

            def max_row(j, u):
                if u >= HU:
                    j, u = j + 1, u - HU
                act.wait_ge(a_full, (j * HU + u) * (NA + 1) + (NA + 1))
                act.copy(qst[u][96:97, :], ps_a[0:1, :]).then_inc(a_free, 1)

            def step(j, u, s, left):
                n = j * HU + u
                if s == NK:
                    return
                act.wait_ge(b_full[s % 2], n * (NK // 2) + (s // 2 + 1))
                if s >= PR or not isinstance(n, int) or n > 0:
                    act.wait_ge(p_used[s % PR], n * (NK // PR) + s // PR)
                act.activation(p[s % PR][:, :], ps_b[s % 2][:, :], ACT.Exp, scale=SCALE).then_inc(exp_done[s % 2], 1)
                if (1, NA) in units[s] and (left is None or left >= 1):
                    max_row(j, u + 1)
                if s == 0 and not (isinstance(n, int) and n == 0):
                    copy_out(*((j, u - 1) if u > 0 else (j - 1, HU - 1)))

            def copy_out(j, u):
                i = u % 2
                act.wait_ge(o_full[i], j * 2 + (u // 2 + 1))
                for r in (0, 64):
                    act.copy(oT[i][r:r + V1, :], ps_o[i][r:r + V1, :]).then_inc(oT_done[i], 1)

            act.wait_ge(preset, HU + 2)
            max_row(0, 0)
            all_turns(act, step, lambda j, u: copy_out(j, u) if isinstance(j, int) and j * HU + u == NH - 1 else None)

        @block.vector
        def _(dve):

            def unit(j, u, a):
                if u >= HU:
                    j, u = j + 1, u - HU
                n = j * HU + u
                if a < NA:
                    dve.wait_ge(a_full, n * (NA + 1) + (a + 1))
                    dve.tensor_reduce(mx[:, a:a + 1], ps_a[:, :], X, ALU.max).then_inc(a_free, 1)
                else:
                    dve.wait_ge(a_free, n * (NA + 1) + NA)
                    dve.tensor_reduce(negm[:, :], mx[:, :].rearrange("p (q c) -> p q c", c=NKC), X, ALU.max,
                                      negate=True).then_inc(negm_done, 1)

            def step(j, u, s, left):
                if s < NK:
                    for ahead, a in units[s]:
                        if left is None or ahead <= left:
                            unit(j, u + ahead, a)

            def end(j, u):
                i = u % 2
                acc = ps_o[i][:, :].rearrange("p (n a d) -> p n a d", a=2, d=64)
                dve.wait_ge(turned[i], j * 2 + (u // 2 + 1))
                dve.reciprocal(inv[i][:, :, :, :], acc[:, :, :, HD:V1]).then_inc(inv_done, 1)
                dve.wait_ge(inv_done, j * HU + (u + 1))
                dve.wait_ge(o_out[i], j * 2 + (u // 2 + 1))
                dst = o[i][:, :, :].rearrange("p (a n) d -> p n a d", a=2)
                dve.tensor_tensor(dst, acc[:, :, :, 0:HD], inv[i][:, :, :, :].to_broadcast([P, NQ // 2, 2, HD]),
                                  ALU.mult).then_inc(o_done[i], 1)
                dve.wait_ge(o_done[i], j * 2 + (u // 2 + 1))
                dve.sem_inc(o_free[i], 1)

            for u in range(HU):
                dve.memset(kst[u][96:97, :].bitcast(F32), 1.0).then_inc(preset, 1)
            for i in range(2):
                dve.sem_inc(o_free[i], 1)
                dve.memset(oT[i][:, :], 0.0).then_inc(preset, 1)
            for a in range(NA + 1):
                unit(0, 0, a)
            for a in range(EARLY):
                unit(0, 1, a)
            all_turns(dve, step, end)

        @block.gpsimd
        def _(pool):
            for i in range(2):
                pool.sem_inc(o_out[i], 1)
            ov = out.rearrange("(b q p) d -> b p q d", b=B, p=P)
            for b in range(B):
                with pool.Fori(0, H // 2) as j:
                    for i in range(2):
                        pool.wait_ge(o_done[i], j + (b * (H // 2) + 1))
                        pool.sem_inc(passed[1], 1)
                        pool.dma_start(ov[b, :, :, bass.ds((2 * j + i) * HD, HD)], o[i][:, :, :]).then_inc(stored[i], 16)
                        pool.wait_ge(stored[i], 16 * j + (16 * b * (H // 2) + 16))
                        pool.sem_inc(o_out[i], 1)


def top_two(steps, dve, prob, ahead, gt, eq, rank, sel):
    other = prob.unsqueeze(2).to_broadcast([P, TT, E0, E0])
    own = prob.unsqueeze(3).to_broadcast([P, TT, E0, E0])
    steps.did(dve.tensor_tensor(gt, other, own, ALU.is_gt))
    steps.did(dve.tensor_tensor(eq, other, own, ALU.is_equal))
    steps.settle()
    steps.did(dve.tensor_tensor(eq, eq, ahead.unsqueeze(1).to_broadcast([P, TT, E0, E0]), ALU.mult))
    steps.settle()
    steps.did(dve.tensor_tensor(gt, gt, eq, ALU.add))
    steps.settle()
    steps.did(dve.tensor_reduce(rank, gt, X, ALU.add))
    steps.settle()
    steps.did(dve.tensor_scalar(sel, rank, 1.5, None, ALU.is_lt))
    steps.settle()


def ffn_moe(nc, x_dram, attn, woT, bo, wqkv, bqkv, wg, bg, we, be, ident, ahead,
            q_hi, q_lo, k_hi, k_lo, v_ones, x_part):
    NG = B * S // G
    with ExitStack() as ctx:
        t = Tools(nc, ctx, "moe")
        w_o = t.sb("w_o", [P, C, D])
        w_qkv = t.sb("w_qkv", [P, C, 3 * D])
        w_g = t.sb("w_g", [P, C, E0])
        w_e = t.sb("w_e", [P, E0, C, D])
        b_e = t.sb("b_e", [E0, D])
        qk_c = t.sb("qk_c", [P, 2 * C])
        rows = t.sb("rows", [P, 2, D])
        bg_r = t.sb("bg_r", [P, E0])
        ao, xin = t.sb("ao", [P, TT, D]), t.sb("xin", [P, TT, D])
        xT = t.sb("xT", [P, C, G])
        acc, ln = t.sb("acc", [P, TT, D]), t.sb("ln", [P, TT, D])
        stats, mv, rstd = t.sb("stats", [P, TT, 6]), t.sb("mv", [P, TT, 2]), t.sb("rstd", [P, 4, TT])
        hi, lo = t.sb("hi", [P, 2 * C, G], F32R), t.sb("lo", [P, 2 * C, G], F32R)
        vo = t.sb("vo", [P, TT, H, V1])
        lg, ex, sel, rank = (t.sb(n, [P, TT, E0]) for n in ("lg", "ex", "sel", "rank"))
        gt, eq = (t.sb(n, [P, TT, E0, E0]) for n in ("gt", "eq"))
        red = t.sb("red", [P, TT, 1])
        comb = t.sb("comb", [P, TT, E0])
        combT = t.sb("combT", [E0, G])
        tb = [t.ps(f"tb{i}", [P, G]) for i in range(4)]
        m = [t.ps(f"m{i}", [P, G]) for i in range(4)]
        w_in, in_sem, preset = t.sem("w_in"), t.sem("in"), t.sem("preset")
        t_full, t_out = t.sems("t_full", 4), t.sems("t_out", 4)
        m_full, m_free = t.sems("m_full", 4), t.sems("m_free", 4)
        dsem, hi_done = t.sem("dve_steps"), t.sem("hi_done")
        ln_done, lg_done, ex_done, comb_done, combT_done = (
            t.sem(n) for n in ("ln_done", "lg_done", "ex_done", "comb_done", "combT_done"))
        qkv_done, out_done, stored = t.sem("qkv_done"), t.sem("out_done"), t.sem("stored")
        TU = [3, 3, 2, 2]
        MU = 4 + 1 + E0
        NST = 6
        passed = t.sems("passed", 4)
        block = t.block()

        @block.sync
        def _(sp):
            sp.dma_start(w_o[:, :, :], woT.rearrange("(c p) n -> p c n", p=P)).then_inc(w_in, 16)
            sp.dma_start(w_qkv[:, :, :], wqkv.rearrange("(c p) n -> p c n", p=P)).then_inc(w_in, 16)
            sp.dma_start(w_g[:, :, :], wg.rearrange("(c p) n -> p c n", p=P)).then_inc(w_in, 16)
            sp.dma_start(b_e[:, :], be).then_inc(w_in, 16)
            sp.dma_start(qk_c[:, :], bqkv[0:2 * D].rearrange("(c p) -> p c", p=P), allow_slow_non_contiguous=True).then_inc(w_in, 16)
            sp.dma_start(rows[:, 0, :], row_of(bo, D)).then_inc(w_in, 16)
            sp.dma_start(rows[:, 1, :], row_of(bqkv[2 * D:3 * D], D)).then_inc(w_in, 16)
            sp.dma_start(bg_r[:, :], row_of(bg, E0)).then_inc(w_in, 16)
            for e in range(E0):
                sp.dma_start(w_e[:, e, :, :], we[e].rearrange("(c p) n -> p c n", p=P)).then_inc(w_in, 16)
            xs = x_dram.rearrange("(n p) d -> p n d", p=P)
            as_ = attn.rearrange("(n p) d -> p n d", p=P)
            with sp.Fori(0, NG) as g:
                sp.wait_ge(ln_done, g)
                sp.sem_inc(passed[0], 1)
                sp.dma_start(xin[:, :, :], xs[:, bass.ds(g * TT, TT), :]).then_inc(in_sem, 16)
                sp.dma_start(ao[:, :, :], as_[:, bass.ds(g * TT, TT), :]).then_inc(in_sem, 16)

        @block.tensor
        def _(pe):
            pe.wait_ge(w_in, 16 * (8 + E0))
            with pe.Fori(0, NG) as g:

                def turn(src, use):
                    for c in range(C):
                        pe.wait_ge(t_out[c], g * TU[c] + use)
                        for n in range(TT):
                            mm = pe.transpose(tb[c][:, n * P:(n + 1) * P], src[:, n, c * P:(c + 1) * P], ident[:, :])
                        mm.then_inc(t_full[c], 1)
                    for c in range(C):
                        pe.wait_ge(t_out[c], g * TU[c] + (use + 1))

                def tile(row, o, left, right):
                    pe.wait_ge(m_free[o], g * MU + row)
                    for c in range(C):
                        mm = pe.matmul(m[o][:, :], left(c), right(c), start=(c == 0), stop=(c == C - 1))
                    mm.then_inc(m_full[o], 1)

                pe.wait_ge(in_sem, 32 * g + 32)
                turn(ao, 0)
                for o in range(4):
                    tile(0, o, lambda c: xT[:, c, o * P:(o + 1) * P], lambda c: w_o[:, c, :])
                pe.wait_ge(ln_done, g + 1)
                turn(ln, 1)
                pe.wait_ge(t_out[0], g * TU[0] + 2)
                for n in range(TT):
                    for c in range(C):
                        mm = pe.matmul(tb[0][:, n * E0:(n + 1) * E0], xT[:, c, n * P:(n + 1) * P], w_g[:, c, :],
                                       start=(c == 0), stop=(c == C - 1))
                mm.then_inc(t_full[0], 1)
                for r in range(2):
                    for o in range(4):
                        k = (4 * r + o) * P
                        tile(1 + r, o, lambda c: w_qkv[:, c, k:k + P], lambda c: xT[:, c, :])
                for o in range(4):
                    tile(3, o, lambda c: xT[:, c, o * P:(o + 1) * P], lambda c: w_qkv[:, c, 2 * D:3 * D])
                pe.wait_ge(comb_done, g + 1)
                pe.wait_ge(t_out[1], g * TU[1] + 2)
                for n in range(TT):
                    mm = pe.transpose(tb[1][0:E0, n * P:(n + 1) * P], comb[:, n, :], ident[:, :])
                mm.then_inc(t_full[1], 1)
                pe.wait_ge(combT_done, g + 1)
                for o in range(4):
                    pe.wait_ge(m_free[o], g * MU + 4)
                    pe.matmul(m[o][:, :], combT[:, o * P:(o + 1) * P], b_e[:, :],
                              start=True, stop=True).then_inc(m_full[o], 1)
                for e in range(E0):
                    for o in range(4):
                        tile(5 + e, o, lambda c: xT[:, c, o * P:(o + 1) * P], lambda c: w_e[:, e, c, :])

        @block.scalar
        def _(act):
            act.wait_ge(w_in, 16 * (8 + E0))
            with act.Fori(0, NG) as g:
                act.wait_ge(m_full[3], g * MU)
                for use in range(2):
                    if use == 1:
                        act.wait_ge(m_full[3], g * MU + 1)
                    for c in range(C):
                        act.wait_ge(t_full[c], g * TU[c] + (use + 1))
                        act.copy(xT[:, c, :], tb[c][:, :]).then_inc(t_out[c], 1)
                act.wait_ge(lg_done, g + 1)
                act.activation(ex[:, :, :], lg[:, :, :], ACT.Exp).then_inc(ex_done, 1)
                act.wait_ge(stored, 16 * NST * g)
                for k in range(2 * C):
                    act.wait_ge(m_full[k % 4], g * MU + (k // 4 + 2))
                    act.activation(hi[:, k, :], m[k % 4][:, :], ACT.Identity, bias=qk_c[:, k:k + 1]).then_inc(hi_done, 1)
                act.wait_ge(t_full[1], g * TU[1] + 3)
                act.copy(combT[:, :], tb[1][0:E0, :]).then_inc(combT_done, 1)
                act.wait_ge(combT_done, g + 1)
                act.sem_inc(t_out[1], 1)

        @block.vector
        def _(dve):
            steps = Steps(dve, dsem, 42)
            dve.memset(vo[:, :, :, HD:V1], 1.0).then_inc(preset, 1)
            dve.wait_ge(preset, 1)
            dve.wait_ge(w_in, 16 * (8 + E0))
            with dve.Fori(0, NG) as g:
                steps.begin(g)
                dve.wait_ge(in_sem, 32 * g + 32)
                dve.wait_ge(stored, 16 * NST * g)
                for n in range(TT):
                    steps.did(dve.tensor_tensor(xin[:, n, :], xin[:, n, :], rows[:, 0, :], ALU.add))
                steps.settle()
                for n in range(TT):
                    dve.wait_ge(m_full[n], g * MU + 1)
                    dve.tensor_tensor(acc[:, n, :], m[n][:, :], xin[:, n, :], ALU.add).then_inc(m_free[n], 1)
                for n in range(TT):
                    dve.wait_ge(m_free[n], g * MU + 1)
                layer_norm(steps, dve, passed[3], acc, ln, stats, mv, rstd)
                dve.sem_inc(ln_done, 1)
                dve.wait_ge(t_full[0], g * TU[0] + 3)
                gate = tb[0][:, 0:TT * E0].rearrange("p (n e) -> p n e", e=E0)
                steps.did(dve.tensor_tensor(lg[:, :, :], gate, bg_r[:, :].unsqueeze(1).to_broadcast([P, TT, E0]), ALU.add))
                steps.settle()
                dve.sem_inc(t_out[0], 1)
                steps.did(dve.tensor_reduce(red[:, :, :], lg[:, :, :], X, ALU.max))
                steps.settle()
                steps.did(dve.tensor_tensor(lg[:, :, :], lg[:, :, :], red[:, :, :].to_broadcast([P, TT, E0]), ALU.subtract))
                steps.settle()
                dve.sem_inc(lg_done, 1)
                dve.wait_ge(ex_done, g + 1)
                steps.did(dve.tensor_reduce(red[:, :, :], ex[:, :, :], X, ALU.add))
                steps.settle()
                steps.did(dve.reciprocal(red[:, :, :], red[:, :, :]))
                steps.settle()
                steps.did(dve.tensor_tensor(ex[:, :, :], ex[:, :, :], red[:, :, :].to_broadcast([P, TT, E0]), ALU.mult))
                steps.settle()
                top_two(steps, dve, ex[:, :, :], ahead[:, :, :], gt[:, :, :, :], eq[:, :, :, :], rank[:, :, :], sel[:, :, :])
                steps.did(dve.tensor_tensor(comb[:, :, :], ex[:, :, :], sel[:, :, :], ALU.mult))
                steps.settle()
                dve.sem_inc(comb_done, 1)
                for k in range(2 * C):
                    dve.wait_ge(m_full[k % 4], g * MU + (k // 4 + 2))
                    dve.wait_ge(hi_done, g * 2 * C + (k + 1))
                    dve.scalar_tensor_tensor(out=lo[:, k, :], in0=m[k % 4][:, :], scalar=qk_c[:, k:k + 1],
                                             in1=hi[:, k, :].bitcast(F32), op0=ALU.add,
                                             op1=ALU.subtract).then_inc(m_free[k % 4], 1)
                for n in range(TT):
                    dve.wait_ge(m_full[n], g * MU + 4)
                    dve.tensor_tensor(vo[:, n, :, 0:HD], m[n][:, :].rearrange("p (h d) -> p h d", h=H),
                                      rows[:, 1, :].rearrange("p (h d) -> p h d", h=H), ALU.add).then_inc(m_free[n], 1)
                for n in range(TT):
                    dve.wait_ge(m_free[n], g * MU + 4)
                dve.sem_inc(qkv_done, 1)
                for n in range(TT):
                    dve.wait_ge(m_full[n], g * MU + 5)
                    dve.tensor_tensor(acc[:, n, :], m[n][:, :], acc[:, n, :], ALU.add).then_inc(m_free[n], 1)
                for e in range(E0):
                    for n in range(TT):
                        dve.wait_ge(m_full[n], g * MU + (6 + e))
                        dve.wait_ge(m_free[n], g * MU + (5 + e))
                        dve.scalar_tensor_tensor(out=acc[:, n, :], in0=m[n][:, :], scalar=comb[:, n, e:e + 1],
                                                 in1=acc[:, n, :], op0=ALU.mult, op1=ALU.add).then_inc(m_free[n], 1)
                for n in range(TT):
                    dve.wait_ge(m_free[n], g * MU + MU)
                dve.sem_inc(out_done, 1)
                steps.end()

        @block.gpsimd
        def _(pool):
            vd = v_ones.rearrange("(n p) f -> p n f", p=P)
            xd = x_part.rearrange("(n p) d -> p n d", p=P)
            with pool.Fori(0, NG) as g:
                pool.wait_ge(qkv_done, g + 1)
                pool.sem_inc(passed[1], 1)
                for dst, src, k in ((q_hi, hi, 0), (q_lo, lo, 0), (k_hi, hi, C), (k_lo, lo, C)):
                    pool.dma_start(dst.rearrange("(g c p) t -> g p c t", c=C, p=P)[bass.ds(g, 1), :, :, :]
                                   .rearrange("a p c t -> (a p) c t").bitcast(F32),
                                   src[:, k:k + C, :].bitcast(F32)).then_inc(stored, 16)
                pool.dma_start(vd[:, bass.ds(g * TT, TT), :],
                               vo[:, :, :, :].rearrange("p n h d -> p n (h d)")).then_inc(stored, 16)
                pool.wait_ge(out_done, g + 1)
                pool.sem_inc(passed[1], 1)
                pool.dma_start(xd[:, bass.ds(g * TT, TT), :], acc[:, :, :]).then_inc(stored, 16)
            pool.wait_ge(stored, 16 * NST * NG)


def sample_positions(nc, x_part, attn, mask, wqT, bq, woffT, boff, ident, x2, qp_dram, idx_dram, wt_dram):
    F = TT * NS
    with ExitStack() as ctx:
        t = Tools(nc, ctx, "pos")
        w_q, w_off = t.sb("w_q", [P, C, D]), t.sb("w_off", [P, C, NS])
        bq_r, boff_r = t.sb("bq_r", [P, D]), t.sb("boff_r", [P, NS])
        mk = t.sb("mk", [P, T], I32)
        mkf = t.sb("mkf", [P, T])
        length, neg_length, inv_length = (t.sb(n, [P, 1]) for n in ("length", "neg_length", "inv_length"))
        pos_i, head_i = t.sb("pos_i", [P, 2, F], I32), t.sb("head_i", [P, F], I32)
        pos, head = t.sb("pos", [P, 2, F]), t.sb("head", [P, F])
        xa, xb = t.sb("xa", [P, TT, D]), t.sb("xb", [P, TT, D])
        ln, xT, qp = t.sb("ln", [P, TT, D]), t.sb("xT", [P, C, G]), t.sb("qp", [P, TT, D])
        stats, mv, rstd = t.sb("stats", [P, TT, 6]), t.sb("mv", [P, TT, 2]), t.sb("rstd", [P, 4, TT])
        at, whole, frac, flag = (t.sb(n, [P, F]) for n in ("at", "whole", "frac", "flag"))
        whole_i = t.sb("whole_i", [P, F], I32)
        wt = t.sb("wt", [P, F, 2])
        idx = t.sb("idx", [P, F], I32)
        tb = [t.ps(f"tb{i}", [P, G]) for i in range(4)]
        m = [t.ps(f"m{i}", [P, G]) for i in range(4)]
        w_in, in_sem, made = t.sem("w_in"), t.sem("in"), t.sem("made")
        mask_in, dsem, bsem = t.sem("mask_in"), t.sem("dve_steps"), t.sem("batch_steps")
        t_full, t_out = t.sems("t_full", 4), t.sems("t_out", 4)
        m_full, m_free = t.sems("m_full", 4), t.sems("m_free", 4)
        ln_done, qp_done, x2_done, idx_done, stored = (
            t.sem(n) for n in ("ln_done", "qp_done", "x2_done", "idx_done", "stored"))
        TU = [3, 2, 2, 2]
        NST = 4
        passed = t.sems("passed", 4)
        block = t.block()

        @block.sync
        def _(sp):
            sp.dma_start(w_q[:, :, :], wqT.rearrange("(c p) n -> p c n", p=P)).then_inc(w_in, 16)
            sp.dma_start(w_off[:, :, :], woffT.rearrange("(c p) n -> p c n", p=P)).then_inc(w_in, 16)
            sp.dma_start(bq_r[:, :], row_of(bq, D)).then_inc(w_in, 16)
            sp.dma_start(boff_r[:, :], row_of(boff, NS)).then_inc(w_in, 16)
            xs = x_part.rearrange("(n p) d -> p n d", p=P)
            as_ = attn.rearrange("(n p) d -> p n d", p=P)
            with sp.Fori(0, B) as b:
                sp.wait_ge(idx_done, 2 * b)
                sp.sem_inc(passed[0], 1)
                sp.dma_start(mk[:, :], mask[bass.ds(b, 1), :].partition_broadcast(P).rearrange("p a t -> p (a t)")).then_inc(mask_in, 16)
                for u in range(2):
                    g = 2 * b + u
                    sp.wait_ge(stored, 16 * NST * g)
                    sp.sem_inc(passed[0], 1)
                    sp.dma_start(xa[:, :, :], xs[:, bass.ds(g * TT, TT), :]).then_inc(in_sem, 16)
                    sp.dma_start(xb[:, :, :], as_[:, bass.ds(g * TT, TT), :]).then_inc(in_sem, 16)

        @block.gpsimd
        def _(pool):
            for u in range(2):
                pool.iota(pos_i[:, u, :], [[P, TT], [0, H], [1, NK5]], base=u * G + (-NK5 // 2),
                          channel_multiplier=1).then_inc(made, 1)
            pool.iota(head_i[:, :], [[0, TT], [1, H], [0, NK5]], base=0, channel_multiplier=0).then_inc(made, 1)
            xd = x2.rearrange("(n p) d -> p n d", p=P)
            qd = qp_dram.rearrange("(n p) d -> p n d", p=P)
            idd = idx_dram.rearrange("(n p) d -> p n d", p=P)
            wd = wt_dram.rearrange("(n p) d -> p n d", p=P)
            with pool.Fori(0, B * S // G) as g:
                pool.wait_ge(x2_done, g + 1)
                pool.sem_inc(passed[1], 1)
                pool.dma_start(xd[:, bass.ds(g * TT, TT), :], xa[:, :, :]).then_inc(stored, 16)
                pool.wait_ge(qp_done, g + 1)
                pool.sem_inc(passed[1], 1)
                pool.dma_start(qd[:, bass.ds(g * TT, TT), :], qp[:, :, :]).then_inc(stored, 16)
                pool.wait_ge(idx_done, g + 1)
                pool.sem_inc(passed[1], 1)
                pool.dma_start(idd[:, bass.ds(g * TT, TT), :], idx[:, :].rearrange("p (n s) -> p n s", n=TT)).then_inc(stored, 16)
                pool.dma_start(wd[:, bass.ds(g * TT, TT), :], wt[:, :, :].rearrange("p (n s) a -> p n (s a)", n=TT)).then_inc(stored, 16)
            pool.wait_ge(stored, 16 * NST * (B * S // G))

        @block.tensor
        def _(pe):
            pe.wait_ge(w_in, 64)
            with pe.Fori(0, B * S // G) as g:

                def turn(src, use):
                    for c in range(C):
                        pe.wait_ge(t_out[c], g * TU[c] + use)
                        for n in range(TT):
                            mm = pe.transpose(tb[c][:, n * P:(n + 1) * P], src[:, n, c * P:(c + 1) * P], ident[:, :])
                        mm.then_inc(t_full[c], 1)
                    for c in range(C):
                        pe.wait_ge(t_out[c], g * TU[c] + (use + 1))

                pe.wait_ge(ln_done, g + 1)
                turn(ln, 0)
                for n in range(TT):
                    pe.wait_ge(m_free[n], g)
                    for c in range(C):
                        mm = pe.matmul(m[n][:, :], xT[:, c, n * P:(n + 1) * P], w_q[:, c, :], start=(c == 0), stop=(c == C - 1))
                    mm.then_inc(m_full[n], 1)
                pe.wait_ge(qp_done, g + 1)
                turn(qp, 1)
                for n in range(TT):
                    for c in range(C):
                        mm = pe.matmul(tb[0][:, n * NS:(n + 1) * NS], xT[:, c, n * P:(n + 1) * P], w_off[:, c, :],
                                       start=(c == 0), stop=(c == C - 1))
                mm.then_inc(t_full[0], 1)

        @block.scalar
        def _(act):
            with act.Fori(0, B * S // G) as g:
                act.wait_ge(t_full[0], g * TU[0])
                for use in range(2):
                    if use == 1:
                        act.wait_ge(m_full[3], g + 1)
                    for c in range(C):
                        act.wait_ge(t_full[c], g * TU[c] + (use + 1))
                        act.copy(xT[:, c, :], tb[c][:, :]).then_inc(t_out[c], 1)

        @block.vector
        def _(dve):
            per_batch = Steps(dve, bsem, 5)
            steps = Steps(dve, dsem, 54)
            dve.wait_ge(w_in, 64)
            dve.wait_ge(made, 3)
            dve.tensor_copy(pos[:, :, :], pos_i[:, :, :]).then_inc(made, 1)
            dve.tensor_scalar(head[:, :], head_i[:, :], float(ROWS * PAIR), float(2 * PAIR), ALU.mult,
                              ALU.add).then_inc(made, 1)
            dve.wait_ge(made, 5)
            with dve.Fori(0, B) as b:
                per_batch.begin(b)
                dve.wait_ge(mask_in, 16 * b + 16)
                per_batch.did(dve.tensor_copy(mkf[:, :], mk[:, :]))
                per_batch.settle()
                per_batch.did(dve.tensor_reduce(length[:, :], mkf[:, :], X, ALU.add))
                per_batch.settle()
                per_batch.did(dve.tensor_scalar(neg_length[:, :], length[:, :], float(T - 1), None, ALU.subtract))
                per_batch.settle()
                per_batch.did(dve.tensor_scalar(length[:, :], neg_length[:, :], -1.0, None, ALU.mult))
                per_batch.settle()
                per_batch.did(dve.reciprocal(inv_length[:, :], length[:, :]))
                per_batch.settle()
                per_batch.end()
                for u in range(2):
                    g = 2 * b + u
                    steps.begin(g)
                    go = lambda ins: (steps.did(ins), steps.settle())
                    dve.wait_ge(in_sem, 32 * g + 32)
                    for n in range(TT):
                        steps.did(dve.tensor_tensor(xa[:, n, :], xa[:, n, :], xb[:, n, :], ALU.add))
                    steps.settle()
                    dve.sem_inc(x2_done, 1)
                    layer_norm(steps, dve, passed[3], xa, ln, stats, mv, rstd)
                    dve.sem_inc(ln_done, 1)
                    dve.wait_ge(stored, 16 * NST * g)
                    for n in range(TT):
                        dve.wait_ge(m_full[n], g + 1)
                        dve.tensor_tensor(qp[:, n, :], m[n][:, :], bq_r[:, :], ALU.add).then_inc(m_free[n], 1)
                    for n in range(TT):
                        dve.wait_ge(m_free[n], g + 1)
                    dve.sem_inc(qp_done, 1)
                    dve.wait_ge(t_full[0], g * TU[0] + 3)
                    go(dve.tensor_tensor(at[:, :].rearrange("p (n s) -> p n s", n=TT),
                                         tb[0][:, 0:F].rearrange("p (n s) -> p n s", n=TT),
                                         boff_r[:, :].unsqueeze(1).to_broadcast([P, TT, NS]), ALU.add))
                    dve.sem_inc(t_out[0], 1)
                    go(dve.tensor_tensor(at[:, :], at[:, :], pos[:, u, :], ALU.add))

                    def floor(src, dst):
                        go(dve.tensor_copy(whole_i[:, :], src))
                        go(dve.tensor_copy(dst, whole_i[:, :]))
                        go(dve.tensor_tensor(flag[:, :], dst, src, ALU.is_gt))
                        go(dve.tensor_tensor(dst, dst, flag[:, :], ALU.subtract))

                    go(dve.tensor_scalar(frac[:, :], at[:, :], inv_length[:, 0:1], None, ALU.mult))
                    floor(frac[:, :], whole[:, :])
                    go(dve.scalar_tensor_tensor(out=at[:, :], in0=whole[:, :], scalar=neg_length[:, 0:1], in1=at[:, :],
                                                op0=ALU.mult, op1=ALU.add))
                    go(dve.tensor_scalar(flag[:, :], at[:, :], inv_length[:, 0:1], 1.0, ALU.mult, ALU.is_ge))
                    go(dve.scalar_tensor_tensor(out=at[:, :], in0=flag[:, :], scalar=neg_length[:, 0:1], in1=at[:, :],
                                                op0=ALU.mult, op1=ALU.add))
                    go(dve.tensor_scalar(flag[:, :], at[:, :], inv_length[:, 0:1], 0.0, ALU.mult, ALU.is_lt))
                    go(dve.scalar_tensor_tensor(out=at[:, :], in0=flag[:, :], scalar=length[:, 0:1], in1=at[:, :],
                                                op0=ALU.mult, op1=ALU.add))
                    go(dve.tensor_scalar(at[:, :], at[:, :], 1.0 / (T - 1), 2.0, ALU.mult, ALU.mult))
                    go(dve.tensor_scalar(at[:, :], at[:, :], -1.0, 1.0, ALU.add, ALU.add))
                    go(dve.tensor_scalar(at[:, :], at[:, :], float(T), -1.0, ALU.mult, ALU.add))
                    go(dve.tensor_scalar(at[:, :], at[:, :], 0.5, None, ALU.mult))
                    floor(at[:, :], whole[:, :])
                    go(dve.tensor_tensor(frac[:, :], at[:, :], whole[:, :], ALU.subtract))
                    steps.did(dve.tensor_scalar(wt[:, :, 0], frac[:, :], -0.5, 0.5, ALU.mult, ALU.add))
                    steps.did(dve.tensor_scalar(wt[:, :, 1], frac[:, :], 0.5, None, ALU.mult))
                    go(dve.tensor_scalar(whole[:, :], whole[:, :], -2.0, float(T), ALU.max, ALU.min))
                    go(dve.scalar_tensor_tensor(out=idx[:, :], in0=whole[:, :], scalar=float(PAIR), in1=head[:, :],
                                                op0=ALU.mult, op1=ALU.add))
                    dve.sem_inc(idx_done, 1)
                    steps.end()


def sampled_attention(nc, tables, qp_dram, idx_dram, wt_dram, out):
    NT = B * S // P
    with ExitStack() as ctx:
        t = Tools(nc, ctx, "smp")
        rows = [t.sb(f"rows{i}", [P, NS, 2 * PAIR]) for i in range(2)]
        idx = [t.sb(f"idx{i}", [P, NS], I32) for i in range(2)]
        wt = [t.sb(f"wt{i}", [P, NS, 2]) for i in range(2)]
        qp = [t.sb(f"qp{i}", [P, D]) for i in range(2)]
        prod = t.sb("prod", [P, H, 2 * NK5, HD])
        s10, a10 = t.sb("s10", [P, H, NK5, 2]), t.sb("a10", [P, H, NK5, 2])
        s5 = t.sb("s5", [P, H, NK5])
        red = t.sb("red", [P, H, 1])
        o = [t.sb(f"o{i}", [P, D]) for i in range(2)]
        in_sem, gathered, rows_used = t.sems("in", 2), t.sems("gathered", 2), t.sems("rows_used", 2)
        dsem, s_done, e_done, o_done, stored = (
            t.sem("dve_steps"), t.sem("s_done"), t.sem("e_done"), t.sems("o_done", 2), t.sems("stored", 2))
        passed = t.sems("passed", 4)
        block = t.block()

        @block.sync
        def _(sp):
            with sp.Fori(0, NT // 2) as j:
                for u in range(2):
                    r = bass.ds((2 * j + u) * P, P)
                    sp.wait_ge(rows_used[u], j)
                    sp.sem_inc(passed[0], 1)
                    sp.dma_start(idx[u][:, :], idx_dram[r, :]).then_inc(in_sem[u], 16)
                    sp.dma_start(wt[u][:, :, :].rearrange("p s a -> p (s a)"), wt_dram[r, :]).then_inc(in_sem[u], 16)
                    sp.dma_start(qp[u][:, :], qp_dram[r, :]).then_inc(in_sem[u], 16)

        @block.gpsimd
        def _(pool):
            for b in range(B):
                with pool.Fori(0, NT // B // 2) as j:
                    for u in range(2):
                        use = j + b * (NT // B // 2)
                        pool.wait_ge(in_sem[u], 48 * use + 48)
                        pool.sem_inc(passed[1], 1)
                        for s in range(NS):
                            pool.indirect_dma_start(rows[u][:, s, :], None, tables[b].rearrange("(n a) -> n a", a=1),
                                                    bass.IndirectOffsetOnAxis(idx[u][:, s:s + 1], 0)).then_inc(gathered[u], 16)

        @block.scalar
        def _(act):
            with act.Fori(0, NT // 2) as j:
                for u in range(2):
                    n = 2 * j + u
                    act.wait_ge(s_done, n + 1)
                    act.activation(s5[:, :, :], s5[:, :, :], ACT.Exp, scale=SCALE).then_inc(e_done, 1)
                    act.wait_ge(o_done[u], j + 1)
                    act.dma_start(out[bass.ds(n * P, P), :], o[u][:, :]).then_inc(stored[u], 16)
            for u in range(2):
                act.wait_ge(stored[u], 16 * (NT // 2))

        @block.vector
        def _(dve):
            steps = Steps(dve, dsem, 12)
            with dve.Fori(0, NT // 2) as j:
                for u in range(2):
                    n = 2 * j + u
                    steps.begin(n)
                    go = lambda ins: (steps.did(ins), steps.settle())
                    kv = rows[u][:, :, :].rearrange("p (h k) (m a d) -> p h (k m) a d", k=NK5, a=2, d=HD)
                    q = qp[u][:, :].rearrange("p (h d) -> p h d", h=H)
                    dve.wait_ge(gathered[u], 16 * NS * j + 16 * NS)
                    dve.wait_ge(in_sem[u], 48 * j + 48)
                    go(dve.tensor_tensor(prod[:, :, :, :], kv[:, :, :, 0, :],
                                         q.unsqueeze(2).to_broadcast([P, H, 2 * NK5, HD]), ALU.mult))
                    go(dve.tensor_reduce(s10[:, :, :, :].rearrange("p h k m -> p h (k m)"), prod[:, :, :, :], X, ALU.add))
                    w = wt[u][:, :, :].rearrange("p (h k) m -> p h k m", h=H)
                    go(dve.tensor_tensor(s10[:, :, :, :], s10[:, :, :, :], w, ALU.mult))
                    go(dve.tensor_tensor(s5[:, :, :], s10[:, :, :, 0], s10[:, :, :, 1], ALU.add))
                    go(dve.tensor_reduce(red[:, :, :], s5[:, :, :], X, ALU.max))
                    go(dve.tensor_tensor(s5[:, :, :], s5[:, :, :], red[:, :, :].to_broadcast([P, H, NK5]), ALU.subtract))
                    dve.sem_inc(s_done, 1)
                    dve.wait_ge(e_done, n + 1)
                    go(dve.tensor_reduce(red[:, :, :], s5[:, :, :], X, ALU.add))
                    go(dve.reciprocal(red[:, :, :], red[:, :, :]))
                    go(dve.tensor_tensor(s5[:, :, :], s5[:, :, :], red[:, :, :].to_broadcast([P, H, NK5]), ALU.mult))
                    go(dve.tensor_tensor(a10[:, :, :, :], w, s5[:, :, :].unsqueeze(3).to_broadcast([P, H, NK5, 2]), ALU.mult))
                    go(dve.tensor_tensor(prod[:, :, :, :], kv[:, :, :, 1, :],
                                         a10[:, :, :, :].rearrange("p h k m -> p h (k m)").unsqueeze(3)
                                         .to_broadcast([P, H, 2 * NK5, HD]), ALU.mult))
                    dve.sem_inc(rows_used[u], 1)
                    dve.wait_ge(stored[u], 16 * j)
                    go(dve.tensor_reduce(o[u][:, :].rearrange("p (h d) -> p h d", h=H),
                                         prod[:, :, :, :].rearrange("p h s d -> p h d s"), X, ALU.add))
                    dve.sem_inc(o_done[u], 1)
                    steps.end()


def ffn_last(nc, x2, cx, woT, bo, w_enc, b_enc, w_s2c, b_s2c, wr, br, w1, b1, w2, b2, w_c2s, b_c2s,
             w_dec, b_dec, ln_g, ln_b, ident, ahead, out):
    NG = B * S // G
    HC = HID // P
    with ExitStack() as ctx:
        t = Tools(nc, ctx, "out")
        wo_s, we_s = t.sb("wo", [P, C, D]), t.sb("we", [P, C, HID])
        ws_s, wr_s = t.sb("ws", [P, HC, MM]), t.sb("wr", [MM, E1])
        w1_s, w2_s = t.sb("w1", [MM, E1, EH]), t.sb("w2", [P, E1, EH // P, MM])
        wc_s, wd_s = t.sb("wc", [MM, HID]), t.sb("wd", [P, HC, D])
        be_c, bs_c, b1_c, bc_c = t.sb("be", [P, HC]), t.sb("bs", [MM, 1]), t.sb("b1", [P, E1, EH // P]), t.sb("bc", [P, HC])
        rows = t.sb("rows", [P, 5, D])
        br_r = t.sb("br_r", [P, E1])
        ca, acc, ln = t.sb("ca", [P, TT, D]), t.sb("acc", [P, TT, D]), t.sb("ln", [P, TT, D])
        xT, hT = t.sb("xT", [P, C, G]), t.sb("hT", [P, HC, G])
        contT, eoT = t.sb("contT", [MM, G]), t.sb("eoT", [MM, G])
        he = [t.sb(f"he{i}", [P, EH // P, G]) for i in range(2)]
        y, eo = t.sb("y", [P, TT, E1, MM]), t.sb("eo", [P, TT, MM])
        stats, mv, rstd = t.sb("stats", [P, TT, 6]), t.sb("mv", [P, TT, 2]), t.sb("rstd", [P, 4, TT])
        lg, ex, sel, rank = (t.sb(n, [P, TT, E1]) for n in ("lg", "ex", "sel", "rank"))
        gt, eq = (t.sb(n, [P, TT, E1, E1]) for n in ("gt", "eq"))
        red = t.sb("red", [P, TT, 1])
        tb = [t.ps(f"tb{i}", [P, G]) for i in range(4)]
        m = [t.ps(f"m{i}", [P, G]) for i in range(4)]
        w_in, in_sem = t.sem("w_in"), t.sem("in")
        t_full, t_out = t.sems("t_full", 4), t.sems("t_out", 4)
        m_full, m_free = t.sems("m_full", 4), t.sems("m_free", 4)
        dsem, ln_done, lg_done, ex_done, eo_done, out_done, stored, he_used = (
            t.sem(n) for n in ("dve_steps", "ln_done", "lg_done", "ex_done", "eo_done", "out_done", "stored", "he_used"))
        TU = [4, 4, 4, 3]
        MU = 1 + 2 + E1 + 2 + 1
        NW = 19
        passed = t.sems("passed", 4)
        block = t.block()

        @block.sync
        def _(sp):
            loads = [(wo_s[:, :, :], woT.rearrange("(c p) n -> p c n", p=P)),
                     (we_s[:, :, :], w_enc.rearrange("(c p) n -> p c n", p=P)),
                     (ws_s[:, :, :], w_s2c.rearrange("(c p) n -> p c n", p=P)), (wr_s[:, :], wr),
                     (w1_s[:, :, :], w1.rearrange("e m h -> m e h")),
                     (w2_s[:, :, :, :], w2.rearrange("e (k p) m -> p e k m", p=P)), (wc_s[:, :], w_c2s),
                     (wd_s[:, :, :], w_dec.rearrange("(c p) n -> p c n", p=P)),
                     (be_c[:, :], b_enc.rearrange("(c p) -> p c", p=P)), (bs_c[:, :], b_s2c.rearrange("(m a) -> m a", a=1)),
                     (b1_c[:, :, :], b1.rearrange("e (k p) -> p e k", p=P)), (bc_c[:, :], b_c2s.rearrange("(c p) -> p c", p=P)),
                     (rows[:, 0, :], row_of(bo, D)), (rows[:, 1, :], row_of(b_dec, D)), (rows[:, 2, :], row_of(ln_g, D)),
                     (rows[:, 3, :], row_of(ln_b, D)), (rows[:, 4, :], row_of(b2, D)), (br_r[:, :], row_of(br, E1))]
            assert len(loads) == NW - 1
            for dst, src in loads:
                sp.dma_start(dst, src, allow_slow_non_contiguous=True).then_inc(w_in, 16)
            xs = x2.rearrange("(n p) d -> p n d", p=P)
            cs = cx.rearrange("(n p) d -> p n d", p=P)
            with sp.Fori(0, NG) as g:
                sp.wait_ge(stored, 16 * g)
                sp.sem_inc(passed[0], 1)
                sp.dma_start(acc[:, :, :], xs[:, bass.ds(g * TT, TT), :]).then_inc(in_sem, 16)
                sp.dma_start(ca[:, :, :], cs[:, bass.ds(g * TT, TT), :]).then_inc(in_sem, 16)

        @block.tensor
        def _(pe):
            pe.wait_ge(w_in, 16 * (NW - 1))
            with pe.Fori(0, NG) as g:

                def turn(src, use):
                    for c in range(C):
                        pe.wait_ge(t_out[c], g * TU[c] + use)
                        for n in range(TT):
                            mm = pe.transpose(tb[c][:, n * P:(n + 1) * P], src[:, n, c * P:(c + 1) * P], ident[:, :])
                        mm.then_inc(t_full[c], 1)
                    for c in range(C):
                        pe.wait_ge(t_out[c], g * TU[c] + (use + 1))

                def tile(row, o, n, left, right):
                    pe.wait_ge(m_free[o], g * MU + row)
                    for c in range(n):
                        mm = pe.matmul(m[o][:, :], left(c), right(c), start=(c == 0), stop=(c == n - 1))
                    mm.then_inc(m_full[o], 1)

                def y_of(e):
                    for k in range(4):
                        pe.wait_ge(m_free[k], g * MU + (3 + e + 1))
                    for n in range(TT):
                        if e == 0:
                            pe.wait_ge(t_out[n], g * TU[n] + [3, 3, 2, 2][n])
                        for k in range(EH // P):
                            mm = pe.matmul(tb[n][:, e * MM:(e + 1) * MM], he[e % 2][:, k, n * P:(n + 1) * P],
                                           w2_s[:, e, k, :], start=(k == 0), stop=(k == EH // P - 1))
                        if e == E1 - 1:
                            mm.then_inc(t_full[n], 1)
                    if e < E1 - 1:
                        mm.then_inc(he_used, 1)

                pe.wait_ge(in_sem, 32 * g + 32)
                turn(ca, 0)
                for o in range(4):
                    tile(0, o, C, lambda c: xT[:, c, o * P:(o + 1) * P], lambda c: wo_s[:, c, :])
                pe.wait_ge(ln_done, 2 * g + 1)
                turn(ln, 1)
                for r in range(2):
                    for o in range(4):
                        k = (4 * r + o) * P
                        tile(1 + r, o, C, lambda c: we_s[:, c, k:k + P], lambda c: xT[:, c, :])
                for o in range(4):
                    pe.wait_ge(m_free[o], g * MU + 3)
                for k in range(HC):
                    mm = pe.matmul(tb[1][0:MM, :], ws_s[:, k, :], hT[:, k, :], start=(k == 0), stop=(k == HC - 1))
                mm.then_inc(t_full[1], 1)
                pe.wait_ge(t_out[1], g * TU[1] + 3)
                for n in range(TT):
                    mm = pe.matmul(tb[0][:, n * E1:(n + 1) * E1], contT[:, n * P:(n + 1) * P], wr_s[:, :], start=True, stop=True)
                mm.then_inc(t_full[0], 1)
                for e in range(E1):
                    for o in range(4):
                        tile(3 + e, o, 1, lambda c: w1_s[:, e, o * P:(o + 1) * P], lambda c: contT[:, :])
                    if e > 0:
                        y_of(e - 1)
                y_of(E1 - 1)
                pe.wait_ge(eo_done, g + 1)
                pe.wait_ge(t_out[2], g * TU[2] + 3)
                pe.sem_inc(passed[2], 1)
                for n in range(TT):
                    mm = pe.transpose(tb[2][0:MM, n * P:(n + 1) * P], eo[:, n, :], ident[:, :])
                mm.then_inc(t_full[2], 1)
                pe.wait_ge(t_out[2], g * TU[2] + 4)
                for r in range(2):
                    for o in range(4):
                        k = (4 * r + o) * P
                        tile(3 + E1 + r, o, 1, lambda c: wc_s[:, k:k + P], lambda c: eoT[:, :])
                for o in range(4):
                    pe.wait_ge(m_free[o], g * MU + (5 + E1))
                for o in range(4):
                    tile(5 + E1, o, HC, lambda c: hT[:, c, o * P:(o + 1) * P], lambda c: wd_s[:, c, :])

        @block.scalar
        def _(act):
            act.wait_ge(w_in, 16 * (NW - 1))
            with act.Fori(0, NG) as g:

                def evac(row, o, dst, func, bias):
                    act.wait_ge(m_full[o], g * MU + (row + 1))
                    act.activation(dst, m[o][:, :], func, bias=bias).then_inc(m_free[o], 1)

                act.wait_ge(m_full[3], g * MU)
                for use in range(2):
                    if use == 1:
                        act.wait_ge(m_full[3], g * MU + 1)
                    for c in range(C):
                        act.wait_ge(t_full[c], g * TU[c] + (use + 1))
                        act.copy(xT[:, c, :], tb[c][:, :]).then_inc(t_out[c], 1)
                for r in range(2):
                    for o in range(4):
                        k = 4 * r + o
                        evac(1 + r, o, hT[:, k, :], ACT.Sigmoid, be_c[:, k:k + 1])
                act.wait_ge(t_full[1], g * TU[1] + 3)
                act.activation(contT[:, :], tb[1][0:MM, :], ACT.Identity, bias=bs_c[:, 0:1]).then_inc(t_out[1], 1)
                for e in range(E1):
                    if e >= 2:
                        act.wait_ge(he_used, g * (E1 - 1) + (e - 1))
                    for o in range(4):
                        evac(3 + e, o, he[e % 2][:, o, :], ACT.Relu, b1_c[:, e, o:o + 1])
                    if e == 0:
                        act.wait_ge(lg_done, g + 1)
                        act.activation(ex[:, :, :], lg[:, :, :], ACT.Exp).then_inc(ex_done, 1)
                act.wait_ge(t_full[2], g * TU[2] + 4)
                act.copy(eoT[:, :], tb[2][0:MM, :]).then_inc(t_out[2], 1)
                for r in range(2):
                    for o in range(4):
                        k = 4 * r + o
                        evac(3 + E1 + r, o, hT[:, k, :], ACT.Sigmoid, bc_c[:, k:k + 1])

        @block.vector
        def _(dve):
            steps = Steps(dve, dsem, 90)
            dve.wait_ge(w_in, 16 * (NW - 1))
            with dve.Fori(0, NG) as g:
                steps.begin(g)
                go = lambda ins: (steps.did(ins), steps.settle())
                dve.wait_ge(in_sem, 32 * g + 32)
                for n in range(TT):
                    steps.did(dve.tensor_tensor(acc[:, n, :], acc[:, n, :], rows[:, 0, :], ALU.add))
                steps.settle()
                for n in range(TT):
                    dve.wait_ge(m_full[n], g * MU + 1)
                    dve.tensor_tensor(acc[:, n, :], m[n][:, :], acc[:, n, :], ALU.add).then_inc(m_free[n], 1)
                for n in range(TT):
                    dve.wait_ge(m_free[n], g * MU + 1)
                layer_norm(steps, dve, passed[3], acc, ln, stats, mv, rstd)
                dve.sem_inc(ln_done, 1)
                dve.wait_ge(t_full[0], g * TU[0] + 3)
                logits = tb[0][:, 0:TT * E1].rearrange("p (n e) -> p n e", e=E1)
                go(dve.tensor_tensor(lg[:, :, :], logits, br_r[:, :].unsqueeze(1).to_broadcast([P, TT, E1]), ALU.add))
                dve.sem_inc(t_out[0], 1)
                go(dve.tensor_reduce(red[:, :, :], lg[:, :, :], X, ALU.max))
                go(dve.tensor_tensor(lg[:, :, :], lg[:, :, :], red[:, :, :].to_broadcast([P, TT, E1]), ALU.subtract))
                dve.sem_inc(lg_done, 1)
                dve.wait_ge(ex_done, g + 1)
                go(dve.tensor_reduce(red[:, :, :], ex[:, :, :], X, ALU.add))
                go(dve.reciprocal(red[:, :, :], red[:, :, :]))
                go(dve.tensor_tensor(ex[:, :, :], ex[:, :, :], red[:, :, :].to_broadcast([P, TT, E1]), ALU.mult))
                top_two(steps, dve, ex[:, :, :], ahead[:, :, :], gt[:, :, :, :], eq[:, :, :, :], rank[:, :, :], sel[:, :, :])
                go(dve.tensor_tensor(ex[:, :, :], ex[:, :, :], sel[:, :, :], ALU.mult))
                go(dve.tensor_reduce(red[:, :, :], ex[:, :, :], X, ALU.add))
                go(dve.reciprocal(red[:, :, :], red[:, :, :]))
                go(dve.tensor_tensor(ex[:, :, :], ex[:, :, :], red[:, :, :].to_broadcast([P, TT, E1]), ALU.mult))
                for n in range(TT):
                    dve.wait_ge(t_full[n], g * TU[n] + [4, 4, 3, 3][n])
                    dve.tensor_tensor(y[:, n, :, :].rearrange("p e d -> p (e d)"), tb[n][:, :], rows[:, 4, :],
                                      ALU.add).then_inc(t_out[n], 1)
                for n in range(TT):
                    dve.wait_ge(t_out[n], g * TU[n] + [4, 4, 3, 3][n])
                    steps.did(dve.tensor_tensor(y[:, n, :, :], y[:, n, :, :],
                                                ex[:, n, :].unsqueeze(2).to_broadcast([P, E1, MM]), ALU.mult))
                steps.settle()
                for n in range(TT):
                    steps.did(dve.tensor_reduce(eo[:, n, :], y[:, n, :, :].rearrange("p e d -> p d e"), X, ALU.add))
                steps.settle()
                dve.sem_inc(eo_done, 1)
                for n in range(TT):
                    dve.wait_ge(m_full[n], g * MU + MU)
                    dve.tensor_tensor(ln[:, n, :], m[n][:, :], rows[:, 1, :], ALU.add).then_inc(m_free[n], 1)
                for n in range(TT):
                    dve.wait_ge(m_free[n], g * MU + MU)
                layer_norm(steps, dve, passed[3], ln, ca, stats, mv, rstd)
                dve.sem_inc(ln_done, 1)
                for n in range(TT):
                    steps.did(dve.tensor_tensor(ca[:, n, :], ca[:, n, :], rows[:, 2, :], ALU.mult))
                steps.settle()
                for n in range(TT):
                    steps.did(dve.tensor_tensor(ca[:, n, :], ca[:, n, :], rows[:, 3, :], ALU.add))
                steps.settle()
                for n in range(TT):
                    steps.did(dve.tensor_tensor(acc[:, n, :], acc[:, n, :], ca[:, n, :], ALU.add))
                steps.settle()
                dve.sem_inc(out_done, 1)
                steps.end()

        @block.gpsimd
        def _(pool):
            od = out.rearrange("(n p) d -> p n d", p=P)
            with pool.Fori(0, NG) as g:
                pool.wait_ge(out_done, g + 1)
                pool.sem_inc(passed[1], 1)
                pool.dma_start(od[:, bass.ds(g * TT, TT), :], acc[:, :, :]).then_inc(stored, 16)
            pool.wait_ge(stored, 16 * NG)


def program(nc, a, out):
    scratch = lambda name, shape, dt=F32: nc.dram_tensor(name, shape, dt).ap()
    k0h, k0l = (scratch(f"k0_{n}", [B * T // G * D, G], F32R) for n in ("hi", "lo"))
    q0h, q0l, q1h, q1l, k1h, k1l = (scratch(n, [B * S // G * D, G], F32R)
                                    for n in ("q0_hi", "q0_lo", "q1_hi", "q1_lo", "k1_hi", "k1_lo"))
    v0, v1 = scratch("v0", [B * T, H * V1]), scratch("v1", [B * S, H * V1])
    tables = [scratch(f"table{b}", [H * ROWS * PAIR]) for b in range(B)]
    att0, att1, x_part, x2, qp, cx = (scratch(n, [B * S, D]) for n in ("att0", "att1", "x_part", "x2", "qp", "cx"))
    idx, wt = scratch("idx", [B * S, NS], I32), scratch("wt", [B * S, NS * 2])
    with ExitStack() as ctx:
        ident = ctx.enter_context(nc.sbuf_tensor("ident", [P, P], F32))
        identb = ctx.enter_context(nc.sbuf_tensor("identb", [P, P], BF16))
        ahead = ctx.enter_context(nc.sbuf_tensor("ahead", [P, E0, E0], F32))
        x = a["x"].rearrange("b s d -> (b s) d")
        constants(nc, ident, identb, ahead)
        project_context(nc, a["ctxT"], a["L0_xattn_WkT"], a["L0_xattn_bk"], a["L0_xattn_WvT"], a["L0_xattn_bv"],
                        a["L1_xattn_WkT"], a["L1_xattn_bk"], a["L1_xattn_WvT"], a["L1_xattn_bv"], k0h, k0l, v0, tables)
        project_query(nc, x, a["L0_xattn_WqT"], a["L0_xattn_bq"], ident, q0h, q0l)
        attention(nc, "cross", T, q0h, q0l, k0h, k0l, v0, ident, identb, att0)
        ffn_moe(nc, x, att0, a["L0_xattn_WoT"], a["L0_xattn_bo"], a["L0_ffn_W_qkv"], a["L0_ffn_b_qkv"],
                a["L0_ffn_W_gate"], a["L0_ffn_b_gate"], a["L0_ffn_W_experts"], a["L0_ffn_b_experts"], ident, ahead,
                q1h, q1l, k1h, k1l, v1, x_part)
        attention(nc, "self", S, q1h, q1l, k1h, k1l, v1, ident, identb, att1)
        sample_positions(nc, x_part, att1, a["mask_BxS2_if0"], a["L1_xattn_WqT"], a["L1_xattn_bq"],
                         a["L1_xattn_WoffT"], a["L1_xattn_boff"], ident, x2, qp, idx, wt)
        sampled_attention(nc, tables, qp, idx, wt, cx)
        ffn_last(nc, x2, cx, a["L1_xattn_WoT"], a["L1_xattn_bo"], a["L1_ffn_W_enc"], a["L1_ffn_b_enc"],
                 a["L1_ffn_W_s2c"], a["L1_ffn_b_s2c"], a["L1_ffn_Wr"], a["L1_ffn_br"], a["L1_ffn_W1"],
                 a["L1_ffn_b1"], a["L1_ffn_W2"], a["L1_ffn_b2"].rearrange("e m -> (e m)"), a["L1_ffn_W_c2s"],
                 a["L1_ffn_b_c2s"], a["L1_ffn_W_dec"], a["L1_ffn_b_dec"], a["L1_ffn_ln_g"], a["L1_ffn_ln_b"],
                 ident, ahead, out.rearrange("b s d -> (b s) d"))


_TURNED = ["L0_xattn_Wq", "L0_xattn_Wk", "L0_xattn_Wv", "L0_xattn_Wo", "L1_xattn_Wq", "L1_xattn_Wk", "L1_xattn_Wv",
           "L1_xattn_Woff", "L1_xattn_Wo"]


def kernel(**inputs):
    import numpy as _np
    import concourse.bacc as _bacc
    from concourse import mybir as _mybir
    from concourse.bass_utils import run_bass_kernel_spmd as _run

    nc = _bacc.Bacc("TRN2", target_bir_lowering=False, num_devices=1)
    arrays, aps = {}, {}
    for name, value in inputs.items():
        v = _np.asarray(value)
        if name in _TURNED:
            name, v = name + "T", v.T
        elif name == "ctx_1024":
            name, v = "ctxT", v.reshape(B * T, D).T
        v = _np.ascontiguousarray(v)
        arrays[f"in_{name}"] = v
        aps[name] = nc.dram_tensor(f"in_{name}", v.shape, _mybir.dt.from_np(v.dtype), kind="ExternalInput").ap()
    out = nc.dram_tensor("out_0", (B, S, D), F32, kind="ExternalOutput").ap()
    program(nc, aps, out)
    r = _run(nc, [arrays], core_ids=[0])
    return r.results[0]["out_0"]
```

```python
from contextlib import ExitStack

import concourse.bass as bass
from concourse import mybir

F32 = mybir.dt.float32
F32R = mybir.dt.float32r
BF16 = mybir.dt.bfloat16
I32 = mybir.dt.int32
ALU = mybir.AluOpType
ACT = mybir.ActivationFunctionType
X = mybir.AxisListType.X

P = 128
B, S, T, D = 2, 1024, 2048, 512
H, HD = 16, 32
C = D // P
G = 512
TT = G // P
NK5 = 5
NS = H * NK5
ROWS = T + 4
PAIR = 2 * HD
E0 = 8
HID, MM, EH, E1 = 1024, 64, 512, 8
V1 = HD + 1
EPS = 1e-5
SCALE = float(HD) ** -0.5


class Steps:

    def __init__(self, eng, sem, per):
        self.eng, self.sem, self.per = eng, sem, per

    def begin(self, it):
        self.it, self.k = it, 0

    def did(self, ins):
        ins.then_inc(self.sem, 1)
        self.k += 1
        return ins

    def settle(self):
        self.eng.wait_ge(self.sem, self.it * self.per + self.k)

    def end(self):
        assert self.k == self.per, f"{self.k} steps, not {self.per}"


class Tools:
    def __init__(self, nc, ctx, tag):
        self.nc, self.ctx, self.tag, self.own = nc, ctx, tag, []

    def sb(self, name, shape, dt=F32):
        return self.ctx.enter_context(self.nc.sbuf_tensor(f"{self.tag}_{name}", shape, dt))

    def ps(self, name, shape, dt=F32):
        return self.ctx.enter_context(self.nc.psum_tensor(f"{self.tag}_{name}", shape, dt))

    def sem(self, name):
        self.own.append(self.nc.alloc_semaphore(f"{self.tag}_{name}"))
        return self.own[-1]

    def sems(self, name, n):
        return [self.sem(f"{name}{i}") for i in range(n)]


    def block(self):
        self.ctx.callback(self.retire)
        return self.ctx.enter_context(self.nc.Block())

    def retire(self):
        self.nc.clear_and_free_semaphores(self.own)
        self.nc.all_engine_barrier()


def row_of(vec, n):
    return bass.AP(vec.tensor, vec.offset, [[0, P], [1, n]])


def layer_norm(steps, eng, passed, x, out, stats, mv, rstd):
    var, half, y, sq = (rstd[:, i, :] for i in range(4))
    for t in range(TT):
        steps.did(eng.bn_stats(stats[:, t, :], x[:, t, :]))
    steps.settle()
    eng.sem_inc(passed, 1)
    for t in range(TT):
        steps.did(eng.bn_aggr(mv[:, t, :], stats[:, t, :]))
    steps.settle()
    steps.did(eng.tensor_scalar(var, mv[:, :, 1], EPS, None, ALU.add))
    steps.settle()
    steps.did(eng.tensor_scalar(y.bitcast(I32), var.bitcast(I32), 1, None, ALU.logical_shift_right))
    steps.did(eng.tensor_scalar(half, var, -0.5, None, ALU.mult))
    steps.settle()
    steps.did(eng.tensor_scalar(y.bitcast(I32), y.bitcast(I32), -1.0, float(0x5F3759DF), ALU.mult, ALU.add))
    steps.settle()
    for _ in range(3):
        steps.did(eng.tensor_tensor(sq, y, y, ALU.mult))
        steps.settle()
        steps.did(eng.tensor_tensor(sq, sq, half, ALU.mult))
        steps.settle()
        steps.did(eng.scalar_tensor_tensor(out=y, in0=sq, scalar=1.5, in1=y, op0=ALU.add, op1=ALU.mult))
        steps.settle()
    for t in range(TT):
        steps.did(eng.tensor_scalar(out[:, t, :], x[:, t, :], mv[:, t, 0:1], y[:, t:t + 1],
                                    ALU.subtract, ALU.mult))
    steps.settle()


def constants(nc, ident, identb, ahead):
    with ExitStack() as ctx:
        t = Tools(nc, ctx, "const")
        made = t.sem("made")
        passed = t.sems("passed", 4)
        block = t.block()

        @block.gpsimd
        def _(pool):
            pool.memset(ident[:, :], 0.0).then_inc(made, 1)
            pool.memset(identb[:, :], 0.0).then_inc(made, 1)
            pool.memset(ahead[:, :, :], 0.0).then_inc(made, 1)
            pool.wait_ge(made, 3)
            for m in (ident, identb):
                pool.affine_select(out=m[:, :], in_=m[:, :], compare_op=ALU.not_equal, fill=1.0, base=0,
                                   pattern=[[-1, P]], channel_multiplier=1).then_inc(made, 1)
            pool.affine_select(out=ahead[:, :, :], in_=ahead[:, :, :], compare_op=ALU.is_ge, fill=1.0, base=0,
                               pattern=[[-1, E0], [1, E0]], channel_multiplier=0).then_inc(made, 1)
            pool.wait_ge(made, 6)


def project_context(nc, ctxT, wkT0, bk0, wvT0, bv0, wkT1, bk1, wvT1, bv1, k_hi, k_lo, v_ones, tables):
    NG = B * T // G
    with ExitStack() as ctx:
        t = Tools(nc, ctx, "ctx")
        w = [t.sb(f"w{i}", [P, C, D]) for i in range(4)]
        bk0_c = t.sb("bk0_c", [P, C])
        rows = t.sb("rows", [P, 3, D])
        x = t.sb("x", [P, 2, C, G])
        kh = t.sb("kh", [P, 2, C, G], F32R)
        kl = t.sb("kl", [P, 2, C, G], F32R)
        vo = t.sb("vo", [P, 2, TT, H, V1])
        kv = t.sb("kv", [P, 2, TT, H, 2, HD])
        zero = t.sb("zero", [H, 2 * PAIR])
        R = 8
        bank = [t.ps(f"bank{i}", [P, G]) for i in range(R)]
        w_in = t.sem("w_in")
        x_in, x_used = t.sems("x_in", 2), t.sems("x_used", 2)
        full, free = t.sems("full", R), t.sems("free", R)
        hi_done, out_ready = t.sem("hi_done"), t.sem("out_ready")
        stored, preset, zeroed, zeros_out = t.sems("stored", 2), t.sem("preset"), t.sem("zeroed"), t.sem("zeros_out")
        ND = 2 + 1 + TT
        N = 4 * TT
        passed = t.sems("passed", 4)
        block = t.block()

        @block.sync
        def _(sp):
            for i, src in enumerate((wkT0, wvT0, wkT1, wvT1)):
                sp.dma_start(w[i][:, :, :], src.rearrange("(c p) n -> p c n", p=P)).then_inc(w_in, 16)
            sp.dma_start(bk0_c[:, :], bk0.rearrange("(c p) -> p c", p=P), allow_slow_non_contiguous=True).then_inc(w_in, 16)
            for i, src in enumerate((bv0, bk1, bv1)):
                sp.dma_start(rows[:, i, :], row_of(src, D)).then_inc(w_in, 16)
            xs = ctxT.rearrange("(c p) t -> p c t", p=P)
            with sp.Fori(0, NG // 2) as j:
                for u in range(2):
                    sp.wait_ge(x_used[u], j)
                    sp.sem_inc(passed[0], 1)
                    sp.dma_start(x[:, u, :, :], xs[:, :, bass.ds((2 * j + u) * G, G)]).then_inc(x_in[u], 16)

        @block.tensor
        def _(pe):
            pe.wait_ge(w_in, 16 * 8)
            with pe.Fori(0, NG // 2) as j:
                for u in range(2):
                    pe.wait_ge(x_in[u], 16 * j + 16)
                    for k in range(N):
                        kind, o = divmod(k, TT)
                        pe.wait_ge(free[k % R], (2 * j + u) * (N // R) + k // R)
                        for c in range(C):
                            if kind == 0:
                                mm = pe.matmul(bank[k % R][:, :], w[0][:, c, o * P:(o + 1) * P], x[:, u, c, :],
                                               start=(c == 0), stop=(c == C - 1))
                            else:
                                mm = pe.matmul(bank[k % R][:, :], x[:, u, c, o * P:(o + 1) * P], w[kind][:, c, :],
                                               start=(c == 0), stop=(c == C - 1))
                        mm.then_inc(full[k % R], 1)
                    pe.wait_ge(full[(N - 1) % R], (2 * j + u + 1) * (N // R))
                    pe.sem_inc(x_used[u], 1)

        @block.scalar
        def _(act):
            act.wait_ge(w_in, 16 * 8)
            with act.Fori(0, NG // 2) as j:
                for u in range(2):
                    act.wait_ge(stored[u], 16 * ND * j)
                    for o in range(C):
                        act.wait_ge(full[o % R], (2 * j + u) * (N // R) + o // R + 1)
                        act.activation(kh[:, u, o, :], bank[o % R][:, :], ACT.Identity,
                                       bias=bk0_c[:, o:o + 1]).then_inc(hi_done, 1)

        @block.vector
        def _(dve):
            dve.memset(vo[:, :, :, :, HD:V1], 1.0).then_inc(preset, 1)
            dve.wait_ge(preset, 1)
            dve.wait_ge(w_in, 16 * 8)
            with dve.Fori(0, NG // 2) as j:
                for u in range(2):
                    dve.wait_ge(stored[u], 16 * ND * j)
                    for k in range(N):
                        kind, o = divmod(k, TT)
                        dve.wait_ge(full[k % R], (2 * j + u) * (N // R) + k // R + 1)
                        if kind == 0:
                            dve.wait_ge(hi_done, (2 * j + u) * C + o + 1)
                            ins = dve.scalar_tensor_tensor(out=kl[:, u, o, :], in0=bank[k % R][:, :],
                                                           scalar=bk0_c[:, o:o + 1], in1=kh[:, u, o, :].bitcast(F32),
                                                           op0=ALU.add, op1=ALU.subtract)
                        else:
                            src = bank[k % R][:, :].rearrange("p (h d) -> p h d", h=H)
                            add = rows[:, kind - 1, :].rearrange("p (h d) -> p h d", h=H)
                            dst = vo[:, u, o, :, 0:HD] if kind == 1 else kv[:, u, o, :, kind - 2, :]
                            ins = dve.tensor_tensor(dst, src, add, ALU.add)
                        ins.then_inc(free[k % R], 1)
                    dve.wait_ge(free[(N - 1) % R], (2 * j + u + 1) * (N // R))
                    dve.sem_inc(out_ready, 1)

        @block.gpsimd
        def _(pool):
            pool.memset(zero[:, :], 0.0).then_inc(zeroed, 1)
            pool.wait_ge(zeroed, 1)
            for tab in tables:
                rv = tab.rearrange("(h r d) -> h r d", h=H, r=ROWS)
                pool.dma_start(rv[:, 0:2, :], zero[:, :].rearrange("h (r d) -> h r d", r=2)).then_inc(zeros_out, 16)
                pool.dma_start(rv[:, T + 2:ROWS, :], zero[:, :].rearrange("h (r d) -> h r d", r=2)).then_inc(zeros_out, 16)
            for b in range(B):
                tab = tables[b].rearrange("(h r d) -> r h d", h=H, r=ROWS)
                with pool.Fori(0, NG // B // 2) as j:
                    for u in range(2):
                        g = (NG // B) * b + 2 * j + u
                        pool.wait_ge(out_ready, g + 1)
                        pool.sem_inc(passed[1], 1)
                        done = stored[u]
                        hi = k_hi.rearrange("(g c p) t -> g p c t", c=C, p=P)
                        lo = k_lo.rearrange("(g c p) t -> g p c t", c=C, p=P)
                        pool.dma_start(hi[bass.ds(g, 1), :, :, :].rearrange("a p c t -> (a p) c t").bitcast(F32),
                                       kh[:, u, :, :].bitcast(F32)).then_inc(done, 16)
                        pool.dma_start(lo[bass.ds(g, 1), :, :, :].rearrange("a p c t -> (a p) c t").bitcast(F32),
                                       kl[:, u, :, :].bitcast(F32)).then_inc(done, 16)
                        vd = v_ones.rearrange("(n p) f -> p n f", p=P)
                        pool.dma_start(vd[:, bass.ds(g * TT, TT), :],
                                       vo[:, u, :, :, :].rearrange("p n h d -> p n (h d)")).then_inc(done, 16)
                        for o in range(TT):
                            pool.dma_start(tab[bass.ds((2 * j + u) * G + (o * P + 2), P), :, :],
                                           kv[:, u, o, :, :, :].rearrange("p h a d -> p h (a d)")).then_inc(done, 16)
            for u in range(2):
                pool.wait_ge(stored[u], 16 * ND * (NG // 2))
            pool.wait_ge(zeros_out, 16 * 2 * B)


def project_query(nc, x_dram, wqT, bq, ident, q_hi, q_lo):
    NG = B * S // G
    with ExitStack() as ctx:
        t = Tools(nc, ctx, "qry")
        w = t.sb("w", [P, C, D])
        bq_c = t.sb("bq_c", [P, C])
        x = t.sb("x", [P, 2, TT, D])
        ln = t.sb("ln", [P, 2, TT, D])
        lnT = t.sb("lnT", [P, 2, C, G])
        stats, mv, rstd = t.sb("stats", [P, TT, 6]), t.sb("mv", [P, TT, 2]), t.sb("rstd", [P, 4, TT])
        qh = t.sb("qh", [P, 2, C, G], F32R)
        ql = t.sb("ql", [P, 2, C, G], F32R)
        tb = [t.ps(f"tb{i}", [P, G]) for i in range(4)]
        qb = [t.ps(f"qb{i}", [P, G]) for i in range(4)]
        w_in, x_in, x_used = t.sem("w_in"), t.sems("x_in", 2), t.sem("x_used")
        dsem, ln_done, t_full, t_out = t.sem("dve_steps"), t.sem("ln_done"), t.sem("t_full"), t.sem("t_out")
        q_full, hi_done, lo_done = t.sem("q_full"), t.sem("hi_done"), t.sem("lo_done")
        stored = t.sems("stored", 2)
        passed = t.sems("passed", 4)
        block = t.block()

        @block.sync
        def _(sp):
            sp.dma_start(w[:, :, :], wqT.rearrange("(c p) n -> p c n", p=P)).then_inc(w_in, 16)
            sp.dma_start(bq_c[:, :], bq.rearrange("(c p) -> p c", p=P), allow_slow_non_contiguous=True).then_inc(w_in, 16)
            xs = x_dram.rearrange("(n p) d -> p n d", p=P)
            with sp.Fori(0, NG // 2) as j:
                for u in range(2):
                    sp.wait_ge(ln_done, 2 * j)
                    sp.sem_inc(passed[0], 1)
                    sp.dma_start(x[:, u, :, :], xs[:, bass.ds((2 * j + u) * TT, TT), :]).then_inc(x_in[u], 16)

        @block.vector
        def _(dve):
            steps = Steps(dve, dsem, 25)
            dve.wait_ge(w_in, 32)
            with dve.Fori(0, NG // 2) as j:
                for u in range(2):
                    g = 2 * j + u
                    steps.begin(g)
                    dve.wait_ge(x_in[u], 16 * j + 16)
                    dve.wait_ge(t_full, 2 * C * j)
                    layer_norm(steps, dve, passed[3], x[:, u, :, :], ln[:, u, :, :], stats, mv, rstd)
                    steps.end()
                    dve.sem_inc(ln_done, 1)
                    dve.wait_ge(stored[u], 32 * j)
                    for o in range(C):
                        dve.wait_ge(q_full, g * C + o + 1)
                        dve.wait_ge(hi_done, g * C + o + 1)
                        dve.scalar_tensor_tensor(out=ql[:, u, o, :], in0=qb[o][:, :], scalar=bq_c[:, o:o + 1],
                                                 in1=qh[:, u, o, :].bitcast(F32), op0=ALU.add,
                                                 op1=ALU.subtract).then_inc(lo_done, 1)

        @block.tensor
        def _(pe):
            pe.wait_ge(w_in, 32)
            with pe.Fori(0, NG // 2) as j:
                for u in range(2):
                    g = 2 * j + u
                    pe.wait_ge(ln_done, g + 1)
                    pe.wait_ge(t_out, g * C)
                    for c in range(C):
                        for n in range(TT):
                            mm = pe.transpose(tb[c][:, n * P:(n + 1) * P], ln[:, u, n, c * P:(c + 1) * P], ident[:, :])
                        mm.then_inc(t_full, 1)
                    pe.wait_ge(t_out, g * C + C)
                    pe.wait_ge(lo_done, g * C)
                    for o in range(C):
                        for c in range(C):
                            mm = pe.matmul(qb[o][:, :], w[:, c, o * P:(o + 1) * P], lnT[:, u, c, :],
                                           start=(c == 0), stop=(c == C - 1))
                        mm.then_inc(q_full, 1)

        @block.scalar
        def _(act):
            act.wait_ge(w_in, 32)
            with act.Fori(0, NG // 2) as j:
                for u in range(2):
                    g = 2 * j + u
                    act.wait_ge(q_full, 2 * C * j)
                    for c in range(C):
                        act.wait_ge(t_full, g * C + c + 1)
                        act.copy(lnT[:, u, c, :], tb[c][:, :]).then_inc(t_out, 1)
                    act.wait_ge(stored[u], 32 * j)
                    for o in range(C):
                        act.wait_ge(q_full, g * C + o + 1)
                        act.activation(qh[:, u, o, :], qb[o][:, :], ACT.Identity,
                                       bias=bq_c[:, o:o + 1]).then_inc(hi_done, 1)

        @block.gpsimd
        def _(pool):
            hi = q_hi.rearrange("(g c p) t -> g p c t", c=C, p=P)
            lo = q_lo.rearrange("(g c p) t -> g p c t", c=C, p=P)
            with pool.Fori(0, NG // 2) as j:
                for u in range(2):
                    g = 2 * j + u
                    pool.wait_ge(lo_done, g * C + C)
                    pool.sem_inc(passed[1], 1)
                    for dst, src in ((hi, qh), (lo, ql)):
                        pool.dma_start(dst[bass.ds(g, 1), :, :, :].rearrange("a p c t -> (a p) c t").bitcast(F32),
                                       src[:, u, :, :].bitcast(F32)).then_inc(stored[u], 16)
            for u in range(2):
                pool.wait_ge(stored[u], 32 * (NG // 2))


class Samples:
    HS = H // 2
    SS = NS // 2

    def __init__(self, t, table, qp_dram, idx_dram, wt_dram, out, first, tiles):
        HS, SS = self.HS, self.SS
        self.table, self.drams, self.first, self.tiles = table, (qp_dram, idx_dram, wt_dram, out), first, tiles
        self.rows = [t.sb(f"rows{i}", [P, SS, 2 * PAIR]) for i in range(2)]
        self.idx = [t.sb(f"idx{i}", [P, SS], I32) for i in range(2)]
        self.wt = [t.sb(f"wt{i}", [P, SS, 2]) for i in range(2)]
        self.qp = [t.sb(f"qp{i}", [P, HS * HD]) for i in range(2)]
        self.prod = t.sb("prod", [P, HS // 2, 2 * NK5, HD])
        self.s10, self.a10 = t.sb("s10", [P, HS, NK5, 2]), t.sb("a10", [P, HS, NK5, 2])
        self.s5, self.red = t.sb("s5", [P, HS, NK5]), t.sb("sred", [P, HS, 1])
        self.o = [t.sb(f"so{i}", [P, HS * HD]) for i in range(2)]
        self.idx_in, self.qw_in, self.gathered = t.sems("idx_in", 2), t.sems("qw_in", 2), t.sems("gathered", 2)
        self.steps_sem, self.s_done, self.e_done = t.sem("sample_steps"), t.sem("s_done"), t.sem("e_done")
        self.o_done, self.o_free, self.stored = t.sems("so_done", 2), t.sems("so_free", 2), t.sems("so_stored", 2)
        self.passed = t.sem("samples_passed")

    def gather(self, pool):
        SS, W = self.SS, self.HS * HD
        qp_dram, idx_dram, wt_dram, out = self.drams

        def load_idx(j, u):
            pool.dma_start(self.idx[u][:, :], idx_dram[bass.ds((j + self.first) * P, P), u * SS:(u + 1) * SS]).then_inc(self.idx_in[u], 16)

        def load_qw(j, u):
            r = bass.ds((j + self.first) * P, P)
            pool.dma_start(self.wt[u][:, :, :].rearrange("p s a -> p (s a)"), wt_dram[r, 2 * u * SS:2 * (u + 1) * SS]).then_inc(self.qw_in[u], 16)
            pool.dma_start(self.qp[u][:, :], qp_dram[r, u * W:(u + 1) * W]).then_inc(self.qw_in[u], 16)

        def rows_of(j, u, s0, s1):
            for s in range(s0, s1):
                pool.indirect_dma_start(self.rows[u][:, s, :], None, self.table.rearrange("(n a) -> n a", a=1),
                                        bass.IndirectOffsetOnAxis(self.idx[u][:, s:s + 1], 0)).then_inc(self.gathered[u], 16)

        def store(j, u):
            pool.wait_ge(self.o_done[u], j + 1)
            pool.sem_inc(self.passed, 1)
            pool.dma_start(out[bass.ds((j + self.first) * P, P), u * W:(u + 1) * W], self.o[u][:, :]).then_inc(self.stored[u], 16)

        def half(j, u, first, last):
            before = None if first and u == 0 else (j, 0) if u == 1 else (j - 1, 1)
            after = None if last and u == 1 else (j, 1) if u == 0 else (j + 1, 0)
            pool.wait_ge(self.idx_in[u], 16 * j + 16)
            pool.sem_inc(self.passed, 1)
            rows_of(j, u, 0, SS // 2)
            if after:
                if before:
                    pool.wait_ge(self.gathered[1 - u], 16 * SS * before[0] + 16 * SS)
                    pool.sem_inc(self.passed, 1)
                load_idx(*after)
            if not first:
                pool.wait_ge(self.stored[u], 16 * j)
                pool.sem_inc(self.o_free[u], 1)
            rows_of(j, u, SS // 2, SS)
            if before:
                store(*before)
            if after:
                load_qw(*after)

        for u in range(2):
            pool.sem_inc(self.o_free[u], 1)
        load_idx(0, 0)
        load_qw(0, 0)
        for u in range(2):
            half(0, u, True, False)
        with pool.Fori(1, self.tiles - 1) as j:
            for u in range(2):
                half(j, u, False, False)
        for u in range(2):
            half(self.tiles - 1, u, False, True)
        store(self.tiles - 1, 1)
        for u in range(2):
            pool.wait_ge(self.stored[u], 16 * self.tiles)

    def views(self, u):
        kv = self.rows[u][:, :, :].rearrange("p (h k) (m a d) -> p h (k m) a d", k=NK5, a=2, d=HD)
        return kv, self.wt[u][:, :, :].rearrange("p (h k) m -> p h k m", h=self.HS)

    def scores(self, dve, j, u):
        HS, s5, red, s10 = self.HS, self.s5[:, :, :], self.red[:, :, :], self.s10
        kv, w = self.views(u)
        self.steps = Steps(dve, self.steps_sem, 16)
        self.steps.begin(2 * j + u)
        go = lambda ins: (self.steps.did(ins), self.steps.settle())
        q = self.qp[u][:, :].rearrange("p (h d) -> p h d", h=HS)
        dve.wait_ge(self.gathered[u], 16 * self.SS * j + 16 * self.SS)
        dve.wait_ge(self.qw_in[u], 32 * j + 32)
        for h in (0, HS // 2):
            r = slice(h, h + HS // 2)
            go(dve.tensor_tensor(self.prod[:, :, :, :], kv[:, r, :, 0, :],
                                 q[:, r, :].unsqueeze(2).to_broadcast([P, HS // 2, 2 * NK5, HD]), ALU.mult))
            go(dve.tensor_reduce(s10[:, r, :, :].rearrange("p h k m -> p h (k m)"), self.prod[:, :, :, :], X, ALU.add))
        go(dve.tensor_tensor(s10[:, :, :, :], s10[:, :, :, :], w, ALU.mult))
        go(dve.tensor_tensor(s5, s10[:, :, :, 0], s10[:, :, :, 1], ALU.add))
        go(dve.tensor_reduce(red, s5, X, ALU.max))
        go(dve.tensor_tensor(s5, s5, red.to_broadcast([P, HS, NK5]), ALU.subtract))
        dve.sem_inc(self.s_done, 1)

    def weights(self, act, j, u):
        act.wait_ge(self.s_done, 2 * j + (u + 1))
        act.activation(self.s5[:, :, :], self.s5[:, :, :], ACT.Exp, scale=SCALE).then_inc(self.e_done, 1)

    def output(self, dve, j, u):
        HS, s5, red, a10 = self.HS, self.s5[:, :, :], self.red[:, :, :], self.a10[:, :, :, :]
        kv, w = self.views(u)
        go = lambda ins: (self.steps.did(ins), self.steps.settle())
        dve.wait_ge(self.e_done, 2 * j + (u + 1))
        go(dve.tensor_reduce(red, s5, X, ALU.add))
        go(dve.reciprocal(red, red))
        go(dve.tensor_tensor(s5, s5, red.to_broadcast([P, HS, NK5]), ALU.mult))
        go(dve.tensor_tensor(a10, w, s5.unsqueeze(3).to_broadcast([P, HS, NK5, 2]), ALU.mult))
        dve.wait_ge(self.o_free[u], j + 1)
        for h in (0, HS // 2):
            r = slice(h, h + HS // 2)
            go(dve.tensor_tensor(self.prod[:, :, :, :], kv[:, r, :, 1, :], a10[:, r, :, :].rearrange("p h k m -> p h (k m)")
                                 .unsqueeze(3).to_broadcast([P, HS // 2, 2 * NK5, HD]), ALU.mult))
            go(dve.tensor_reduce(self.o[u][:, h * HD:(h + HS // 2) * HD].rearrange("p (h d) -> p h d", h=HS // 2),
                                 self.prod[:, :, :, :].rearrange("p h s d -> p h d s"), X, ALU.add))
        dve.sem_inc(self.o_done[u], 1)
        self.steps.end()


def attention(nc, tag, TK, q_hi, q_lo, k_hi, k_lo, v_ones, ident, identb, out, batches, samples=None):
    NK = TK // P
    QG, KG = S // G, TK // G
    WA = 1024
    NKC = TK // WA
    NA = (S // P) * NKC
    NQ = S // P
    HALF = S // 2
    HU = 4
    NH = len(batches) * H
    PR = 4
    R = 4
    EARLY = 3
    assert NA == NK
    units = [[(1, s + EARLY)] if s + EARLY <= NA else [(2, s + EARLY - NA - 1)] for s in range(NK)]
    units[NK - 1].append((2, EARLY - 1))
    assert units[NK - 2] == [(2, 0)] and units[NK - 1] == [(2, 1), (2, 2)]
    with ExitStack() as ctx:
        t = Tools(nc, ctx, tag)
        kst = [t.sb(f"kst{i}", [P, TK], F32R) for i in range(HU)]
        qst = [t.sb(f"qst{i}", [P, S], F32R) for i in range(HU)]
        v = [t.sb(f"v{i}", [P, NK, V1]) for i in range(HU)]
        p = [t.sb(f"p{i}", [P, S]) for i in range(PR)]
        oT = [t.sb(f"oT{i}", [P, HALF]) for i in range(2)]
        o = [t.sb(f"o{i}", [P, NQ, HD]) for i in range(2)]
        inv = [t.sb(f"inv{i}", [P, NQ // 2, 2, 1]) for i in range(2)]
        mx = t.sb("mx", [P, NA, 2])
        negm = t.sb("negm", [P, NQ], BF16)
        ps_a = [t.ps(f"ps_a{i}", [P, WA // 2]) for i in range(2)]
        ps_b = [t.ps(f"ps_b{i}", [P, S]) for i in range(2)]
        ps_o = [t.ps(f"ps_o{i}", [P, HALF]) for i in range(2)]
        preset, loaded = t.sem("preset"), t.sems("loaded", HU)
        a_full, a_free, negm_done = t.sems("a_full", 2), t.sems("a_free", 2), t.sem("negm_done")
        b_full, exp_done, p_used = t.sems("b_full", 2), t.sems("exp_done", 2), t.sems("p_used", PR)
        o_full, oT_done, turned = t.sems("o_full", 2), t.sems("oT_done", 2), t.sems("turned", 2)
        o_done, o_free, o_out, inv_done = t.sems("o_done", 2), t.sems("o_free", 2), t.sems("o_out", 2), t.sem("inv_done")
        stored = t.sems("stored", 2)
        LOADS = 7
        passed = t.sems("passed", 4)
        smp = Samples(t, *samples) if samples else None
        block = t.block()

        @block.sync
        def _(sp):
            qh = q_hi.rearrange("(b g r) t -> b r g t", b=B, g=QG)
            ql = q_lo.rearrange("(b g r) t -> b r g t", b=B, g=QG)
            kh = k_hi.rearrange("(b g r) t -> b r g t", b=B, g=KG)
            kl = k_lo.rearrange("(b g r) t -> b r g t", b=B, g=KG)
            vs = v_ones.rearrange("(b n p) f -> b p n f", b=B, p=P)
            ov = out.rearrange("(b q p) d -> b p q d", b=B, p=P)

            def load(b, h, u):
                for i, (part, full) in enumerate(((qh, qst), (qh, qst), (ql, qst), (kh, kst), (kl, kst), (kh, kst))):
                    r = HD * (i % 3)
                    dst = full[u][r:r + HD, :].rearrange("r (g t) -> r g t", t=G)
                    sp.dma_start(dst.bitcast(F32), part[b, bass.ds(h * HD, HD), :, :].bitcast(F32)).then_inc(loaded[u], 16)
                sp.dma_start(v[u][:, :, :], vs[b, :, :, bass.ds(h * V1, V1)]).then_inc(loaded[u], 16)

            def store(b, h, u, use):
                i, k = u % 2, use * 2 + (u // 2 + 1)
                sp.wait_ge(o_done[i], k)
                sp.sem_inc(passed[1], 1)
                sp.dma_start(ov[b, :, :, bass.ds(h * HD, HD)], o[i][:, :, :]).then_inc(stored[i], 16)
                return i, k

            def stored_out(i, k):
                sp.wait_ge(stored[i], 16 * k)
                sp.sem_inc(o_out[i], 1)

            for i in range(2):
                sp.sem_inc(o_out[i], 1)
            for u in range(HU):
                load(batches[0], u, u)
            for nb, b in enumerate(batches):
                base = nb * (H // HU)
                with sp.Fori(0, H // HU - 1) as j:
                    for u in range(HU):
                        k = store(b, j * HU + u, u, j + base)
                        load(b, j * HU + (HU + u), u)
                        stored_out(*k)
                for u in range(HU):
                    k = store(b, H - HU + u, u, base + H // HU - 1)
                    if nb + 1 < len(batches):
                        load(batches[nb + 1], u, u)
                    stored_out(*k)

        def turns(j, u, left, step, end):
            for s in range(R, NK):
                step(j, u, s, left)
            if left != 0:
                nj, nu = (j, u + 1) if u + 1 < HU else (j + 1, 0)
                for s in range(R):
                    step(nj, nu, s, None if left is None else left - 1)
            else:
                step(j, u, NK, 0)
            end(j, u)

        def all_turns(eng, step, end):
            for s in range(R):
                step(0, 0, s, None)
            with eng.Fori(0, NH // HU - 1) as j:
                for u in range(HU):
                    turns(j, u, None, step, end)
            for u in range(HU):
                turns(NH // HU - 1, u, HU - 1 - u, step, end)

        @block.tensor
        def _(pe):

            def unit(j, u, a):
                if u >= HU:
                    j, u = j + 1, u - HU
                at = (j * HU + u) * (NA + 1) + a
                if a == NA:
                    pe.wait_ge(negm_done, j * HU + u + 1)
                    for i in range(2):
                        for q in range(NQ // 2):
                            k = i * (NQ // 2) + q
                            mm = pe.matmul(ps_a[i][0:1, q * P:(q + 1) * P], negm[:, k:k + 1], identb[:, :], start=True, stop=True)
                        mm.then_inc(a_full[i], 1)
                else:
                    if a == 0:
                        pe.wait_ge(loaded[u], 16 * LOADS * j + 16 * LOADS)
                    qt, kc = divmod(a, NKC)
                    for i in range(2):
                        if not isinstance(at, int) or at > 0:
                            pe.wait_ge(a_free[i], at)
                        k = kc * WA + i * (WA // 2)
                        pe.matmul(ps_a[i][:, :], qst[u][0:96, qt * P:(qt + 1) * P], kst[u][0:96, k:k + WA // 2],
                                  start=True, stop=True).then_inc(a_full[i], 1)

            def with_v(j, u, s):
                pe.wait_ge(exp_done[s % 2], (j * HU + u) * (NK // 2) + (s // 2 + 1))
                if s == 0:
                    pe.wait_ge(o_free[u % 2], j * 2 + (u // 2 + 1))
                for i in range(2):
                    mm = pe.matmul(ps_o[u % 2][64 * i:64 * i + V1, :], v[u][:, s, :], p[s % PR][:, i * HALF:(i + 1) * HALF],
                                   start=(s == 0), stop=(s == NK - 1), skip_group_check=True)
                mm.then_inc(p_used[s % PR], 1)

            def step(j, u, s, left):
                n = j * HU + u
                if s == 0:
                    for i in range(2):
                        pe.wait_ge(a_free[i], n * (NA + 1) + (NA + 1))
                if s < NK:
                    if s >= 2 or not isinstance(n, int) or n > 0:
                        pe.wait_ge(exp_done[s % 2], n * (NK // 2) + s // 2)
                    for i in range(2):
                        mm = pe.matmul(ps_b[s % 2][:, i * 512:(i + 1) * 512], kst[u][0:97, s * P:(s + 1) * P],
                                       qst[u][0:97, i * 512:(i + 1) * 512], start=True, stop=True)
                    mm.then_inc(b_full[s % 2], 1)
                    for ahead, a in units[s][:1]:
                        if left is None or ahead <= left:
                            unit(j, u + ahead, a)
                if s > 0:
                    with_v(j, u, s - 1)
                elif not isinstance(n, int) or n > 0:
                    with_v(*((j, u - 1) if u > 0 else (j - 1, HU - 1)), NK - 1)
                if s < NK:
                    for ahead, a in units[s][1:]:
                        if left is None or ahead <= left:
                            unit(j, u + ahead, a)
                if s == 0 and not (isinstance(n, int) and n == 0) or s == NK:
                    pj, pu = (j, u) if s == NK else (j, u - 1) if u > 0 else (j - 1, HU - 1)
                    pe.wait_ge(p_used[(NK - 1) % PR], (pj * HU + pu) * (NK // PR) + NK // PR)
                    pe.sem_inc(o_full[pu % 2], 1)

            def end(j, u):
                i = u % 2
                pe.wait_ge(oT_done[i], j * 4 + (2 * (u // 2) + 2))
                for q in range(HALF // P):
                    mm = pe.transpose(ps_o[i][:, q * P:q * P + 97], oT[i][0:97, q * P:(q + 1) * P], ident[0:97, 0:97])
                mm.then_inc(turned[i], 1)

            pe.wait_ge(preset, HU + 2)
            for a in range(NA + 1):
                unit(0, 0, a)
            for a in range(EARLY):
                unit(0, 1, a)
            all_turns(pe, step, end)

        @block.scalar
        def _(act):

            def max_row(j, u):
                if u >= HU:
                    j, u = j + 1, u - HU
                for i in range(2):
                    act.wait_ge(a_full[i], (j * HU + u) * (NA + 1) + (NA + 1))
                    act.copy(qst[u][96:97, i * HALF:(i + 1) * HALF], ps_a[i][0:1, :]).then_inc(a_free[i], 1)

            def step(j, u, s, left):
                n = j * HU + u
                if s == NK:
                    return
                if smp and s == R + 3 and u % 2 == 0:
                    smp.weights(act, j, u // 2)
                act.wait_ge(b_full[s % 2], n * (NK // 2) + (s // 2 + 1))
                if s >= PR or not isinstance(n, int) or n > 0:
                    act.wait_ge(p_used[s % PR], n * (NK // PR) + s // PR)
                act.activation(p[s % PR][:, :], ps_b[s % 2][:, :], ACT.Exp, scale=SCALE).then_inc(exp_done[s % 2], 1)
                if (1, NA) in units[s] and (left is None or left >= 1):
                    max_row(j, u + 1)
                if s == 0 and not (isinstance(n, int) and n == 0):
                    copy_out(*((j, u - 1) if u > 0 else (j - 1, HU - 1)))

            def copy_out(j, u):
                i = u % 2
                act.wait_ge(o_full[i], j * 2 + (u // 2 + 1))
                for r in (0, 64):
                    act.copy(oT[i][r:r + V1, :], ps_o[i][r:r + V1, :]).then_inc(oT_done[i], 1)

            act.wait_ge(preset, HU + 2)
            max_row(0, 0)
            all_turns(act, step, lambda j, u: copy_out(j, u) if isinstance(j, int) and j * HU + u == NH - 1 else None)

        @block.vector
        def _(dve):

            def unit(j, u, a):
                if u >= HU:
                    j, u = j + 1, u - HU
                n = j * HU + u
                if a < NA:
                    for i in range(2):
                        dve.wait_ge(a_full[i], n * (NA + 1) + (a + 1))
                        dve.tensor_reduce(mx[:, a, i:i + 1], ps_a[i][:, :], X, ALU.max).then_inc(a_free[i], 1)
                else:
                    for i in range(2):
                        dve.wait_ge(a_free[i], n * (NA + 1) + NA)
                    dve.tensor_reduce(negm[:, :], mx[:, :, :].rearrange("p (q c) i -> p q (c i)", c=NKC), X, ALU.max,
                                      negate=True).then_inc(negm_done, 1)

            def step(j, u, s, left):
                if smp and s == R + 1 and u % 2 == 0:
                    smp.scores(dve, j, u // 2)
                if smp and s == R + 1 and u % 2 == 1:
                    smp.output(dve, j, u // 2)
                if s < NK:
                    for ahead, a in units[s]:
                        if left is None or ahead <= left:
                            unit(j, u + ahead, a)

            def end(j, u):
                i = u % 2
                acc = ps_o[i][:, :].rearrange("p (n a d) -> p n a d", a=2, d=64)
                dve.wait_ge(turned[i], j * 2 + (u // 2 + 1))
                dve.reciprocal(inv[i][:, :, :, :], acc[:, :, :, HD:V1]).then_inc(inv_done, 1)
                dve.wait_ge(inv_done, j * HU + (u + 1))
                dve.wait_ge(o_out[i], j * 2 + (u // 2 + 1))
                dst = o[i][:, :, :].rearrange("p (a n) d -> p n a d", a=2)
                dve.tensor_tensor(dst, acc[:, :, :, 0:HD], inv[i][:, :, :, :].to_broadcast([P, NQ // 2, 2, HD]),
                                  ALU.mult).then_inc(o_done[i], 1)
                dve.wait_ge(o_done[i], j * 2 + (u // 2 + 1))
                dve.sem_inc(o_free[i], 1)

            for u in range(HU):
                dve.memset(kst[u][96:97, :].bitcast(F32), 1.0).then_inc(preset, 1)
            for i in range(2):
                dve.sem_inc(o_free[i], 1)
                dve.memset(oT[i][:, :], 0.0).then_inc(preset, 1)
            for a in range(NA + 1):
                unit(0, 0, a)
            for a in range(EARLY):
                unit(0, 1, a)
            all_turns(dve, step, end)

        @block.gpsimd
        def _(pool):
            if smp:
                smp.gather(pool)


def top_two(steps, dve, prob, ahead, gt, eq, rank, sel):
    other = prob.unsqueeze(2).to_broadcast([P, TT, E0, E0])
    own = prob.unsqueeze(3).to_broadcast([P, TT, E0, E0])
    steps.did(dve.tensor_tensor(gt, other, own, ALU.is_gt))
    steps.did(dve.tensor_tensor(eq, other, own, ALU.is_equal))
    steps.settle()
    steps.did(dve.tensor_tensor(eq, eq, ahead.unsqueeze(1).to_broadcast([P, TT, E0, E0]), ALU.mult))
    steps.settle()
    steps.did(dve.tensor_tensor(gt, gt, eq, ALU.add))
    steps.settle()
    steps.did(dve.tensor_reduce(rank, gt, X, ALU.add))
    steps.settle()
    steps.did(dve.tensor_scalar(sel, rank, 1.5, None, ALU.is_lt))
    steps.settle()


def ffn_moe(nc, x_dram, attn, woT, bo, wqkv, bqkv, wg, bg, we, be, ident, ahead,
            q_hi, q_lo, k_hi, k_lo, v_ones, x_part, batch, samples=None):
    NG = S // G
    G0 = batch * NG
    with ExitStack() as ctx:
        t = Tools(nc, ctx, f"moe{batch}")
        w_o = t.sb("w_o", [P, C, D])
        w_qkv = t.sb("w_qkv", [P, C, 3 * D])
        w_g = t.sb("w_g", [P, C, E0])
        w_e = t.sb("w_e", [P, E0, C, D])
        b_e = t.sb("b_e", [E0, D])
        qk_c = t.sb("qk_c", [P, 2 * C])
        rows = t.sb("rows", [P, 2, D])
        bg_r = t.sb("bg_r", [P, E0])
        ao = t.sb("ao", [P, TT, D])
        xT = t.sb("xT", [P, C, G])
        acc = t.sb("acc", [P, TT, D])
        ln = ao
        stats, mv, rstd = t.sb("stats", [P, TT, 6]), t.sb("mv", [P, TT, 2]), t.sb("rstd", [P, 4, TT])
        hi, lo = t.sb("hi", [P, C, G], F32R), t.sb("lo", [P, C, G], F32R)
        vo = t.sb("vo", [P, TT, H, V1])
        lg, ex, sel, rank = (t.sb(n, [P, TT, E0]) for n in ("lg", "ex", "sel", "rank"))
        gt, eq = (t.sb(n, [P, TT, E0, E0]) for n in ("gt", "eq"))
        red = t.sb("red", [P, TT, 1])
        comb = t.sb("comb", [P, TT, E0])
        combT = t.sb("combT", [E0, G])
        tb = [t.ps(f"tb{i}", [P, G]) for i in range(4)]
        m = [t.ps(f"m{i}", [P, G]) for i in range(4)]
        w_in, we_in, in_sem, preset = t.sem("w_in"), t.sem("we_in"), t.sem("in"), t.sem("preset")
        t_full, t_out = t.sems("t_full", 4), t.sems("t_out", 4)
        m_full, m_free = t.sems("m_full", 4), t.sems("m_free", 4)
        dsem, hi_done = t.sem("dve_steps"), t.sem("hi_done")
        ln_done, lg_done, ex_done, comb_done, combT_done = (
            t.sem(n) for n in ("ln_done", "lg_done", "ex_done", "comb_done", "combT_done"))
        q_done, kv_done, out_done, turned = t.sem("q_done"), t.sem("kv_done"), t.sem("out_done"), t.sem("turned")
        q_out, kv_out, x_out = t.sem("q_out"), t.sem("kv_out"), t.sem("x_out")
        hilo_free, v_free, x_in, xT_free = (t.sem(n) for n in ("hilo_free", "v_free", "x_in", "xT_free"))
        TU = [3, 3, 2, 2]
        MU = 4 + 1 + E0
        SAMPLE_AT = (1, 4, 7)
        passed = t.sems("passed", 4)
        smp = Samples(t, *samples) if samples else None
        block = t.block()

        @block.sync
        def _(sp):
            sp.dma_start(w_o[:, :, :], woT.rearrange("(c p) n -> p c n", p=P)).then_inc(w_in, 16)
            sp.dma_start(w_qkv[:, :, :], wqkv.rearrange("(c p) n -> p c n", p=P)).then_inc(w_in, 16)
            sp.dma_start(w_g[:, :, :], wg.rearrange("(c p) n -> p c n", p=P)).then_inc(w_in, 16)
            sp.dma_start(b_e[:, :], be).then_inc(w_in, 16)
            sp.dma_start(qk_c[:, :], bqkv[0:2 * D].rearrange("(c p) -> p c", p=P), allow_slow_non_contiguous=True).then_inc(w_in, 16)
            sp.dma_start(rows[:, 0, :], row_of(bo, D)).then_inc(w_in, 16)
            sp.dma_start(rows[:, 1, :], row_of(bqkv[2 * D:3 * D], D)).then_inc(w_in, 16)
            sp.dma_start(bg_r[:, :], row_of(bg, E0)).then_inc(w_in, 16)
            xs = x_dram.rearrange("(n p) d -> p n d", p=P)
            as_ = attn.rearrange("(n p) d -> p n d", p=P)
            vd = v_ones.rearrange("(n p) f -> p n f", p=P)
            xd = x_part.rearrange("(n p) d -> p n d", p=P)

            def load(g):
                n = (G0 + g) * TT
                sp.dma_start(ao[:, :, :], as_[:, n:n + TT, :]).then_inc(in_sem, 16)

            def load_x(g):
                n = (G0 + g) * TT
                sp.dma_start(acc[:, :, :], xs[:, n:n + TT, :]).then_inc(x_in, 16)

            def store(src, dst, g, done):
                sp.dma_start(dst.rearrange("(g c p) t -> g p c t", c=C, p=P)[G0 + g, :, :, :].bitcast(F32),
                             src[:, :, :].bitcast(F32)).then_inc(done, 16)

            for free in (hilo_free, v_free, xT_free):
                sp.sem_inc(free, 1)
            load(0)
            load_x(0)
            for e in range(E0):
                sp.dma_start(w_e[:, e, :, :], we[e].rearrange("(c p) n -> p c n", p=P)).then_inc(we_in, 16)
            for g in range(NG):
                n = (G0 + g) * TT
                sp.wait_ge(q_done, g + 1)
                store(hi, q_hi, g, q_out)
                store(lo, q_lo, g, q_out)
                sp.wait_ge(q_out, 32 * (g + 1))
                sp.sem_inc(hilo_free, 1)
                if g + 1 < NG:
                    sp.wait_ge(turned, g + 1)
                    load(g + 1)
                sp.wait_ge(kv_done, g + 1)
                store(hi, k_hi, g, kv_out)
                store(lo, k_lo, g, kv_out)
                sp.dma_start(vd[:, n:n + TT, :], vo[:, :, :, :].rearrange("p n h d -> p n (h d)")).then_inc(kv_out, 16)
                sp.wait_ge(kv_out, 48 * (g + 1))
                sp.sem_inc(hilo_free, 1)
                sp.sem_inc(v_free, 1)
                sp.wait_ge(out_done, g + 1)
                sp.dma_start(xd[:, n:n + TT, :], acc[:, :, :]).then_inc(x_out, 16)
                sp.wait_ge(x_out, 16 * (g + 1))
                if g + 1 < NG:
                    load_x(g + 1)

        @block.tensor
        def _(pe):
            for k in range(4):
                pe.sem_inc(m_free[k], 1)
                pe.sem_inc(t_out[k], 1)
            pe.wait_ge(w_in, 16 * 8)
            with pe.Fori(0, NG) as g:

                def turn(src, use):
                    for c in range(C):
                        pe.wait_ge(t_out[c], g * TU[c] + (use + 1))
                        for n in range(TT):
                            mm = pe.transpose(tb[c][:, n * P:(n + 1) * P], src[:, n, c * P:(c + 1) * P], ident[:, :])
                        mm.then_inc(t_full[c], 1)
                    for c in range(C):
                        pe.wait_ge(t_out[c], g * TU[c] + (use + 2))

                def tile(row, o, left, right):
                    pe.wait_ge(m_free[o], g * MU + (row + 1))
                    for c in range(C):
                        mm = pe.matmul(m[o][:, :], left(c), right(c), start=(c == 0), stop=(c == C - 1))
                    mm.then_inc(m_full[o], 1)

                pe.wait_ge(in_sem, 16 * g + 16)
                turn(ao, 0)
                for o in range(4):
                    tile(0, o, lambda c: xT[:, c, o * P:(o + 1) * P], lambda c: w_o[:, c, :])
                pe.wait_ge(ln_done, g + 1)
                turn(ln, 1)
                pe.sem_inc(turned, 1)
                pe.wait_ge(t_out[0], g * TU[0] + 3)
                for n in range(TT):
                    for c in range(C):
                        mm = pe.matmul(tb[0][:, n * E0:(n + 1) * E0], xT[:, c, n * P:(n + 1) * P], w_g[:, c, :],
                                       start=(c == 0), stop=(c == C - 1))
                mm.then_inc(t_full[0], 1)
                for r in range(2):
                    for o in range(4):
                        k = (4 * r + o) * P
                        tile(1 + r, o, lambda c: w_qkv[:, c, k:k + P], lambda c: xT[:, c, :])
                for o in range(4):
                    tile(3, o, lambda c: xT[:, c, o * P:(o + 1) * P], lambda c: w_qkv[:, c, 2 * D:3 * D])
                pe.wait_ge(comb_done, g + 1)
                pe.wait_ge(t_out[1], g * TU[1] + 3)
                for n in range(TT):
                    mm = pe.transpose(tb[1][0:E0, n * P:(n + 1) * P], comb[:, n, :], ident[:, :])
                mm.then_inc(t_full[1], 1)
                pe.wait_ge(combT_done, g + 1)
                for o in range(4):
                    pe.wait_ge(m_free[o], g * MU + 5)
                    pe.matmul(m[o][:, :], combT[:, o * P:(o + 1) * P], b_e[:, :],
                              start=True, stop=True).then_inc(m_full[o], 1)
                pe.wait_ge(we_in, 16 * E0)
                for e in range(E0):
                    for o in range(4):
                        tile(5 + e, o, lambda c: xT[:, c, o * P:(o + 1) * P], lambda c: w_e[:, e, c, :])

        @block.scalar
        def _(act):
            act.wait_ge(w_in, 16 * 8)
            with act.Fori(0, NG) as g:
                act.wait_ge(xT_free, g + 1)
                for use in range(2):
                    if use == 1:
                        act.wait_ge(m_full[3], g * MU + 1)
                    for c in range(C):
                        act.wait_ge(t_full[c], g * TU[c] + (use + 1))
                        act.copy(xT[:, c, :], tb[c][:, :]).then_inc(t_out[c], 1)
                act.wait_ge(lg_done, g + 1)
                act.activation(ex[:, :, :], lg[:, :, :], ACT.Exp).then_inc(ex_done, 1)
                for k in range(2 * C):
                    if k % C == 0:
                        act.wait_ge(hilo_free, 2 * g + (k // C + 1))
                    act.wait_ge(m_full[k % 4], g * MU + (k // 4 + 2))
                    act.activation(hi[:, k % C, :], m[k % 4][:, :], ACT.Identity, bias=qk_c[:, k:k + 1]).then_inc(hi_done, 1)
                act.wait_ge(t_full[1], g * TU[1] + 3)
                act.copy(combT[:, :], tb[1][0:E0, :]).then_inc(combT_done, 1)
                act.wait_ge(combT_done, g + 1)
                act.sem_inc(t_out[1], 1)
                for k in range(4 if smp else 0):
                    smp.weights(act, 2 * g + k // 2, k % 2)

        @block.vector
        def _(dve):
            steps = Steps(dve, dsem, 42)
            dve.memset(vo[:, :, :, HD:V1], 1.0).then_inc(preset, 1)
            dve.wait_ge(preset, 1)
            dve.wait_ge(w_in, 16 * 8)
            with dve.Fori(0, NG) as g:

                def sample(k):
                    if smp:
                        smp.scores(dve, 2 * g + k // 2, k % 2)
                        smp.output(dve, 2 * g + k // 2, k % 2)

                steps.begin(g)
                dve.wait_ge(x_in, 16 * g + 16)
                for n in range(TT):
                    steps.did(dve.tensor_tensor(acc[:, n, :], acc[:, n, :], rows[:, 0, :], ALU.add))
                steps.settle()
                for n in range(TT):
                    dve.wait_ge(m_full[n], g * MU + 1)
                    dve.tensor_tensor(acc[:, n, :], m[n][:, :], acc[:, n, :], ALU.add).then_inc(m_free[n], 1)
                for n in range(TT):
                    dve.wait_ge(m_free[n], g * MU + 2)
                layer_norm(steps, dve, passed[3], acc, ln, stats, mv, rstd)
                dve.sem_inc(ln_done, 1)
                dve.wait_ge(t_full[0], g * TU[0] + 3)
                gate = tb[0][:, 0:TT * E0].rearrange("p (n e) -> p n e", e=E0)
                steps.did(dve.tensor_tensor(lg[:, :, :], gate, bg_r[:, :].unsqueeze(1).to_broadcast([P, TT, E0]), ALU.add))
                steps.settle()
                dve.sem_inc(t_out[0], 1)
                steps.did(dve.tensor_reduce(red[:, :, :], lg[:, :, :], X, ALU.max))
                steps.settle()
                steps.did(dve.tensor_tensor(lg[:, :, :], lg[:, :, :], red[:, :, :].to_broadcast([P, TT, E0]), ALU.subtract))
                steps.settle()
                dve.sem_inc(lg_done, 1)
                dve.wait_ge(ex_done, g + 1)
                steps.did(dve.tensor_reduce(red[:, :, :], ex[:, :, :], X, ALU.add))
                steps.settle()
                steps.did(dve.reciprocal(red[:, :, :], red[:, :, :]))
                steps.settle()
                steps.did(dve.tensor_tensor(ex[:, :, :], ex[:, :, :], red[:, :, :].to_broadcast([P, TT, E0]), ALU.mult))
                steps.settle()
                top_two(steps, dve, ex[:, :, :], ahead[:, :, :], gt[:, :, :, :], eq[:, :, :, :], rank[:, :, :], sel[:, :, :])
                steps.did(dve.tensor_tensor(comb[:, :, :], ex[:, :, :], sel[:, :, :], ALU.mult))
                steps.settle()
                dve.sem_inc(comb_done, 1)
                for k in range(2 * C):
                    dve.wait_ge(m_full[k % 4], g * MU + (k // 4 + 2))
                    dve.wait_ge(hi_done, g * 2 * C + (k + 1))
                    dve.scalar_tensor_tensor(out=lo[:, k % C, :], in0=m[k % 4][:, :], scalar=qk_c[:, k:k + 1],
                                             in1=hi[:, k % C, :].bitcast(F32), op0=ALU.add,
                                             op1=ALU.subtract).then_inc(m_free[k % 4], 1)
                    if k == C - 1:
                        for o in range(4):
                            dve.wait_ge(m_free[o], g * MU + 3)
                        dve.sem_inc(q_done, 1)
                dve.wait_ge(v_free, g + 1)
                for n in range(TT):
                    dve.wait_ge(m_full[n], g * MU + 4)
                    dve.tensor_tensor(vo[:, n, :, 0:HD], m[n][:, :].rearrange("p (h d) -> p h d", h=H),
                                      rows[:, 1, :].rearrange("p (h d) -> p h d", h=H), ALU.add).then_inc(m_free[n], 1)
                for n in range(TT):
                    dve.wait_ge(m_free[n], g * MU + 5)
                dve.sem_inc(kv_done, 1)
                sample(0)
                for n in range(TT):
                    dve.wait_ge(m_full[n], g * MU + 5)
                    dve.tensor_tensor(acc[:, n, :], m[n][:, :], acc[:, n, :], ALU.add).then_inc(m_free[n], 1)
                for e in range(E0):
                    for n in range(TT):
                        dve.wait_ge(m_full[n], g * MU + (6 + e))
                        dve.wait_ge(m_free[n], g * MU + (6 + e))
                        dve.scalar_tensor_tensor(out=acc[:, n, :], in0=m[n][:, :], scalar=comb[:, n, e:e + 1],
                                                 in1=acc[:, n, :], op0=ALU.mult, op1=ALU.add).then_inc(m_free[n], 1)
                    if e in SAMPLE_AT:
                        sample(SAMPLE_AT.index(e) + 1)
                for n in range(TT):
                    dve.wait_ge(m_free[n], g * MU + (MU + 1))
                dve.sem_inc(out_done, 1)
                dve.sem_inc(xT_free, 1)
                steps.end()

        @block.gpsimd
        def _(pool):
            if smp:
                smp.gather(pool)


def sample_positions(nc, x_part, attn, mask, wqT, bq, woffT, boff, ident, x2, qp_dram, idx_dram, wt_dram, batch):
    F = TT * NS
    NG = S // G
    G0 = batch * NG
    with ExitStack() as ctx:
        t = Tools(nc, ctx, f"pos{batch}")
        w_q, w_off = t.sb("w_q", [P, C, D]), t.sb("w_off", [P, C, NS])
        bq_r, boff_r = t.sb("bq_r", [P, D]), t.sb("boff_r", [P, NS])
        mk = t.sb("mk", [P, T], I32)
        mkf = t.sb("mkf", [P, T])
        length, neg_length, inv_length = (t.sb(n, [P, 1]) for n in ("length", "neg_length", "inv_length"))
        pos_i, head_i = t.sb("pos_i", [P, 2, F], I32), t.sb("head_i", [P, F], I32)
        pos, head = t.sb("pos", [P, 2, F]), t.sb("head", [P, F])
        xa, xb = t.sb("xa", [P, TT, D]), t.sb("xb", [P, TT, D])
        ln, xT, qp = t.sb("ln", [P, TT, D]), t.sb("xT", [P, C, G]), t.sb("qp", [P, TT, D])
        stats, mv, rstd = t.sb("stats", [P, TT, 6]), t.sb("mv", [P, TT, 2]), t.sb("rstd", [P, 4, TT])
        at, whole, frac, flag = (t.sb(n, [P, F]) for n in ("at", "whole", "frac", "flag"))
        whole_i = t.sb("whole_i", [P, F], I32)
        wt = t.sb("wt", [P, F, 2])
        idx = t.sb("idx", [P, F], I32)
        tb = [t.ps(f"tb{i}", [P, G]) for i in range(4)]
        m = [t.ps(f"m{i}", [P, G]) for i in range(4)]
        w_in, in_sem, made = t.sem("w_in"), t.sem("in"), t.sem("made")
        mask_in, dsem, bsem = t.sem("mask_in"), t.sem("dve_steps"), t.sem("batch_steps")
        t_full, t_out = t.sems("t_full", 4), t.sems("t_out", 4)
        m_full, m_free = t.sems("m_full", 4), t.sems("m_free", 4)
        ln_done, qp_done, x2_done, idx_done, xT_free, stored = (
            t.sem(n) for n in ("ln_done", "qp_done", "x2_done", "idx_done", "xT_free", "stored"))
        TU = [3, 2, 2, 2]
        NST = 4
        passed = t.sems("passed", 4)
        block = t.block()

        @block.sync
        def _(sp):
            sp.dma_start(w_q[:, :, :], wqT.rearrange("(c p) n -> p c n", p=P)).then_inc(w_in, 16)
            sp.dma_start(w_off[:, :, :], woffT.rearrange("(c p) n -> p c n", p=P)).then_inc(w_in, 16)
            sp.dma_start(bq_r[:, :], row_of(bq, D)).then_inc(w_in, 16)
            sp.dma_start(boff_r[:, :], row_of(boff, NS)).then_inc(w_in, 16)
            xs = x_part.rearrange("(n p) d -> p n d", p=P)
            as_ = attn.rearrange("(n p) d -> p n d", p=P)
            sp.dma_start(mk[:, :], mask[batch:batch + 1, :].partition_broadcast(P).rearrange("p a t -> p (a t)")).then_inc(mask_in, 16)
            for g in range(NG):
                if g > 0:
                    sp.wait_ge(stored, 16 * NST * g)
                n = (G0 + g) * TT
                sp.dma_start(xa[:, :, :], xs[:, n:n + TT, :]).then_inc(in_sem, 16)
                sp.dma_start(xb[:, :, :], as_[:, n:n + TT, :]).then_inc(in_sem, 16)

        @block.gpsimd
        def _(pool):
            for u in range(2):
                pool.iota(pos_i[:, u, :], [[P, TT], [0, H], [1, NK5]], base=u * G + (-NK5 // 2),
                          channel_multiplier=1).then_inc(made, 1)
            pool.iota(head_i[:, :], [[0, TT], [1, H], [0, NK5]], base=0, channel_multiplier=0).then_inc(made, 1)
            xd = x2.rearrange("(n p) d -> p n d", p=P)
            qd = qp_dram.rearrange("(n p) d -> p n d", p=P)
            idd = idx_dram.rearrange("(n p) d -> p n d", p=P)
            wd = wt_dram.rearrange("(n p) d -> p n d", p=P)
            with pool.Fori(0, NG) as g:
                pool.wait_ge(x2_done, g + 1)
                pool.sem_inc(passed[1], 1)
                pool.dma_start(xd[:, bass.ds((g + G0) * TT, TT), :], xa[:, :, :]).then_inc(stored, 16)
                pool.wait_ge(qp_done, g + 1)
                pool.sem_inc(passed[1], 1)
                pool.dma_start(qd[:, bass.ds((g + G0) * TT, TT), :], qp[:, :, :]).then_inc(stored, 16)
                pool.wait_ge(idx_done, g + 1)
                pool.sem_inc(passed[1], 1)
                pool.dma_start(idd[:, bass.ds((g + G0) * TT, TT), :], idx[:, :].rearrange("p (n s) -> p n s", n=TT)).then_inc(stored, 16)
                pool.dma_start(wd[:, bass.ds((g + G0) * TT, TT), :], wt[:, :, :].rearrange("p (n s) a -> p n (s a)", n=TT)).then_inc(stored, 16)
            pool.wait_ge(stored, 16 * NST * NG)

        @block.tensor
        def _(pe):
            for k in range(4):
                pe.sem_inc(m_free[k], 1)
                pe.sem_inc(t_out[k], 1)
            pe.wait_ge(w_in, 64)
            with pe.Fori(0, NG) as g:

                def turn(src, use):
                    for c in range(C):
                        pe.wait_ge(t_out[c], g * TU[c] + (use + 1))
                        for n in range(TT):
                            mm = pe.transpose(tb[c][:, n * P:(n + 1) * P], src[:, n, c * P:(c + 1) * P], ident[:, :])
                        mm.then_inc(t_full[c], 1)
                    for c in range(C):
                        pe.wait_ge(t_out[c], g * TU[c] + (use + 2))

                pe.wait_ge(ln_done, g + 1)
                turn(ln, 0)
                for n in range(TT):
                    pe.wait_ge(m_free[n], g + 1)
                    for c in range(C):
                        mm = pe.matmul(m[n][:, :], xT[:, c, n * P:(n + 1) * P], w_q[:, c, :], start=(c == 0), stop=(c == C - 1))
                    mm.then_inc(m_full[n], 1)
                pe.wait_ge(qp_done, g + 1)
                turn(qp, 1)
                for n in range(TT):
                    for c in range(C):
                        mm = pe.matmul(tb[0][:, n * NS:(n + 1) * NS], xT[:, c, n * P:(n + 1) * P], w_off[:, c, :],
                                       start=(c == 0), stop=(c == C - 1))
                mm.then_inc(t_full[0], 1)

        @block.scalar
        def _(act):
            act.sem_inc(xT_free, 1)
            with act.Fori(0, NG) as g:
                act.wait_ge(xT_free, g + 1)
                for use in range(2):
                    if use == 1:
                        act.wait_ge(m_full[3], g + 1)
                    for c in range(C):
                        act.wait_ge(t_full[c], g * TU[c] + (use + 1))
                        act.copy(xT[:, c, :], tb[c][:, :]).then_inc(t_out[c], 1)

        @block.vector
        def _(dve):
            per_batch = Steps(dve, bsem, 5)
            steps = Steps(dve, dsem, 54)
            dve.wait_ge(w_in, 64)
            dve.wait_ge(made, 3)
            dve.tensor_copy(pos[:, :, :], pos_i[:, :, :]).then_inc(made, 1)
            dve.tensor_scalar(head[:, :], head_i[:, :], float(ROWS * PAIR), float(2 * PAIR), ALU.mult,
                              ALU.add).then_inc(made, 1)
            dve.wait_ge(made, 5)
            per_batch.begin(0)
            dve.wait_ge(mask_in, 16)
            per_batch.did(dve.tensor_copy(mkf[:, :], mk[:, :]))
            per_batch.settle()
            per_batch.did(dve.tensor_reduce(length[:, :], mkf[:, :], X, ALU.add))
            per_batch.settle()
            per_batch.did(dve.tensor_scalar(neg_length[:, :], length[:, :], float(T - 1), None, ALU.subtract))
            per_batch.settle()
            per_batch.did(dve.tensor_scalar(length[:, :], neg_length[:, :], -1.0, None, ALU.mult))
            per_batch.settle()
            per_batch.did(dve.reciprocal(inv_length[:, :], length[:, :]))
            per_batch.settle()
            per_batch.end()
            for g in range(NG):
                steps.begin(g)
                go = lambda ins: (steps.did(ins), steps.settle())
                dve.wait_ge(in_sem, 32 * g + 32)
                for n in range(TT):
                    steps.did(dve.tensor_tensor(xa[:, n, :], xa[:, n, :], xb[:, n, :], ALU.add))
                steps.settle()
                dve.sem_inc(x2_done, 1)
                layer_norm(steps, dve, passed[3], xa, ln, stats, mv, rstd)
                dve.sem_inc(ln_done, 1)
                if g > 0:
                    dve.wait_ge(stored, 16 * NST * g)
                for n in range(TT):
                    dve.wait_ge(m_full[n], g + 1)
                    dve.tensor_tensor(qp[:, n, :], m[n][:, :], bq_r[:, :], ALU.add).then_inc(m_free[n], 1)
                for n in range(TT):
                    dve.wait_ge(m_free[n], g + 2)
                dve.sem_inc(qp_done, 1)
                dve.wait_ge(t_full[0], g * TU[0] + 3)
                go(dve.tensor_tensor(at[:, :].rearrange("p (n s) -> p n s", n=TT),
                                     tb[0][:, 0:F].rearrange("p (n s) -> p n s", n=TT),
                                     boff_r[:, :].unsqueeze(1).to_broadcast([P, TT, NS]), ALU.add))
                dve.sem_inc(t_out[0], 1)
                dve.sem_inc(xT_free, 1)
                go(dve.tensor_tensor(at[:, :], at[:, :], pos[:, g, :], ALU.add))

                def floor(src, dst):
                    go(dve.tensor_copy(whole_i[:, :], src))
                    go(dve.tensor_copy(dst, whole_i[:, :]))
                    go(dve.tensor_tensor(flag[:, :], dst, src, ALU.is_gt))
                    go(dve.tensor_tensor(dst, dst, flag[:, :], ALU.subtract))

                go(dve.tensor_scalar(frac[:, :], at[:, :], inv_length[:, 0:1], None, ALU.mult))
                floor(frac[:, :], whole[:, :])
                go(dve.scalar_tensor_tensor(out=at[:, :], in0=whole[:, :], scalar=neg_length[:, 0:1], in1=at[:, :],
                                            op0=ALU.mult, op1=ALU.add))
                go(dve.tensor_scalar(flag[:, :], at[:, :], inv_length[:, 0:1], 1.0, ALU.mult, ALU.is_ge))
                go(dve.scalar_tensor_tensor(out=at[:, :], in0=flag[:, :], scalar=neg_length[:, 0:1], in1=at[:, :],
                                            op0=ALU.mult, op1=ALU.add))
                go(dve.tensor_scalar(flag[:, :], at[:, :], inv_length[:, 0:1], 0.0, ALU.mult, ALU.is_lt))
                go(dve.scalar_tensor_tensor(out=at[:, :], in0=flag[:, :], scalar=length[:, 0:1], in1=at[:, :],
                                            op0=ALU.mult, op1=ALU.add))
                go(dve.tensor_scalar(at[:, :], at[:, :], 1.0 / (T - 1), 2.0, ALU.mult, ALU.mult))
                go(dve.tensor_scalar(at[:, :], at[:, :], -1.0, 1.0, ALU.add, ALU.add))
                go(dve.tensor_scalar(at[:, :], at[:, :], float(T), -1.0, ALU.mult, ALU.add))
                go(dve.tensor_scalar(at[:, :], at[:, :], 0.5, None, ALU.mult))
                floor(at[:, :], whole[:, :])
                go(dve.tensor_tensor(frac[:, :], at[:, :], whole[:, :], ALU.subtract))
                steps.did(dve.tensor_scalar(wt[:, :, 0], frac[:, :], -0.5, 0.5, ALU.mult, ALU.add))
                steps.did(dve.tensor_scalar(wt[:, :, 1], frac[:, :], 0.5, None, ALU.mult))
                go(dve.tensor_scalar(whole[:, :], whole[:, :], -2.0, float(T), ALU.max, ALU.min))
                go(dve.scalar_tensor_tensor(out=idx[:, :], in0=whole[:, :], scalar=float(PAIR), in1=head[:, :],
                                            op0=ALU.mult, op1=ALU.add))
                dve.sem_inc(idx_done, 1)
                steps.end()


def ffn_last(nc, x2, cx, woT, bo, w_enc, b_enc, w_s2c, b_s2c, wr, br, w1, b1, w2, b2, w_c2s, b_c2s,
             w_dec, b_dec, ln_g, ln_b, ident, ahead, out, samples):
    NG = B * S // G
    TILES = [3, 3, 2, 0]
    HC = HID // P
    with ExitStack() as ctx:
        t = Tools(nc, ctx, "out")
        wo_s, we_s = t.sb("wo", [P, C, D]), t.sb("we", [P, C, HID])
        ws_s, wr_s = t.sb("ws", [P, HC, MM]), t.sb("wr", [MM, E1])
        w1_s, w2_s = t.sb("w1", [MM, E1, EH]), t.sb("w2", [P, E1, EH // P, MM])
        wc_s, wd_s = t.sb("wc", [MM, HID]), t.sb("wd", [P, HC, D])
        be_c, bs_c, b1_c, bc_c = t.sb("be", [P, HC]), t.sb("bs", [MM, 1]), t.sb("b1", [P, E1, EH // P]), t.sb("bc", [P, HC])
        rows = t.sb("rows", [P, 5, D])
        br_r = t.sb("br_r", [P, E1])
        ca, acc, ln = t.sb("ca", [P, TT, D]), t.sb("acc", [P, TT, D]), t.sb("ln", [P, TT, D])
        xT, hT = t.sb("xT", [P, C, G]), t.sb("hT", [P, HC, G])
        contT, eoT = t.sb("contT", [MM, G]), t.sb("eoT", [MM, G])
        he = [t.sb(f"he{i}", [P, EH // P, G]) for i in range(2)]
        y = ln[:, :, :].rearrange("p n (e d) -> p n e d", e=E1)
        eo = t.sb("eo", [P, TT, MM])
        stats, mv, rstd = t.sb("stats", [P, TT, 6]), t.sb("mv", [P, TT, 2]), t.sb("rstd", [P, 4, TT])
        lg, ex, sel, rank = (t.sb(n, [P, TT, E1]) for n in ("lg", "ex", "sel", "rank"))
        gt, eq = (t.sb(n, [P, TT, E1, E1]) for n in ("gt", "eq"))
        red = t.sb("red", [P, TT, 1])
        tb = [t.ps(f"tb{i}", [P, G]) for i in range(4)]
        m = [t.ps(f"m{i}", [P, G]) for i in range(4)]
        w_in, in_sem = t.sem("w_in"), t.sem("in")
        t_full, t_out = t.sems("t_full", 4), t.sems("t_out", 4)
        m_full, m_free = t.sems("m_full", 4), t.sems("m_free", 4)
        dsem, ln_done, lg_done, ex_done, eo_done, out_done, stored, he_used, xT_free = (
            t.sem(n) for n in ("dve_steps", "ln_done", "lg_done", "ex_done", "eo_done", "out_done", "stored", "he_used", "xT_free"))
        TU = [4, 4, 4, 3]
        MU = 1 + 2 + E1 + 2 + 1
        NW = 19
        passed = t.sems("passed", 4)
        smp = Samples(t, *samples)
        block = t.block()

        @block.sync
        def _(sp):
            loads = [(wo_s[:, :, :], woT.rearrange("(c p) n -> p c n", p=P)),
                     (we_s[:, :, :], w_enc.rearrange("(c p) n -> p c n", p=P)),
                     (ws_s[:, :, :], w_s2c.rearrange("(c p) n -> p c n", p=P)), (wr_s[:, :], wr),
                     (w1_s[:, :, :], w1.rearrange("e m h -> m e h")),
                     (w2_s[:, :, :, :], w2.rearrange("e (k p) m -> p e k m", p=P)), (wc_s[:, :], w_c2s),
                     (wd_s[:, :, :], w_dec.rearrange("(c p) n -> p c n", p=P)),
                     (be_c[:, :], b_enc.rearrange("(c p) -> p c", p=P)), (bs_c[:, :], b_s2c.rearrange("(m a) -> m a", a=1)),
                     (b1_c[:, :, :], b1.rearrange("e (k p) -> p e k", p=P)), (bc_c[:, :], b_c2s.rearrange("(c p) -> p c", p=P)),
                     (rows[:, 0, :], row_of(bo, D)), (rows[:, 1, :], row_of(b_dec, D)), (rows[:, 2, :], row_of(ln_g, D)),
                     (rows[:, 3, :], row_of(ln_b, D)), (rows[:, 4, :], row_of(b2, D)), (br_r[:, :], row_of(br, E1))]
            assert len(loads) == NW - 1
            for dst, src in loads:
                sp.dma_start(dst, src, allow_slow_non_contiguous=True).then_inc(w_in, 16)
            xs = x2.rearrange("(n p) d -> p n d", p=P)
            cs = cx.rearrange("(n p) d -> p n d", p=P)
            od = out.rearrange("(n p) d -> p n d", p=P)
            for g in range(NG):
                if g > 0:
                    sp.wait_ge(stored, 16 * g)
                sp.dma_start(acc[:, :, :], xs[:, g * TT:(g + 1) * TT, :]).then_inc(in_sem, 16)
                if g >= NG // B:
                    for u in range(2):
                        sp.wait_ge(smp.stored[u], 16 * TT * (g - NG // B + 1))
                sp.dma_start(ca[:, :, :], cs[:, g * TT:(g + 1) * TT, :]).then_inc(in_sem, 16)
                sp.wait_ge(out_done, g + 1)
                sp.dma_start(od[:, g * TT:(g + 1) * TT, :], acc[:, :, :]).then_inc(stored, 16)
            sp.wait_ge(stored, 16 * NG)

        @block.tensor
        def _(pe):
            for k in range(4):
                pe.sem_inc(m_free[k], 1)
                pe.sem_inc(t_out[k], 1)
            pe.wait_ge(w_in, 16 * (NW - 1))
            with pe.Fori(0, NG) as g:

                def turn(src, use):
                    for c in range(C):
                        pe.wait_ge(t_out[c], g * TU[c] + (use + 1))
                        for n in range(TT):
                            mm = pe.transpose(tb[c][:, n * P:(n + 1) * P], src[:, n, c * P:(c + 1) * P], ident[:, :])
                        mm.then_inc(t_full[c], 1)
                    for c in range(C):
                        pe.wait_ge(t_out[c], g * TU[c] + (use + 2))

                def tile(row, o, n, left, right):
                    pe.wait_ge(m_free[o], g * MU + (row + 1))
                    for c in range(n):
                        mm = pe.matmul(m[o][:, :], left(c), right(c), start=(c == 0), stop=(c == n - 1))
                    mm.then_inc(m_full[o], 1)

                def y_of(e):
                    for k in range(4):
                        pe.wait_ge(m_free[k], g * MU + (3 + e + 2))
                    for n in range(TT):
                        if e == 0:
                            pe.wait_ge(t_out[n], g * TU[n] + [4, 4, 3, 3][n])
                        for k in range(EH // P):
                            mm = pe.matmul(tb[n][:, e * MM:(e + 1) * MM], he[e % 2][:, k, n * P:(n + 1) * P],
                                           w2_s[:, e, k, :], start=(k == 0), stop=(k == EH // P - 1))
                        if e == E1 - 1:
                            mm.then_inc(t_full[n], 1)
                    if e < E1 - 1:
                        mm.then_inc(he_used, 1)

                pe.wait_ge(in_sem, 32 * g + 32)
                turn(ca, 0)
                for o in range(4):
                    tile(0, o, C, lambda c: xT[:, c, o * P:(o + 1) * P], lambda c: wo_s[:, c, :])
                pe.wait_ge(ln_done, 2 * g + 1)
                turn(ln, 1)
                for r in range(2):
                    for o in range(4):
                        k = (4 * r + o) * P
                        tile(1 + r, o, C, lambda c: we_s[:, c, k:k + P], lambda c: xT[:, c, :])
                for o in range(4):
                    pe.wait_ge(m_free[o], g * MU + 4)
                for k in range(HC):
                    mm = pe.matmul(tb[1][0:MM, :], ws_s[:, k, :], hT[:, k, :], start=(k == 0), stop=(k == HC - 1))
                mm.then_inc(t_full[1], 1)
                pe.wait_ge(t_out[1], g * TU[1] + 4)
                for n in range(TT):
                    mm = pe.matmul(tb[0][:, n * E1:(n + 1) * E1], contT[:, n * P:(n + 1) * P], wr_s[:, :], start=True, stop=True)
                mm.then_inc(t_full[0], 1)
                for e in range(E1):
                    for o in range(4):
                        tile(3 + e, o, 1, lambda c: w1_s[:, e, o * P:(o + 1) * P], lambda c: contT[:, :])
                    if e > 0:
                        y_of(e - 1)
                y_of(E1 - 1)
                pe.wait_ge(eo_done, g + 1)
                pe.wait_ge(t_out[2], g * TU[2] + 4)
                pe.sem_inc(passed[2], 1)
                for n in range(TT):
                    mm = pe.transpose(tb[2][0:MM, n * P:(n + 1) * P], eo[:, n, :], ident[:, :])
                mm.then_inc(t_full[2], 1)
                pe.wait_ge(t_out[2], g * TU[2] + 5)
                for r in range(2):
                    for o in range(4):
                        k = (4 * r + o) * P
                        tile(3 + E1 + r, o, 1, lambda c: wc_s[:, k:k + P], lambda c: eoT[:, :])
                for o in range(4):
                    pe.wait_ge(m_free[o], g * MU + (6 + E1))
                for o in range(4):
                    tile(5 + E1, o, HC, lambda c: hT[:, c, o * P:(o + 1) * P], lambda c: wd_s[:, c, :])

        @block.scalar
        def _(act):
            act.wait_ge(w_in, 16 * (NW - 1))
            act.sem_inc(xT_free, 1)

            def group(g, before, tiles):

                def sample(k):
                    if k < 2 * tiles:
                        smp.weights(act, before + k // 2, k % 2)

                def evac(row, o, dst, func, bias):
                    act.wait_ge(m_full[o], g * MU + (row + 1))
                    act.activation(dst, m[o][:, :], func, bias=bias).then_inc(m_free[o], 1)

                act.wait_ge(xT_free, g + 1)
                for use in range(2):
                    if use == 1:
                        act.wait_ge(m_full[3], g * MU + 1)
                    for c in range(C):
                        act.wait_ge(t_full[c], g * TU[c] + (use + 1))
                        act.copy(xT[:, c, :], tb[c][:, :]).then_inc(t_out[c], 1)
                for r in range(2):
                    for o in range(4):
                        k = 4 * r + o
                        evac(1 + r, o, hT[:, k, :], ACT.Sigmoid, be_c[:, k:k + 1])
                    sample(r)
                act.wait_ge(t_full[1], g * TU[1] + 3)
                act.activation(contT[:, :], tb[1][0:MM, :], ACT.Identity, bias=bs_c[:, 0:1]).then_inc(t_out[1], 1)
                for e in range(E1):
                    if e >= 2:
                        act.wait_ge(he_used, g * (E1 - 1) + (e - 1))
                    for o in range(4):
                        evac(3 + e, o, he[e % 2][:, o, :], ACT.Relu, b1_c[:, e, o:o + 1])
                    if e == 0:
                        act.wait_ge(lg_done, g + 1)
                        act.activation(ex[:, :, :], lg[:, :, :], ACT.Exp).then_inc(ex_done, 1)
                    if e == 3:
                        sample(2)
                    if e == 6:
                        sample(3)
                act.wait_ge(t_full[2], g * TU[2] + 4)
                act.copy(eoT[:, :], tb[2][0:MM, :]).then_inc(t_out[2], 1)
                for r in range(2):
                    for o in range(4):
                        k = 4 * r + o
                        evac(3 + E1 + r, o, hT[:, k, :], ACT.Sigmoid, bc_c[:, k:k + 1])
                sample(4)
                sample(5)

            with act.Fori(0, 2) as g:
                group(g, TILES[0] * g, TILES[0])
            for g in range(2, NG):
                group(g, sum(TILES[:g]), TILES[g])

        @block.vector
        def _(dve):
            steps = Steps(dve, dsem, 90)
            dve.wait_ge(w_in, 16 * (NW - 1))

            def group(g, before, tiles):
                def sample(k):
                    if k < 2 * tiles:
                        smp.scores(dve, before + k // 2, k % 2)
                        smp.output(dve, before + k // 2, k % 2)

                steps.begin(g)
                go = lambda ins: (steps.did(ins), steps.settle())
                dve.wait_ge(in_sem, 32 * g + 32)
                for n in range(TT):
                    steps.did(dve.tensor_tensor(acc[:, n, :], acc[:, n, :], rows[:, 0, :], ALU.add))
                steps.settle()
                for n in range(TT):
                    dve.wait_ge(m_full[n], g * MU + 1)
                    dve.tensor_tensor(acc[:, n, :], m[n][:, :], acc[:, n, :], ALU.add).then_inc(m_free[n], 1)
                for n in range(TT):
                    dve.wait_ge(m_free[n], g * MU + 2)
                layer_norm(steps, dve, passed[3], acc, ln, stats, mv, rstd)
                dve.sem_inc(ln_done, 1)
                sample(0)
                sample(1)
                dve.wait_ge(t_full[0], g * TU[0] + 3)
                logits = tb[0][:, 0:TT * E1].rearrange("p (n e) -> p n e", e=E1)
                go(dve.tensor_tensor(lg[:, :, :], logits, br_r[:, :].unsqueeze(1).to_broadcast([P, TT, E1]), ALU.add))
                dve.sem_inc(t_out[0], 1)
                go(dve.tensor_reduce(red[:, :, :], lg[:, :, :], X, ALU.max))
                go(dve.tensor_tensor(lg[:, :, :], lg[:, :, :], red[:, :, :].to_broadcast([P, TT, E1]), ALU.subtract))
                dve.sem_inc(lg_done, 1)
                dve.wait_ge(ex_done, g + 1)
                go(dve.tensor_reduce(red[:, :, :], ex[:, :, :], X, ALU.add))
                go(dve.reciprocal(red[:, :, :], red[:, :, :]))
                go(dve.tensor_tensor(ex[:, :, :], ex[:, :, :], red[:, :, :].to_broadcast([P, TT, E1]), ALU.mult))
                top_two(steps, dve, ex[:, :, :], ahead[:, :, :], gt[:, :, :, :], eq[:, :, :, :], rank[:, :, :], sel[:, :, :])
                go(dve.tensor_tensor(ex[:, :, :], ex[:, :, :], sel[:, :, :], ALU.mult))
                go(dve.tensor_reduce(red[:, :, :], ex[:, :, :], X, ALU.add))
                go(dve.reciprocal(red[:, :, :], red[:, :, :]))
                go(dve.tensor_tensor(ex[:, :, :], ex[:, :, :], red[:, :, :].to_broadcast([P, TT, E1]), ALU.mult))
                sample(2)
                sample(3)
                for n in range(TT):
                    dve.wait_ge(t_full[n], g * TU[n] + [4, 4, 3, 3][n])
                    dve.tensor_tensor(y[:, n, :, :].rearrange("p e d -> p (e d)"), tb[n][:, :], rows[:, 4, :],
                                      ALU.add).then_inc(t_out[n], 1)
                for n in range(TT):
                    dve.wait_ge(t_out[n], g * TU[n] + [5, 5, 4, 4][n])
                    steps.did(dve.tensor_tensor(y[:, n, :, :], y[:, n, :, :],
                                                ex[:, n, :].unsqueeze(2).to_broadcast([P, E1, MM]), ALU.mult))
                steps.settle()
                for n in range(TT):
                    steps.did(dve.tensor_reduce(eo[:, n, :], y[:, n, :, :].rearrange("p e d -> p d e"), X, ALU.add))
                steps.settle()
                dve.sem_inc(eo_done, 1)
                sample(4)
                for n in range(TT):
                    dve.wait_ge(m_full[n], g * MU + MU)
                    dve.tensor_tensor(ln[:, n, :], m[n][:, :], rows[:, 1, :], ALU.add).then_inc(m_free[n], 1)
                for n in range(TT):
                    dve.wait_ge(m_free[n], g * MU + (MU + 1))
                dve.sem_inc(xT_free, 1)
                layer_norm(steps, dve, passed[3], ln, ca, stats, mv, rstd)
                dve.sem_inc(ln_done, 1)
                for n in range(TT):
                    steps.did(dve.tensor_tensor(ca[:, n, :], ca[:, n, :], rows[:, 2, :], ALU.mult))
                steps.settle()
                for n in range(TT):
                    steps.did(dve.tensor_tensor(ca[:, n, :], ca[:, n, :], rows[:, 3, :], ALU.add))
                steps.settle()
                for n in range(TT):
                    steps.did(dve.tensor_tensor(acc[:, n, :], acc[:, n, :], ca[:, n, :], ALU.add))
                steps.settle()
                dve.sem_inc(out_done, 1)
                steps.end()
                sample(5)

            with dve.Fori(0, 2) as g:
                group(g, TILES[0] * g, TILES[0])
            for g in range(2, NG):
                group(g, sum(TILES[:g]), TILES[g])

        @block.gpsimd
        def _(pool):
            smp.gather(pool)


def program(nc, a, out):
    scratch = lambda name, shape, dt=F32: nc.dram_tensor(name, shape, dt).ap()
    k0h, k0l = (scratch(f"k0_{n}", [B * T // G * D, G], F32R) for n in ("hi", "lo"))
    q0h, q0l, q1h, q1l, k1h, k1l = (scratch(n, [B * S // G * D, G], F32R)
                                    for n in ("q0_hi", "q0_lo", "q1_hi", "q1_lo", "k1_hi", "k1_lo"))
    v0, v1 = scratch("v0", [B * T, H * V1]), scratch("v1", [B * S, H * V1])
    tables = [scratch(f"table{b}", [H * ROWS * PAIR]) for b in range(B)]
    att0, att1, x_part, x2, qp, cx = (scratch(n, [B * S, D]) for n in ("att0", "att1", "x_part", "x2", "qp", "cx"))
    idx, wt = scratch("idx", [B * S, NS], I32), scratch("wt", [B * S, NS * 2])
    with ExitStack() as ctx:
        ident = ctx.enter_context(nc.sbuf_tensor("ident", [P, P], F32))
        identb = ctx.enter_context(nc.sbuf_tensor("identb", [P, P], BF16))
        ahead = ctx.enter_context(nc.sbuf_tensor("ahead", [P, E0, E0], F32))
        x = a["x"].rearrange("b s d -> (b s) d")
        constants(nc, ident, identb, ahead)
        project_context(nc, a["ctxT"], a["L0_xattn_WkT"], a["L0_xattn_bk"], a["L0_xattn_WvT"], a["L0_xattn_bv"],
                        a["L1_xattn_WkT"], a["L1_xattn_bk"], a["L1_xattn_WvT"], a["L1_xattn_bv"], k0h, k0l, v0, tables)
        project_query(nc, x, a["L0_xattn_WqT"], a["L0_xattn_bq"], ident, q0h, q0l)
        attention(nc, "cross", T, q0h, q0l, k0h, k0l, v0, ident, identb, att0, range(B))
        NT = S // P
        for b in range(B):
            along = lambda batch, first, tiles: (tables[batch], qp, idx, wt, cx, batch * NT + first, tiles)
            moe_along, self_along = (along(b - 1, 0, NT // 2), along(b - 1, NT // 2, NT // 2)) if b > 0 else (None, None)
            ffn_moe(nc, x, att0, a["L0_xattn_WoT"], a["L0_xattn_bo"], a["L0_ffn_W_qkv"], a["L0_ffn_b_qkv"],
                    a["L0_ffn_W_gate"], a["L0_ffn_b_gate"], a["L0_ffn_W_experts"], a["L0_ffn_b_experts"], ident, ahead,
                    q1h, q1l, k1h, k1l, v1, x_part, b, moe_along)
            attention(nc, f"self{b}", S, q1h, q1l, k1h, k1l, v1, ident, identb, att1, [b], self_along)
            sample_positions(nc, x_part, att1, a["mask_BxS2_if0"], a["L1_xattn_WqT"], a["L1_xattn_bq"],
                             a["L1_xattn_WoffT"], a["L1_xattn_boff"], ident, x2, qp, idx, wt, b)
        ffn_last(nc, x2, cx, a["L1_xattn_WoT"], a["L1_xattn_bo"], a["L1_ffn_W_enc"], a["L1_ffn_b_enc"],
                 a["L1_ffn_W_s2c"], a["L1_ffn_b_s2c"], a["L1_ffn_Wr"], a["L1_ffn_br"], a["L1_ffn_W1"],
                 a["L1_ffn_b1"], a["L1_ffn_W2"], a["L1_ffn_b2"].rearrange("e m -> (e m)"), a["L1_ffn_W_c2s"],
                 a["L1_ffn_b_c2s"], a["L1_ffn_W_dec"], a["L1_ffn_b_dec"], a["L1_ffn_ln_g"], a["L1_ffn_ln_b"],
                 ident, ahead, out.rearrange("b s d -> (b s) d"), along(B - 1, 0, NT))


_TURNED = ["L0_xattn_Wq", "L0_xattn_Wk", "L0_xattn_Wv", "L0_xattn_Wo", "L1_xattn_Wq", "L1_xattn_Wk", "L1_xattn_Wv",
           "L1_xattn_Woff", "L1_xattn_Wo"]


def kernel(**inputs):
    import numpy as _np
    import concourse.bacc as _bacc
    from concourse import mybir as _mybir
    from concourse.bass_utils import run_bass_kernel_spmd as _run

    nc = _bacc.Bacc("TRN2", target_bir_lowering=False, num_devices=1)
    arrays, aps = {}, {}
    for name, value in inputs.items():
        v = _np.asarray(value)
        if name in _TURNED:
            name, v = name + "T", v.T
        elif name == "ctx_1024":
            name, v = "ctxT", v.reshape(B * T, D).T
        v = _np.ascontiguousarray(v)
        arrays[f"in_{name}"] = v
        aps[name] = nc.dram_tensor(f"in_{name}", v.shape, _mybir.dt.from_np(v.dtype), kind="ExternalInput").ap()
    out = nc.dram_tensor("out_0", (B, S, D), F32, kind="ExternalOutput").ap()
    program(nc, aps, out)
    r = _run(nc, [arrays], core_ids=[0])
    return r.results[0]["out_0"]
```

```python
from contextlib import ExitStack

import concourse.bass as bass
from concourse import mybir

F32 = mybir.dt.float32
F32R = mybir.dt.float32r
BF16 = mybir.dt.bfloat16
I32 = mybir.dt.int32
ALU = mybir.AluOpType
ACT = mybir.ActivationFunctionType
X = mybir.AxisListType.X

P = 128
B, S, T, D = 2, 1024, 2048, 512
H, HD = 16, 32
C = D // P
G = 512
TT = G // P
NK5 = 5
NS = H * NK5
ROWS = T + 4
PAIR = 2 * HD
E0 = 8
HID, MM, EH, E1 = 1024, 64, 512, 8
V1 = HD + 1
EPS = 1e-5
SCALE = float(HD) ** -0.5


class Steps:

    def __init__(self, eng, sem, per):
        self.eng, self.sem, self.per = eng, sem, per

    def begin(self, it):
        self.it, self.k = it, 0

    def did(self, ins):
        ins.then_inc(self.sem, 1)
        self.k += 1
        return ins

    def settle(self):
        self.eng.wait_ge(self.sem, self.it * self.per + self.k)

    def end(self):
        assert self.k == self.per, f"{self.k} steps, not {self.per}"


class Tools:
    def __init__(self, nc, ctx, tag):
        self.nc, self.ctx, self.tag, self.own = nc, ctx, tag, []

    def sb(self, name, shape, dt=F32):
        return self.ctx.enter_context(self.nc.sbuf_tensor(f"{self.tag}_{name}", shape, dt))

    def ps(self, name, shape, dt=F32):
        return self.ctx.enter_context(self.nc.psum_tensor(f"{self.tag}_{name}", shape, dt))

    def sem(self, name):
        self.own.append(self.nc.alloc_semaphore(f"{self.tag}_{name}"))
        return self.own[-1]

    def sems(self, name, n):
        return [self.sem(f"{name}{i}") for i in range(n)]


    def block(self):
        self.ctx.callback(self.retire)
        return self.ctx.enter_context(self.nc.Block())

    def retire(self):
        self.nc.clear_and_free_semaphores(self.own)
        self.nc.all_engine_barrier()


def row_of(vec, n):
    return bass.AP(vec.tensor, vec.offset, [[0, P], [1, n]])


def layer_norm(steps, eng, passed, x, out, stats, mv, rstd):
    var, half, y, sq = (rstd[:, i, :] for i in range(4))
    for t in range(TT):
        steps.did(eng.bn_stats(stats[:, t, :], x[:, t, :]))
    steps.settle()
    if passed:
        eng.sem_inc(passed, 1)
    for t in range(TT):
        steps.did(eng.bn_aggr(mv[:, t, :], stats[:, t, :]))
    steps.settle()
    steps.did(eng.tensor_scalar(var, mv[:, :, 1], EPS, None, ALU.add))
    steps.settle()
    steps.did(eng.tensor_scalar(y.bitcast(I32), var.bitcast(I32), 1, None, ALU.logical_shift_right))
    steps.did(eng.tensor_scalar(half, var, -0.5, None, ALU.mult))
    steps.settle()
    steps.did(eng.tensor_scalar(y.bitcast(I32), y.bitcast(I32), -1.0, float(0x5F3759DF), ALU.mult, ALU.add))
    steps.settle()
    for _ in range(3):
        steps.did(eng.tensor_tensor(sq, y, y, ALU.mult))
        steps.settle()
        steps.did(eng.tensor_tensor(sq, sq, half, ALU.mult))
        steps.settle()
        steps.did(eng.scalar_tensor_tensor(out=y, in0=sq, scalar=1.5, in1=y, op0=ALU.add, op1=ALU.mult))
        steps.settle()
    if out is not None:
        for t in range(TT):
            steps.did(eng.tensor_scalar(out[:, t, :], x[:, t, :], mv[:, t, 0:1], y[:, t:t + 1],
                                        ALU.subtract, ALU.mult))
        steps.settle()


def constants(nc, ident, identb, ahead):
    with ExitStack() as ctx:
        t = Tools(nc, ctx, "const")
        made = t.sem("made")
        passed = t.sems("passed", 4)
        block = t.block()

        @block.gpsimd
        def _(pool):
            pool.memset(ident[:, :], 0.0).then_inc(made, 1)
            pool.memset(identb[:, :], 0.0).then_inc(made, 1)
            pool.memset(ahead[:, :, :], 0.0).then_inc(made, 1)
            pool.wait_ge(made, 3)
            for m in (ident, identb):
                pool.affine_select(out=m[:, :], in_=m[:, :], compare_op=ALU.not_equal, fill=1.0, base=0,
                                   pattern=[[-1, P]], channel_multiplier=1).then_inc(made, 1)
            pool.affine_select(out=ahead[:, :, :], in_=ahead[:, :, :], compare_op=ALU.is_ge, fill=1.0, base=0,
                               pattern=[[-1, E0], [1, E0]], channel_multiplier=0).then_inc(made, 1)
            pool.wait_ge(made, 6)


def split(act, dve, src, hi, lo, loaded, free, hi_done, lo_done):
    if act:
        act.wait_ge(*loaded)
        if free:
            act.wait_ge(*free)
        act.copy(hi, src).then_inc(hi_done[0], 1)
    if dve:
        dve.wait_ge(*loaded)
        dve.wait_ge(*hi_done)
        dve.tensor_tensor(lo, src, hi.bitcast(F32), ALU.subtract).then_inc(lo_done, 1)


def product(pe, out, left, right, n):
    for c in range(n):
        (lh, ll), (rh, rl) = left(c), right(c)
        pe.matmul(out, lh, rh, start=(c == 0), stop=False)
        pe.matmul(out, lh, rl, start=False, stop=False)
        mm = pe.matmul(out, ll, rh, start=False, stop=(c == n - 1))
    return mm


def project_context(nc, ctxT, wkT0, bk0, wvT0, bv0, wkT1, bk1, wvT1, bv1, k_hi, k_lo, v_ones, tables):
    NG = B * T // G
    W = (wkT0, wvT0, wkT1, wvT1)
    with ExitStack() as ctx:
        t = Tools(nc, ctx, "ctx")
        wh = [t.sb(f"wh{i}", [P, C, D], F32R) for i in range(4)]
        wl = [t.sb(f"wl{i}", [P, C, D], F32R) for i in range(4)]
        bk0_c = t.sb("bk0_c", [P, C])
        rows = t.sb("rows", [P, 3, D])
        x = t.sb("x", [P, 2, C, G])
        xh, xl = t.sb("xh", [P, 2, C, G], F32R), t.sb("xl", [P, 2, C, G], F32R)
        kh, kl = t.sb("kh", [P, 2, C, G], F32R), t.sb("kl", [P, 2, C, G], F32R)
        vo = t.sb("vo", [P, 2, TT, H, V1])
        kv = t.sb("kv", [P, TT, H, 2, HD])
        zero = t.sb("zero", [H, 2 * PAIR])
        R = 8
        bank = [t.ps(f"bank{i}", [P, G]) for i in range(R)]
        b_in = t.sem("b_in")
        x_in, x_hi, x_lo, x_used = t.sems("x_in", 2), t.sems("x_hi", 2), t.sems("x_lo", 2), t.sems("x_used", 2)
        full, free = t.sems("full", R), t.sems("free", R)
        hi_done, out_ready, kv_ready = t.sem("hi_done"), t.sem("out_ready"), t.sem("kv_ready")
        out_free, kv_free = t.sems("out_free", 2), t.sem("kv_free")
        stored, kv_stored, preset, zeroed, zeros_out = (t.sem(n) for n in ("stored", "kv_stored", "preset", "zeroed", "zeros_out"))
        N = 4 * TT
        passed = t.sems("passed", 4)
        block = t.block()

        @block.sync
        def _(sp):
            for i, src in enumerate(W):
                if i >= 2:
                    sp.wait_ge(x_lo[i % 2], i // 2)
                sp.dma_start(x[:, i % 2, :, :], src.rearrange("(c p) n -> p c n", p=P)).then_inc(x_in[i % 2], 16)
            sp.dma_start(bk0_c[:, :], bk0.rearrange("(c p) -> p c", p=P), allow_slow_non_contiguous=True).then_inc(b_in, 16)
            for i, src in enumerate((bv0, bk1, bv1)):
                sp.dma_start(rows[:, i, :], row_of(src, D)).then_inc(b_in, 16)
            xs = ctxT.rearrange("(c p) t -> p c t", p=P)
            with sp.Fori(0, NG // 2) as j:
                for u in range(2):
                    sp.wait_ge(x_lo[u], j + 2)
                    sp.sem_inc(passed[0], 1)
                    sp.dma_start(x[:, u, :, :], xs[:, :, bass.ds((2 * j + u) * G, G)]).then_inc(x_in[u], 16)

        @block.tensor
        def _(pe):
            for u in range(2):
                pe.sem_inc(x_used[u], 1)
            for k in range(R):
                pe.sem_inc(free[k], 1)
            with pe.Fori(0, NG // 2) as j:
                for u in range(2):
                    pe.wait_ge(x_lo[u], j + 3)
                    for k in range(N):
                        kind, o = divmod(k, TT)
                        r = slice(o * P, (o + 1) * P)
                        whole = lambda c: (xh[:, u, c, :], xl[:, u, c, :])
                        part = lambda c: (xh[:, u, c, r], xl[:, u, c, r])
                        pe.wait_ge(free[k % R], (2 * j + u) * (N // R) + (k // R + 1))
                        if kind == 0:
                            mm = product(pe, bank[k % R][:, :], lambda c: (wh[0][:, c, r], wl[0][:, c, r]), whole, C)
                        else:
                            mm = product(pe, bank[k % R][:, :], part, lambda c: (wh[kind][:, c, :], wl[kind][:, c, :]), C)
                        mm.then_inc(full[k % R], 1)
                    pe.wait_ge(full[(N - 1) % R], (2 * j + u + 1) * (N // R))
                    pe.sem_inc(x_used[u], 1)

        def split_weights(act, dve):
            for i in range(len(W)):
                u, k = i % 2, i // 2 + 1
                split(act, dve, x[:, u, :, :], wh[i][:, :, :], wl[i][:, :, :], (x_in[u], 16 * k), None, (x_hi[u], k), x_lo[u])

        def split_group(act, dve, j, u):
            split(act, dve, x[:, u, :, :], xh[:, u, :, :], xl[:, u, :, :], (x_in[u], 16 * j + 48), (x_used[u], j + 1),
                  (x_hi[u], j + 3), x_lo[u])

        def ahead(act, dve, j, u):
            if u == 0 or not isinstance(j, int):
                split_group(act, dve, *((j, 1) if u == 0 else (j + 1, 0)))

        def groups(eng, group):
            with eng.Fori(0, NG // 2 - 1) as j:
                for u in range(2):
                    group(j, u)
            for u in range(2):
                group(NG // 2 - 1, u)

        @block.scalar
        def _(act):
            split_weights(act, None)
            split_group(act, None, 0, 0)
            act.wait_ge(b_in, 16 * 4)

            def group(j, u):
                act.wait_ge(out_free[u], j + 1)
                for o in range(C):
                    act.wait_ge(full[o % R], (2 * j + u) * (N // R) + (o // R + 1))
                    act.activation(kh[:, u, o, :], bank[o % R][:, :], ACT.Identity,
                                   bias=bk0_c[:, o:o + 1]).then_inc(hi_done, 1)
                ahead(act, None, j, u)

            groups(act, group)

        @block.vector
        def _(dve):
            dve.memset(vo[:, :, :, :, HD:V1], 1.0).then_inc(preset, 1)
            dve.wait_ge(preset, 1)
            split_weights(None, dve)
            split_group(None, dve, 0, 0)
            dve.wait_ge(b_in, 16 * 4)

            def group(j, u):
                dve.wait_ge(out_free[u], j + 1)
                for k in range(N):
                    kind, o = divmod(k, TT)
                    if k == TT:
                        ahead(None, dve, j, u)
                    if k == 2 * TT:
                        dve.wait_ge(kv_free, 2 * j + (u + 1))
                    dve.wait_ge(full[k % R], (2 * j + u) * (N // R) + (k // R + 1))
                    if kind == 0:
                        dve.wait_ge(hi_done, (2 * j + u) * C + (o + 1))
                        ins = dve.scalar_tensor_tensor(out=kl[:, u, o, :], in0=bank[k % R][:, :],
                                                       scalar=bk0_c[:, o:o + 1], in1=kh[:, u, o, :].bitcast(F32),
                                                       op0=ALU.add, op1=ALU.subtract)
                    else:
                        src = bank[k % R][:, :].rearrange("p (h d) -> p h d", h=H)
                        add = rows[:, kind - 1, :].rearrange("p (h d) -> p h d", h=H)
                        dst = vo[:, u, o, :, 0:HD] if kind == 1 else kv[:, o, :, kind - 2, :]
                        ins = dve.tensor_tensor(dst, src, add, ALU.add)
                    ins.then_inc(free[k % R], 1)
                    if k == 2 * TT - 1:
                        dve.wait_ge(free[k % R], (2 * j + u) * (N // R) + (k // R + 2))
                        dve.sem_inc(out_ready, 1)
                dve.wait_ge(free[(N - 1) % R], (2 * j + u) * (N // R) + (N // R + 1))
                dve.sem_inc(kv_ready, 1)

            groups(dve, group)

        @block.gpsimd
        def _(pool):
            for u in range(2):
                pool.sem_inc(out_free[u], 1)
            pool.sem_inc(kv_free, 1)
            pool.memset(zero[:, :], 0.0).then_inc(zeroed, 1)
            pool.wait_ge(zeroed, 1)
            for tab in tables:
                rv = tab.rearrange("(h r d) -> h r d", h=H, r=ROWS)
                pool.dma_start(rv[:, 0:2, :], zero[:, :].rearrange("h (r d) -> h r d", r=2)).then_inc(zeros_out, 16)
                pool.dma_start(rv[:, T + 2:ROWS, :], zero[:, :].rearrange("h (r d) -> h r d", r=2)).then_inc(zeros_out, 16)
            hi = k_hi.rearrange("(g c p) t -> g p c t", c=C, p=P)
            lo = k_lo.rearrange("(g c p) t -> g p c t", c=C, p=P)
            vd = v_ones.rearrange("(n p) f -> p n f", p=P)
            for b in range(B):
                tab = tables[b].rearrange("(h r d) -> r h d", h=H, r=ROWS)
                with pool.Fori(0, NG // B // 2) as j:
                    for u in range(2):
                        g = 2 * j + (u + (NG // B) * b)
                        pool.wait_ge(out_ready, g + 1)
                        pool.sem_inc(passed[1], 1)
                        pool.dma_start(hi[bass.ds(g, 1), :, :, :].rearrange("a p c t -> (a p) c t").bitcast(F32),
                                       kh[:, u, :, :].bitcast(F32)).then_inc(stored, 16)
                        pool.dma_start(lo[bass.ds(g, 1), :, :, :].rearrange("a p c t -> (a p) c t").bitcast(F32),
                                       kl[:, u, :, :].bitcast(F32)).then_inc(stored, 16)
                        pool.dma_start(vd[:, bass.ds(g * TT, TT), :],
                                       vo[:, u, :, :, :].rearrange("p n h d -> p n (h d)")).then_inc(stored, 16)
                        pool.wait_ge(kv_ready, g + 1)
                        pool.sem_inc(passed[1], 1)
                        for o in range(TT):
                            pool.dma_start(tab[bass.ds((2 * j + u) * G + (o * P + 2), P), :, :],
                                           kv[:, o, :, :, :].rearrange("p h a d -> p h (a d)")).then_inc(kv_stored, 16)
                        pool.wait_ge(stored, 48 * g + 48)
                        pool.sem_inc(out_free[u], 1)
                        pool.wait_ge(kv_stored, 16 * TT * g + 16 * TT)
                        pool.sem_inc(kv_free, 1)
            pool.wait_ge(zeros_out, 16 * 2 * B)


def project_query(nc, x_dram, wqT, bq, ident, q_hi, q_lo):
    NG = B * S // G
    with ExitStack() as ctx:
        t = Tools(nc, ctx, "qry")
        w, wh, wl = t.sb("w", [P, C, D]), t.sb("wh", [P, C, D], F32R), t.sb("wl", [P, C, D], F32R)
        bq_c = t.sb("bq_c", [P, C])
        x = [t.sb(f"x{g}", [P, TT, D]) for g in range(NG)]
        ln = t.sb("ln", [P, 2, TT, D])
        lnh, lnl = t.sb("lnh", [P, C, G], F32R), t.sb("lnl", [P, C, G], F32R)
        stats, mv, rstd = t.sb("stats", [P, TT, 6]), t.sb("mv", [P, TT, 2]), t.sb("rstd", [P, 4, TT])
        qh, ql = t.sb("qh", [P, 2, C, G], F32R), t.sb("ql", [P, 2, C, G], F32R)
        tb = [t.ps(f"tb{i}", [P, G]) for i in range(4)]
        qb = [t.ps(f"qb{i}", [P, G]) for i in range(4)]
        w_in, b_in, x_in = t.sem("w_in"), t.sem("b_in"), t.sems("x_in", NG)
        w_hi, w_lo = t.sem("w_hi"), t.sem("w_lo")
        dsem, ln_done, t_full, lnh_done, lnl_done = (t.sem(n) for n in ("dve_steps", "ln_done", "t_full", "lnh_done", "lnl_done"))
        q_full, hi_done, lo_done = t.sem("q_full"), t.sem("hi_done"), t.sem("lo_done")
        stored, out_free = t.sem("stored"), t.sem("out_free")
        passed = t.sem("passed")
        block = t.block()

        @block.sync
        def _(sp):
            xs = x_dram.rearrange("(n p) d -> p n d", p=P)
            sp.dma_start(x[0][:, :, :], xs[:, 0:TT, :]).then_inc(x_in[0], 16)
            sp.dma_start(w[:, :, :], wqT.rearrange("(c p) n -> p c n", p=P)).then_inc(w_in, 16)
            sp.dma_start(bq_c[:, :], bq.rearrange("(c p) -> p c", p=P), allow_slow_non_contiguous=True).then_inc(b_in, 16)
            for g in range(1, NG):
                sp.dma_start(x[g][:, :, :], xs[:, g * TT:(g + 1) * TT, :]).then_inc(x_in[g], 16)

        @block.vector
        def _(dve):
            steps = Steps(dve, dsem, 25)

            def normalize(g):
                steps.begin(g)
                dve.wait_ge(x_in[g], 16)
                if g >= 2:
                    dve.wait_ge(t_full, C * (g - 1))
                layer_norm(steps, dve, None, x[g], ln[:, g % 2, :, :], stats, mv, rstd)
                steps.end()
                dve.sem_inc(ln_done, 1)

            normalize(0)
            split(None, dve, w[:, :, :], wh[:, :, :], wl[:, :, :], (w_in, 16), None, (w_hi, 1), w_lo)
            dve.wait_ge(b_in, 16)
            for g in range(NG):
                for c in range(C):
                    dve.wait_ge(lnh_done, g * C + c + 1)
                    dve.tensor_tensor(lnl[:, c, :], tb[c][:, :], lnh[:, c, :].bitcast(F32), ALU.subtract).then_inc(lnl_done, 1)
                if g + 1 < NG:
                    normalize(g + 1)
                dve.wait_ge(out_free, g + 1)
                for o in range(C):
                    dve.wait_ge(q_full, g * C + o + 1)
                    dve.wait_ge(hi_done, g * C + o + 1)
                    dve.scalar_tensor_tensor(out=ql[:, g % 2, o, :], in0=qb[o][:, :], scalar=bq_c[:, o:o + 1],
                                             in1=qh[:, g % 2, o, :].bitcast(F32), op0=ALU.add,
                                             op1=ALU.subtract).then_inc(lo_done, 1)

        @block.tensor
        def _(pe):
            pe.sem_inc(lo_done, 1)
            pe.wait_ge(w_lo, 1)
            with pe.Fori(0, NG // 2) as j:
                for u in range(2):
                    g = 2 * j + u
                    pe.wait_ge(ln_done, g + 1)
                    for c in range(C):
                        for n in range(TT):
                            mm = pe.transpose(tb[c][:, n * P:(n + 1) * P], ln[:, u, n, c * P:(c + 1) * P], ident[:, :])
                        mm.then_inc(t_full, 1)
                    pe.wait_ge(lnl_done, g * C + C)
                    pe.wait_ge(lo_done, g * C + 1)
                    for o in range(C):
                        r = slice(o * P, (o + 1) * P)
                        product(pe, qb[o][:, :], lambda c: (wh[:, c, r], wl[:, c, r]), lambda c: (lnh[:, c, :], lnl[:, c, :]),
                                C).then_inc(q_full, 1)

        @block.scalar
        def _(act):
            split(act, None, w[:, :, :], wh[:, :, :], wl[:, :, :], (w_in, 16), None, (w_hi, 1), w_lo)
            act.wait_ge(b_in, 16)
            for g in range(NG):
                for c in range(C):
                    act.wait_ge(t_full, g * C + c + 1)
                    act.copy(lnh[:, c, :], tb[c][:, :]).then_inc(lnh_done, 1)
                act.wait_ge(out_free, g + 1)
                for o in range(C):
                    act.wait_ge(q_full, g * C + o + 1)
                    act.activation(qh[:, g % 2, o, :], qb[o][:, :], ACT.Identity, bias=bq_c[:, o:o + 1]).then_inc(hi_done, 1)

        @block.gpsimd
        def _(pool):
            for _ in range(2):
                pool.sem_inc(out_free, 1)
            hi = q_hi.rearrange("(g c p) t -> g p c t", c=C, p=P)
            lo = q_lo.rearrange("(g c p) t -> g p c t", c=C, p=P)
            with pool.Fori(0, NG // 2) as j:
                for u in range(2):
                    g = 2 * j + u
                    pool.wait_ge(lo_done, g * C + (C + 1))
                    pool.sem_inc(passed, 1)
                    for dst, src in ((hi, qh), (lo, ql)):
                        pool.dma_start(dst[bass.ds(g, 1), :, :, :].rearrange("a p c t -> (a p) c t").bitcast(F32),
                                       src[:, u, :, :].bitcast(F32)).then_inc(stored, 16)
                    pool.wait_ge(stored, 32 * g + 32)
                    pool.sem_inc(out_free, 1)


class Samples:
    HS = H // 2
    SS = NS // 2

    def __init__(self, t, table, qp_dram, idx_dram, wt_dram, out, first, tiles, sums_on_pool=False):
        HS, SS = self.HS, self.SS
        self.sums_on_pool = sums_on_pool
        self.pool_steps, self.sums_done, self.a_done = t.sem("pool_steps"), t.sem("sums_done"), t.sem("a_done")
        self.table, self.drams, self.first, self.tiles = table, (qp_dram, idx_dram, wt_dram, out), first, tiles
        self.rows = [t.sb(f"rows{i}", [P, SS, 2 * PAIR]) for i in range(2)]
        self.idx = [t.sb(f"idx{i}", [P, SS], I32) for i in range(2)]
        self.wt = [t.sb(f"wt{i}", [P, SS, 2]) for i in range(2)]
        self.qp = [t.sb(f"qp{i}", [P, HS * HD]) for i in range(2)]
        self.prod = t.sb("prod", [P, HS // 2, 2 * NK5, HD])
        self.s10, self.a10 = t.sb("s10", [P, HS, NK5, 2]), t.sb("a10", [P, HS, NK5, 2])
        self.s5, self.red = t.sb("s5", [P, HS, NK5]), t.sb("sred", [P, HS, 1])
        self.o = [t.sb(f"so{i}", [P, HS * HD]) for i in range(2)]
        self.idx_in, self.qw_in, self.gathered = t.sems("idx_in", 2), t.sems("qw_in", 2), t.sems("gathered", 2)
        self.steps_sem, self.s_done, self.e_done = t.sem("sample_steps"), t.sem("s_done"), t.sem("e_done")
        self.o_done, self.o_free, self.stored = t.sems("so_done", 2), t.sems("so_free", 2), t.sems("so_stored", 2)
        self.passed = t.sem("samples_passed")

    def gather(self, pool):
        SS, W = self.SS, self.HS * HD
        out = self.drams[3]

        def rows_of(j, u, s0, s1):
            for s in range(s0, s1):
                pool.indirect_dma_start(self.rows[u][:, s, :], None, self.table.rearrange("(n a) -> n a", a=1),
                                        bass.IndirectOffsetOnAxis(self.idx[u][:, s:s + 1], 0)).then_inc(self.gathered[u], 16)

        def store(j, u):
            pool.wait_ge(self.o_done[u], j + 1)
            pool.sem_inc(self.passed, 1)
            pool.dma_start(out[bass.ds((j + self.first) * P, P), u * W:(u + 1) * W], self.o[u][:, :]).then_inc(self.stored[u], 16)

        def half(j, u, first):
            before = None if first and u == 0 else (j, 0) if u == 1 else (j - 1, 1)
            pool.wait_ge(self.idx_in[u], 16 * j + 16)
            pool.sem_inc(self.passed, 1)
            rows_of(j, u, 0, SS // 2)
            if not first:
                pool.wait_ge(self.stored[u], 16 * j)
                pool.sem_inc(self.o_free[u], 1)
            if before and self.sums_on_pool:
                self.pool_scores(pool, *before)
            rows_of(j, u, SS // 2, SS)
            if before:
                if self.sums_on_pool:
                    self.pool_output(pool, *before)
                store(*before)

        for u in range(2):
            pool.sem_inc(self.o_free[u], 1)
        for u in range(2):
            half(0, u, True)
        if self.tiles > 2:
            with pool.Fori(1, self.tiles - 1) as j:
                for u in range(2):
                    half(j, u, False)
        if self.tiles > 1:
            for u in range(2):
                half(self.tiles - 1, u, False)
        if self.sums_on_pool:
            self.pool_scores(pool, self.tiles - 1, 1)
            self.pool_output(pool, self.tiles - 1, 1)
        store(self.tiles - 1, 1)
        for u in range(2):
            pool.wait_ge(self.stored[u], 16 * self.tiles)

    def load_first(self, act):
        for u in range(2):
            self.load_idx(act, 0, u)
        self.load_qw(act, 0, 0)

    def load_idx(self, eng, j, u):
        SS = self.SS
        eng.dma_start(self.idx[u][:, :], self.drams[1][bass.ds((j + self.first) * P, P), u * SS:(u + 1) * SS]).then_inc(self.idx_in[u], 16)

    def load_qw(self, eng, j, u):
        qp_dram, _, wt_dram, _ = self.drams
        SS, W = self.SS, self.HS * HD
        r = bass.ds((j + self.first) * P, P)
        eng.dma_start(self.wt[u][:, :, :].rearrange("p s a -> p (s a)"), wt_dram[r, 2 * u * SS:2 * (u + 1) * SS]).then_inc(self.qw_in[u], 16)
        eng.dma_start(self.qp[u][:, :], qp_dram[r, u * W:(u + 1) * W]).then_inc(self.qw_in[u], 16)

    def views(self, u):
        kv = self.rows[u][:, :, :].rearrange("p (h k) (m a d) -> p h (k m) a d", k=NK5, a=2, d=HD)
        return kv, self.wt[u][:, :, :].rearrange("p (h k) m -> p h k m", h=self.HS)

    def pool_scores(self, pool, j, u):
        HS, prod = self.HS, self.prod
        kv, _ = self.views(u)
        q = self.qp[u][:, :].rearrange("p (h d) -> p h d", h=HS)
        self.psteps = Steps(pool, self.pool_steps, 22)
        self.psteps.begin(2 * j + u)
        go = lambda ins: (self.psteps.did(ins), self.psteps.settle())
        pool.wait_ge(self.gathered[u], 16 * self.SS * j + 16 * self.SS)
        pool.wait_ge(self.qw_in[u], 32 * j + 32)
        pool.sem_inc(self.passed, 1)
        for h in (0, HS // 2):
            r = slice(h, h + HS // 2)
            go(pool.tensor_tensor(prod[:, :, :, :], kv[:, r, :, 0, :],
                                  q[:, r, :].unsqueeze(2).to_broadcast([P, HS // 2, 2 * NK5, HD]), ALU.mult))
            n = HD // 2
            while n > 1:
                go(pool.tensor_tensor(prod[:, :, :, 0:n], prod[:, :, :, 0:n], prod[:, :, :, n:2 * n], ALU.add))
                n //= 2
            go(pool.tensor_tensor(self.s10[:, r, :, :].rearrange("p h k m -> p h (k m)"), prod[:, :, :, 0],
                                  prod[:, :, :, 1], ALU.add))
        pool.sem_inc(self.sums_done, 1)

    def pool_output(self, pool, j, u):
        HS, prod = self.HS, self.prod
        kv, _ = self.views(u)
        go = lambda ins: (self.psteps.did(ins), self.psteps.settle())
        pool.wait_ge(self.a_done, 2 * j + (u + 1))
        pool.sem_inc(self.passed, 1)
        for h in (0, HS // 2):
            r = slice(h, h + HS // 2)
            go(pool.tensor_tensor(prod[:, :, :, :], kv[:, r, :, 1, :], self.a10[:, r, :, :].rearrange("p h k m -> p h (k m)")
                                  .unsqueeze(3).to_broadcast([P, HS // 2, 2 * NK5, HD]), ALU.mult))
            n = NK5
            go(pool.tensor_tensor(prod[:, :, 0:n, :], prod[:, :, 0:n, :], prod[:, :, n:2 * n, :], ALU.add))
            go(pool.tensor_tensor(prod[:, :, 0:2, :], prod[:, :, 0:2, :], prod[:, :, 2:4, :], ALU.add))
            go(pool.tensor_tensor(prod[:, :, 0, :], prod[:, :, 0, :], prod[:, :, 1, :], ALU.add))
            go(pool.tensor_tensor(self.o[u][:, h * HD:(h + HS // 2) * HD].rearrange("p (h d) -> p h d", h=HS // 2),
                                  prod[:, :, 0, :], prod[:, :, 4, :], ALU.add))
        pool.sem_inc(self.o_done[u], 1)
        self.psteps.end()

    def scores(self, dve, j, u):
        HS, s5, red, s10 = self.HS, self.s5[:, :, :], self.red[:, :, :], self.s10
        kv, w = self.views(u)
        self.steps = Steps(dve, self.steps_sem, 8 if self.sums_on_pool else 16)
        self.steps.begin(2 * j + u)
        go = lambda ins: (self.steps.did(ins), self.steps.settle())
        q = self.qp[u][:, :].rearrange("p (h d) -> p h d", h=HS)
        dve.wait_ge(self.qw_in[u], 32 * j + 32)
        if self.sums_on_pool:
            dve.wait_ge(self.sums_done, 2 * j + (u + 1))
        else:
            dve.wait_ge(self.gathered[u], 16 * self.SS * j + 16 * self.SS)
            for h in (0, HS // 2):
                r = slice(h, h + HS // 2)
                go(dve.tensor_tensor(self.prod[:, :, :, :], kv[:, r, :, 0, :],
                                     q[:, r, :].unsqueeze(2).to_broadcast([P, HS // 2, 2 * NK5, HD]), ALU.mult))
                go(dve.tensor_reduce(s10[:, r, :, :].rearrange("p h k m -> p h (k m)"), self.prod[:, :, :, :], X, ALU.add))
        go(dve.tensor_tensor(s10[:, :, :, :], s10[:, :, :, :], w, ALU.mult))
        go(dve.tensor_tensor(s5, s10[:, :, :, 0], s10[:, :, :, 1], ALU.add))
        go(dve.tensor_reduce(red, s5, X, ALU.max))
        go(dve.tensor_tensor(s5, s5, red.to_broadcast([P, HS, NK5]), ALU.subtract))
        dve.sem_inc(self.s_done, 1)

    def weights(self, act, j, u):
        act.wait_ge(self.s_done, 2 * j + (u + 1))
        act.activation(self.s5[:, :, :], self.s5[:, :, :], ACT.Exp, scale=SCALE).then_inc(self.e_done, 1)
        if not (isinstance(j, int) and j == self.tiles - 1 and u == 1):
            self.load_qw(act, *((j, 1) if u == 0 else (j + 1, 0)))
        if not (isinstance(j, int) and j == self.tiles - 1):
            self.load_idx(act, j + 1, u)

    def output(self, dve, j, u):
        HS, s5, red, a10 = self.HS, self.s5[:, :, :], self.red[:, :, :], self.a10[:, :, :, :]
        kv, w = self.views(u)
        go = lambda ins: (self.steps.did(ins), self.steps.settle())
        dve.wait_ge(self.e_done, 2 * j + (u + 1))
        go(dve.tensor_reduce(red, s5, X, ALU.add))
        go(dve.reciprocal(red, red))
        go(dve.tensor_tensor(s5, s5, red.to_broadcast([P, HS, NK5]), ALU.mult))
        go(dve.tensor_tensor(a10, w, s5.unsqueeze(3).to_broadcast([P, HS, NK5, 2]), ALU.mult))
        if self.sums_on_pool:
            dve.sem_inc(self.a_done, 1)
        else:
            dve.wait_ge(self.o_free[u], j + 1)
            for h in (0, HS // 2):
                r = slice(h, h + HS // 2)
                go(dve.tensor_tensor(self.prod[:, :, :, :], kv[:, r, :, 1, :], a10[:, r, :, :].rearrange("p h k m -> p h (k m)")
                                     .unsqueeze(3).to_broadcast([P, HS // 2, 2 * NK5, HD]), ALU.mult))
                go(dve.tensor_reduce(self.o[u][:, h * HD:(h + HS // 2) * HD].rearrange("p (h d) -> p h d", h=HS // 2),
                                     self.prod[:, :, :, :].rearrange("p h s d -> p h d s"), X, ALU.add))
            dve.sem_inc(self.o_done[u], 1)
        self.steps.end()


def attention(nc, tag, TK, q_hi, q_lo, k_hi, k_lo, v_ones, ident, identb, out, batches, samples=None):
    NK = TK // P
    QG, KG = S // G, TK // G
    WA = 1024
    NKC = TK // WA
    NA = (S // P) * NKC
    NQ = S // P
    HALF = S // 2
    HU = 4
    NH = len(batches) * H
    PR = 4
    R = 4
    EARLY = 3
    S_SCORES, S_WEIGHTS, S_OUT = (R + 1, R + 3, R + 5) if NK > 2 * R else (R + 1, R + 2, R + 3)
    assert NA == NK
    units = [[(1, s + EARLY)] if s + EARLY <= NA else [(2, s + EARLY - NA - 1)] for s in range(NK)]
    units[NK - 1].append((2, EARLY - 1))
    assert units[NK - 2] == [(2, 0)] and units[NK - 1] == [(2, 1), (2, 2)]
    with ExitStack() as ctx:
        t = Tools(nc, ctx, tag)
        kst = [t.sb(f"kst{i}", [P, TK], F32R) for i in range(HU)]
        qst = [t.sb(f"qst{i}", [P, S], F32R) for i in range(HU)]
        v = [t.sb(f"v{i}", [P, NK, V1]) for i in range(HU)]
        p = [t.sb(f"p{i}", [P, S]) for i in range(PR)]
        oT = [t.sb(f"oT{i}", [P, HALF]) for i in range(2)]
        o = [t.sb(f"o{i}", [P, NQ, HD]) for i in range(2)]
        inv = [t.sb(f"inv{i}", [P, NQ // 2, 2, 1]) for i in range(2)]
        mx = t.sb("mx", [P, NA, 2])
        negm = t.sb("negm", [P, NQ], BF16)
        ps_a = [t.ps(f"ps_a{i}", [P, WA // 2]) for i in range(2)]
        ps_b = [t.ps(f"ps_b{i}", [P, S]) for i in range(2)]
        ps_o = [t.ps(f"ps_o{i}", [P, HALF]) for i in range(2)]
        preset, loaded = t.sem("preset"), t.sems("loaded", HU)
        a_full, a_free, negm_done = t.sems("a_full", 2), t.sems("a_free", 2), t.sem("negm_done")
        b_full, exp_done, p_used = t.sems("b_full", 2), t.sems("exp_done", 2), t.sems("p_used", PR)
        o_full, oT_done, turned = t.sems("o_full", 2), t.sems("oT_done", 2), t.sems("turned", 2)
        o_done, o_free, o_out, inv_done = t.sems("o_done", 2), t.sems("o_free", 2), t.sems("o_out", 2), t.sem("inv_done")
        stored = t.sems("stored", 2)
        v_in = t.sems("v_in", HU)
        LOADS = 6
        passed = t.sems("passed", 4)
        smp = Samples(t, *samples, sums_on_pool=True) if samples else None
        block = t.block()

        @block.sync
        def _(sp):
            qh = q_hi.rearrange("(b g r) t -> b r g t", b=B, g=QG)
            ql = q_lo.rearrange("(b g r) t -> b r g t", b=B, g=QG)
            kh = k_hi.rearrange("(b g r) t -> b r g t", b=B, g=KG)
            kl = k_lo.rearrange("(b g r) t -> b r g t", b=B, g=KG)
            vs = v_ones.rearrange("(b n p) f -> b p n f", b=B, p=P)
            ov = out.rearrange("(b q p) d -> b p q d", b=B, p=P)

            def load(b, h, u):
                for i, (part, full) in enumerate(((qh, qst), (qh, qst), (ql, qst), (kh, kst), (kl, kst), (kh, kst))):
                    r = HD * (i % 3)
                    dst = full[u][r:r + HD, :].rearrange("r (g t) -> r g t", t=G)
                    sp.dma_start(dst.bitcast(F32), part[b, bass.ds(h * HD, HD), :, :].bitcast(F32)).then_inc(loaded[u], 16)
                sp.dma_start(v[u][:, :, :], vs[b, :, :, bass.ds(h * V1, V1)]).then_inc(v_in[u], 16)

            def store(b, h, u, use):
                i, k = u % 2, use * 2 + (u // 2 + 1)
                sp.wait_ge(o_done[i], k)
                sp.sem_inc(passed[1], 1)
                sp.dma_start(ov[b, :, :, bass.ds(h * HD, HD)], o[i][:, :, :]).then_inc(stored[i], 16)
                return i, k

            def stored_out(i, k):
                sp.wait_ge(stored[i], 16 * k)
                sp.sem_inc(o_out[i], 1)

            for i in range(2):
                sp.sem_inc(o_out[i], 1)
            for u in range(HU):
                load(batches[0], u, u)
            for nb, b in enumerate(batches):
                base = nb * (H // HU)
                with sp.Fori(0, H // HU - 1) as j:
                    for u in range(HU):
                        k = store(b, j * HU + u, u, j + base)
                        load(b, j * HU + (HU + u), u)
                        stored_out(*k)
                for u in range(HU):
                    k = store(b, H - HU + u, u, base + H // HU - 1)
                    if nb + 1 < len(batches):
                        load(batches[nb + 1], u, u)
                    stored_out(*k)

        def tile_of(j):
            behind = isinstance(j, int) and j == NH // HU - 1
            if smp and smp.tiles == 1:
                return 0 if behind else None
            if smp:
                assert smp.tiles in (NH // HU - 1, NH // HU)
                return j if not behind or smp.tiles == NH // HU else None

        def turns(j, u, left, step, end):
            for s in range(R, NK):
                step(j, u, s, left)
            if left != 0:
                nj, nu = (j, u + 1) if u + 1 < HU else (j + 1, 0)
                for s in range(R):
                    step(nj, nu, s, None if left is None else left - 1)
            else:
                step(j, u, NK, 0)
            end(j, u)

        def all_turns(eng, step, end):
            for s in range(R):
                step(0, 0, s, None)
            with eng.Fori(0, NH // HU - 1) as j:
                for u in range(HU):
                    turns(j, u, None, step, end)
            for u in range(HU):
                turns(NH // HU - 1, u, HU - 1 - u, step, end)

        @block.tensor
        def _(pe):

            def unit(j, u, a):
                if u >= HU:
                    j, u = j + 1, u - HU
                at = (j * HU + u) * (NA + 1) + a
                if a == NA:
                    pe.wait_ge(negm_done, j * HU + u + 1)
                    for i in range(2):
                        for q in range(NQ // 2):
                            k = i * (NQ // 2) + q
                            mm = pe.matmul(ps_a[i][0:1, q * P:(q + 1) * P], negm[:, k:k + 1], identb[:, :], start=True, stop=True)
                        mm.then_inc(a_full[i], 1)
                else:
                    if a == 0:
                        pe.wait_ge(loaded[u], 16 * LOADS * j + 16 * LOADS)
                    qt, kc = divmod(a, NKC)
                    for i in range(2):
                        if not isinstance(at, int) or at > 0:
                            pe.wait_ge(a_free[i], at)
                        k = kc * WA + i * (WA // 2)
                        pe.matmul(ps_a[i][:, :], qst[u][0:96, qt * P:(qt + 1) * P], kst[u][0:96, k:k + WA // 2],
                                  start=True, stop=True).then_inc(a_full[i], 1)

            def with_v(j, u, s):
                pe.wait_ge(exp_done[s % 2], (j * HU + u) * (NK // 2) + (s // 2 + 1))
                if s == 0:
                    pe.wait_ge(o_free[u % 2], j * 2 + (u // 2 + 1))
                    pe.wait_ge(v_in[u], 16 * j + 16)
                for i in range(2):
                    mm = pe.matmul(ps_o[u % 2][64 * i:64 * i + V1, :], v[u][:, s, :], p[s % PR][:, i * HALF:(i + 1) * HALF],
                                   start=(s == 0), stop=(s == NK - 1), skip_group_check=True)
                mm.then_inc(p_used[s % PR], 1)

            def step(j, u, s, left):
                n = j * HU + u
                if s == 0:
                    for i in range(2):
                        pe.wait_ge(a_free[i], n * (NA + 1) + (NA + 1))
                if s < NK:
                    if s >= 2 or not isinstance(n, int) or n > 0:
                        pe.wait_ge(exp_done[s % 2], n * (NK // 2) + s // 2)
                    for i in range(2):
                        mm = pe.matmul(ps_b[s % 2][:, i * 512:(i + 1) * 512], kst[u][0:97, s * P:(s + 1) * P],
                                       qst[u][0:97, i * 512:(i + 1) * 512], start=True, stop=True)
                    mm.then_inc(b_full[s % 2], 1)
                    for ahead, a in units[s][:1]:
                        if left is None or ahead <= left:
                            unit(j, u + ahead, a)
                if s > 0:
                    with_v(j, u, s - 1)
                elif not isinstance(n, int) or n > 0:
                    with_v(*((j, u - 1) if u > 0 else (j - 1, HU - 1)), NK - 1)
                if s < NK:
                    for ahead, a in units[s][1:]:
                        if left is None or ahead <= left:
                            unit(j, u + ahead, a)
                if s == 0 and not (isinstance(n, int) and n == 0) or s == NK:
                    pj, pu = (j, u) if s == NK else (j, u - 1) if u > 0 else (j - 1, HU - 1)
                    pe.wait_ge(p_used[(NK - 1) % PR], (pj * HU + pu) * (NK // PR) + NK // PR)
                    pe.sem_inc(o_full[pu % 2], 1)

            def end(j, u):
                i = u % 2
                pe.wait_ge(oT_done[i], j * 4 + (2 * (u // 2) + 2))
                for q in range(HALF // P):
                    mm = pe.transpose(ps_o[i][:, q * P:q * P + 97], oT[i][0:97, q * P:(q + 1) * P], ident[0:97, 0:97])
                mm.then_inc(turned[i], 1)

            pe.wait_ge(preset, HU + 2)
            for a in range(NA + 1):
                unit(0, 0, a)
            for a in range(EARLY):
                unit(0, 1, a)
            all_turns(pe, step, end)

        @block.scalar
        def _(act):

            def max_row(j, u):
                if u >= HU:
                    j, u = j + 1, u - HU
                for i in range(2):
                    act.wait_ge(a_full[i], (j * HU + u) * (NA + 1) + (NA + 1))
                    act.copy(qst[u][96:97, i * HALF:(i + 1) * HALF], ps_a[i][0:1, :]).then_inc(a_free[i], 1)

            def step(j, u, s, left):
                n = j * HU + u
                if s == NK:
                    return
                if s == S_WEIGHTS and u % 2 == 1 and tile_of(j) is not None:
                    smp.weights(act, tile_of(j), u // 2)
                act.wait_ge(b_full[s % 2], n * (NK // 2) + (s // 2 + 1))
                if s >= PR or not isinstance(n, int) or n > 0:
                    act.wait_ge(p_used[s % PR], n * (NK // PR) + s // PR)
                act.activation(p[s % PR][:, :], ps_b[s % 2][:, :], ACT.Exp, scale=SCALE).then_inc(exp_done[s % 2], 1)
                if (1, NA) in units[s] and (left is None or left >= 1):
                    max_row(j, u + 1)
                if s == 0 and not (isinstance(n, int) and n == 0):
                    copy_out(*((j, u - 1) if u > 0 else (j - 1, HU - 1)))

            def copy_out(j, u):
                i = u % 2
                act.wait_ge(o_full[i], j * 2 + (u // 2 + 1))
                for r in (0, 64):
                    act.copy(oT[i][r:r + V1, :], ps_o[i][r:r + V1, :]).then_inc(oT_done[i], 1)

            if smp:
                smp.load_first(act)
            act.wait_ge(preset, HU + 2)
            max_row(0, 0)
            all_turns(act, step, lambda j, u: copy_out(j, u) if isinstance(j, int) and j * HU + u == NH - 1 else None)

        @block.vector
        def _(dve):

            def unit(j, u, a):
                if u >= HU:
                    j, u = j + 1, u - HU
                n = j * HU + u
                if a < NA:
                    for i in range(2):
                        dve.wait_ge(a_full[i], n * (NA + 1) + (a + 1))
                        dve.tensor_reduce(mx[:, a, i:i + 1], ps_a[i][:, :], X, ALU.max).then_inc(a_free[i], 1)
                else:
                    for i in range(2):
                        dve.wait_ge(a_free[i], n * (NA + 1) + NA)
                    dve.tensor_reduce(negm[:, :], mx[:, :, :].rearrange("p (q c) i -> p q (c i)", c=NKC), X, ALU.max,
                                      negate=True).then_inc(negm_done, 1)

            def step(j, u, s, left):
                if s == S_SCORES and u % 2 == 1 and tile_of(j) is not None:
                    smp.scores(dve, tile_of(j), u // 2)
                if s == S_OUT and u % 2 == 1 and tile_of(j) is not None:
                    smp.output(dve, tile_of(j), u // 2)
                if s < NK:
                    for ahead, a in units[s]:
                        if left is None or ahead <= left:
                            unit(j, u + ahead, a)

            def end(j, u):
                i = u % 2
                acc = ps_o[i][:, :].rearrange("p (n a d) -> p n a d", a=2, d=64)
                dve.wait_ge(turned[i], j * 2 + (u // 2 + 1))
                dve.reciprocal(inv[i][:, :, :, :], acc[:, :, :, HD:V1]).then_inc(inv_done, 1)
                dve.wait_ge(inv_done, j * HU + (u + 1))
                dve.wait_ge(o_out[i], j * 2 + (u // 2 + 1))
                dst = o[i][:, :, :].rearrange("p (a n) d -> p n a d", a=2)
                dve.tensor_tensor(dst, acc[:, :, :, 0:HD], inv[i][:, :, :, :].to_broadcast([P, NQ // 2, 2, HD]),
                                  ALU.mult).then_inc(o_done[i], 1)
                dve.wait_ge(o_done[i], j * 2 + (u // 2 + 1))
                dve.sem_inc(o_free[i], 1)

            for u in range(HU):
                dve.memset(kst[u][96:97, :].bitcast(F32), 1.0).then_inc(preset, 1)
            for i in range(2):
                dve.sem_inc(o_free[i], 1)
                dve.memset(oT[i][:, :], 0.0).then_inc(preset, 1)
            for a in range(NA + 1):
                unit(0, 0, a)
            for a in range(EARLY):
                unit(0, 1, a)
            all_turns(dve, step, end)

        @block.gpsimd
        def _(pool):
            if smp:
                smp.gather(pool)


def top_two(steps, dve, prob, ahead, gt, eq, rank, sel):
    other = prob.unsqueeze(2).to_broadcast([P, TT, E0, E0])
    own = prob.unsqueeze(3).to_broadcast([P, TT, E0, E0])
    steps.did(dve.tensor_tensor(gt, other, own, ALU.is_gt))
    steps.did(dve.tensor_tensor(eq, other, own, ALU.is_equal))
    steps.settle()
    steps.did(dve.tensor_tensor(eq, eq, ahead.unsqueeze(1).to_broadcast([P, TT, E0, E0]), ALU.mult))
    steps.settle()
    steps.did(dve.tensor_tensor(gt, gt, eq, ALU.add))
    steps.settle()
    steps.did(dve.tensor_reduce(rank, gt, X, ALU.add))
    steps.settle()
    steps.did(dve.tensor_scalar(sel, rank, 1.5, None, ALU.is_lt))
    steps.settle()


def ffn_moe(nc, x_dram, attn, woT, bo, wqkv, bqkv, wg, bg, we, be, ident, ahead,
            q_hi, q_lo, k_hi, k_lo, v_ones, x_part, batch, samples=None):
    NG = S // G
    G0 = batch * NG
    KS = 4 + E0
    with ExitStack() as ctx:
        t = Tools(nc, ctx, f"moe{batch}")
        raw = [t.sb(f"raw{i}", [P, C, D]) for i in range(2)]
        wh = [t.sb(f"wh{i}", [P, C, D], F32R) for i in range(2)]
        wl = [t.sb(f"wl{i}", [P, C, D], F32R) for i in range(2)]
        w_g = t.sb("w_g", [P, C, E0])
        b_e = t.sb("b_e", [E0, D])
        qk_c = t.sb("qk_c", [P, 2 * C])
        rows = t.sb("rows", [P, 2, D])
        bg_r = t.sb("bg_r", [P, E0])
        ao = t.sb("ao", [P, TT, D])
        xT = t.sb("xT", [P, C, G])
        xh, xl = t.sb("xh", [P, C, G], F32R), t.sb("xl", [P, C, G], F32R)
        acc = t.sb("acc", [P, TT, D])
        ln = ao
        stats, mv, rstd = t.sb("stats", [P, TT, 6]), t.sb("mv", [P, TT, 2]), t.sb("rstd", [P, 4, TT])
        hi, lo = t.sb("hi", [P, C, G], F32R), t.sb("lo", [P, C, G], F32R)
        vo = t.sb("vo", [P, TT, H, V1])
        lg, ex, sel, rank = (t.sb(n, [P, TT, E0]) for n in ("lg", "ex", "sel", "rank"))
        gt, eq = (t.sb(n, [P, TT, E0, E0]) for n in ("gt", "eq"))
        red = t.sb("red", [P, TT, 1])
        comb = t.sb("comb", [P, TT, E0])
        combT = t.sb("combT", [E0, G])
        tb = [t.ps(f"tb{i}", [P, G]) for i in range(4)]
        m = [t.ps(f"m{i}", [P, G]) for i in range(4)]
        w_in, raw_in, in_sem, preset = t.sem("w_in"), t.sems("raw_in", 2), t.sem("in"), t.sem("preset")
        hi_split, lo_split, xh_done = t.sem("hi_split"), t.sem("lo_split"), t.sem("xh_done")
        t_full, t_out = t.sems("t_full", 4), t.sems("t_out", 4)
        m_full, m_free = t.sems("m_full", 4), t.sems("m_free", 4)
        dsem, hi_done = t.sem("dve_steps"), t.sem("hi_done")
        ln_done, lg_done, ex_done, comb_done, combT_done = (
            t.sem(n) for n in ("ln_done", "lg_done", "ex_done", "comb_done", "combT_done"))
        q_done, kv_done, out_done, turned = t.sem("q_done"), t.sem("kv_done"), t.sem("out_done"), t.sem("turned")
        q_out, kv_out, x_out = t.sem("q_out"), t.sem("kv_out"), t.sem("x_out")
        hilo_free, v_free, x_in = (t.sem(n) for n in ("hilo_free", "v_free", "x_in"))
        TU = [3, 3, 2, 2]
        MU = 4 + 1 + E0
        SAMPLE_AT = (-1, 2, 5)
        HALVES = len(SAMPLE_AT)
        smp = Samples(t, *samples) if samples else None
        row = lambda k: k if k < 4 else k + 1
        block = t.block()

        @block.sync
        def _(sp):
            xs = x_dram.rearrange("(n p) d -> p n d", p=P)
            as_ = attn.rearrange("(n p) d -> p n d", p=P)
            vd = v_ones.rearrange("(n p) f -> p n f", p=P)
            xd = x_part.rearrange("(n p) d -> p n d", p=P)
            tiles_of = lambda g: slice((G0 + g) * TT, (G0 + g + 1) * TT)
            chunks = [woT] + [wqkv[:, i * D:(i + 1) * D] for i in range(3)] + [we[e] for e in range(E0)]

            def load_chunk(n):
                if n >= 2:
                    sp.wait_ge(lo_split, n - 1)
                sp.dma_start(raw[n % 2][:, :, :], chunks[n % KS].rearrange("(c p) n -> p c n", p=P)).then_inc(raw_in[n % 2], 16)

            def load_attention(g):
                sp.dma_start(ao[:, :, :], as_[:, tiles_of(g), :]).then_inc(in_sem, 16)

            def load_x(g):
                sp.dma_start(acc[:, :, :], xs[:, tiles_of(g), :]).then_inc(x_in, 16)

            def store(src, dst, g, done):
                sp.dma_start(dst.rearrange("(g c p) t -> g p c t", c=C, p=P)[G0 + g, :, :, :].bitcast(F32),
                             src[:, :, :].bitcast(F32)).then_inc(done, 16)

            def store_x(g):
                sp.wait_ge(out_done, g + 1)
                sp.dma_start(xd[:, tiles_of(g), :], acc[:, :, :]).then_inc(x_out, 16)
                sp.wait_ge(x_out, 16 * (g + 1))

            load_attention(0)
            load_chunk(0)
            load_x(0)
            sp.dma_start(w_g[:, :, :], wg.rearrange("(c p) n -> p c n", p=P)).then_inc(w_in, 16)
            sp.dma_start(b_e[:, :], be).then_inc(w_in, 16)
            sp.dma_start(qk_c[:, :], bqkv[0:2 * D].rearrange("(c p) -> p c", p=P), allow_slow_non_contiguous=True).then_inc(w_in, 16)
            sp.dma_start(rows[:, 0, :], row_of(bo, D)).then_inc(w_in, 16)
            sp.dma_start(rows[:, 1, :], row_of(bqkv[2 * D:3 * D], D)).then_inc(w_in, 16)
            sp.dma_start(bg_r[:, :], row_of(bg, E0)).then_inc(w_in, 16)
            for g in range(NG):
                for k in range(KS):
                    if g > 0 or k > 0:
                        load_chunk(g * KS + k)
                    if k == 1 and g > 0:
                        store_x(g - 1)
                        load_x(g)
                    if k == 5:
                        sp.wait_ge(q_done, g + 1)
                        store(hi, q_hi, g, q_out)
                        store(lo, q_lo, g, q_out)
                        sp.wait_ge(q_out, 32 * (g + 1))
                        sp.sem_inc(hilo_free, 1)
                    if k == 7:
                        sp.wait_ge(kv_done, g + 1)
                        store(hi, k_hi, g, kv_out)
                        store(lo, k_lo, g, kv_out)
                        sp.dma_start(vd[:, tiles_of(g), :], vo[:, :, :, :].rearrange("p n h d -> p n (h d)")).then_inc(kv_out, 16)
                        sp.wait_ge(kv_out, 48 * (g + 1))
                        sp.sem_inc(hilo_free, 1)
                        sp.sem_inc(v_free, 1)
                        if g + 1 < NG:
                            sp.wait_ge(turned, g + 1)
                            load_attention(g + 1)
            store_x(NG - 1)

        @block.tensor
        def _(pe):
            for k in range(4):
                pe.sem_inc(m_free[k], 1)
                pe.sem_inc(t_out[k], 1)
            with pe.Fori(0, NG) as g:

                def turn(src, use):
                    for c in range(C):
                        pe.wait_ge(t_out[c], g * TU[c] + (use + 1))
                        for n in range(TT):
                            mm = pe.transpose(tb[c][:, n * P:(n + 1) * P], src[:, n, c * P:(c + 1) * P], ident[:, :])
                        mm.then_inc(t_full[c], 1)
                    for c in range(C):
                        pe.wait_ge(t_out[c], g * TU[c] + (use + 2))

                def chunk(k, weights_left):
                    pe.wait_ge(lo_split, g * KS + (k + 1))
                    wk = lambda c, r: (wh[k % 2][:, c, r], wl[k % 2][:, c, r])
                    xk = lambda c, r: (xh[:, c, r], xl[:, c, r])
                    left, right = (wk, xk) if weights_left else (xk, wk)
                    for o in range(4):
                        pe.wait_ge(m_free[o], g * MU + (row(k) + 1))
                        product(pe, m[o][:, :], lambda c: left(c, slice(o * P, (o + 1) * P)),
                                lambda c: right(c, slice(0, D)), C).then_inc(m_full[o], 1)

                pe.wait_ge(in_sem, 16 * g + 16)
                turn(ao, 0)
                chunk(0, False)
                pe.wait_ge(ln_done, g + 1)
                turn(ln, 1)
                pe.sem_inc(turned, 1)
                pe.wait_ge(w_in, 16 * 6)
                for n in range(TT):
                    for c in range(C):
                        mm = pe.matmul(tb[0][:, n * E0:(n + 1) * E0], xT[:, c, n * P:(n + 1) * P], w_g[:, c, :],
                                       start=(c == 0), stop=(c == C - 1))
                mm.then_inc(t_full[0], 1)
                chunk(1, True)
                chunk(2, True)
                pe.wait_ge(comb_done, g + 1)
                pe.wait_ge(t_out[1], g * TU[1] + 3)
                for n in range(TT):
                    mm = pe.transpose(tb[1][0:E0, n * P:(n + 1) * P], comb[:, n, :], ident[:, :])
                mm.then_inc(t_full[1], 1)
                chunk(3, False)
                pe.wait_ge(combT_done, g + 1)
                for o in range(4):
                    pe.wait_ge(m_free[o], g * MU + 5)
                    pe.matmul(m[o][:, :], combT[:, o * P:(o + 1) * P], b_e[:, :],
                              start=True, stop=True).then_inc(m_full[o], 1)
                for e in range(E0):
                    chunk(4 + e, False)

        def split_chunk(act, dve, n):
            if n < NG * KS:
                free = None
                if n >= 2:
                    g, k = divmod(n - 2, KS)
                    free = (m_full[3], g * MU + row(k) + 1)
                split(act, dve, raw[n % 2][:, :, :], wh[n % 2][:, :, :], wl[n % 2][:, :, :],
                      (raw_in[n % 2], 16 * (n // 2 + 1)), free, (hi_split, n + 1), lo_split)

        @block.scalar
        def _(act):
            if smp:
                smp.load_first(act)
            split_chunk(act, None, 0)
            act.wait_ge(w_in, 16 * 6)
            for g in range(NG):
                K0 = g * KS
                for use in range(2):
                    if use == 1 or g > 0:
                        act.wait_ge(m_full[3], g * MU + use)
                    for c in range(C):
                        act.wait_ge(t_full[c], g * TU[c] + (use + 1))
                        act.copy(xh[:, c, :], tb[c][:, :]).then_inc(xh_done, 1)
                        if use == 1:
                            act.copy(xT[:, c, :], tb[c][:, :]).then_inc(xh_done, 1)
                    split_chunk(act, None, K0 + use + 1)
                act.wait_ge(lg_done, g + 1)
                act.activation(ex[:, :, :], lg[:, :, :], ACT.Exp).then_inc(ex_done, 1)
                for k in range(2 * C):
                    if k % C == 0 and 2 * g + k // C > 0:
                        act.wait_ge(hilo_free, 2 * g + k // C)
                    act.wait_ge(m_full[k % 4], g * MU + (k // 4 + 2))
                    act.activation(hi[:, k % C, :], m[k % 4][:, :], ACT.Identity, bias=qk_c[:, k:k + 1]).then_inc(hi_done, 1)
                    if k % C == C - 1:
                        split_chunk(act, None, K0 + 3 + k // C)
                act.wait_ge(t_full[1], g * TU[1] + 3)
                act.copy(combT[:, :], tb[1][0:E0, :]).then_inc(combT_done, 1)
                act.wait_ge(combT_done, g + 1)
                act.sem_inc(t_out[1], 1)
                split_chunk(act, None, K0 + 5)
                for k in range(-1, E0):
                    if 0 <= k < E0 - 1:
                        split_chunk(act, None, K0 + 6 + k)
                    if smp and k in SAMPLE_AT:
                        smp.weights(act, *divmod(HALVES * g + SAMPLE_AT.index(k), 2))

        @block.vector
        def _(dve):
            steps = Steps(dve, dsem, 42)
            dve.memset(vo[:, :, :, HD:V1], 1.0).then_inc(preset, 1)
            dve.wait_ge(preset, 1)
            split_chunk(None, dve, 0)
            dve.wait_ge(w_in, 16 * 6)
            for g in range(NG):
                K0 = g * KS

                def sample(k):
                    if smp and k in SAMPLE_AT:
                        smp.scores(dve, *divmod(HALVES * g + SAMPLE_AT.index(k), 2))
                    if smp and k - 1 in SAMPLE_AT:
                        smp.output(dve, *divmod(HALVES * g + SAMPLE_AT.index(k - 1), 2))

                def low_parts(use):
                    for c in range(C):
                        dve.wait_ge(xh_done, g * 3 * C + ((c + 1) if use == 0 else C + 2 * (c + 1)))
                        dve.tensor_tensor(xl[:, c, :], tb[c][:, :], xh[:, c, :].bitcast(F32), ALU.subtract).then_inc(t_out[c], 1)

                steps.begin(g)
                low_parts(0)
                split_chunk(None, dve, K0 + 1)
                dve.wait_ge(x_in, 16 * g + 16)
                for n in range(TT):
                    steps.did(dve.tensor_tensor(acc[:, n, :], acc[:, n, :], rows[:, 0, :], ALU.add))
                steps.settle()
                for n in range(TT):
                    dve.wait_ge(m_full[n], g * MU + 1)
                    dve.tensor_tensor(acc[:, n, :], m[n][:, :], acc[:, n, :], ALU.add).then_inc(m_free[n], 1)
                for n in range(TT):
                    dve.wait_ge(m_free[n], g * MU + 2)
                layer_norm(steps, dve, None, acc, ln, stats, mv, rstd)
                dve.sem_inc(ln_done, 1)
                low_parts(1)
                split_chunk(None, dve, K0 + 2)
                dve.wait_ge(t_full[0], g * TU[0] + 3)
                gate = tb[0][:, 0:TT * E0].rearrange("p (n e) -> p n e", e=E0)
                steps.did(dve.tensor_tensor(lg[:, :, :], gate, bg_r[:, :].unsqueeze(1).to_broadcast([P, TT, E0]), ALU.add))
                steps.settle()
                dve.sem_inc(t_out[0], 1)
                steps.did(dve.tensor_reduce(red[:, :, :], lg[:, :, :], X, ALU.max))
                steps.settle()
                steps.did(dve.tensor_tensor(lg[:, :, :], lg[:, :, :], red[:, :, :].to_broadcast([P, TT, E0]), ALU.subtract))
                steps.settle()
                dve.sem_inc(lg_done, 1)
                dve.wait_ge(ex_done, g + 1)
                steps.did(dve.tensor_reduce(red[:, :, :], ex[:, :, :], X, ALU.add))
                steps.settle()
                steps.did(dve.reciprocal(red[:, :, :], red[:, :, :]))
                steps.settle()
                steps.did(dve.tensor_tensor(ex[:, :, :], ex[:, :, :], red[:, :, :].to_broadcast([P, TT, E0]), ALU.mult))
                steps.settle()
                top_two(steps, dve, ex[:, :, :], ahead[:, :, :], gt[:, :, :, :], eq[:, :, :, :], rank[:, :, :], sel[:, :, :])
                steps.did(dve.tensor_tensor(comb[:, :, :], ex[:, :, :], sel[:, :, :], ALU.mult))
                steps.settle()
                dve.sem_inc(comb_done, 1)
                for k in range(2 * C):
                    dve.wait_ge(m_full[k % 4], g * MU + (k // 4 + 2))
                    dve.wait_ge(hi_done, g * 2 * C + (k + 1))
                    dve.scalar_tensor_tensor(out=lo[:, k % C, :], in0=m[k % 4][:, :], scalar=qk_c[:, k:k + 1],
                                             in1=hi[:, k % C, :].bitcast(F32), op0=ALU.add,
                                             op1=ALU.subtract).then_inc(m_free[k % 4], 1)
                    if k == C - 1:
                        for o in range(4):
                            dve.wait_ge(m_free[o], g * MU + 3)
                        dve.sem_inc(q_done, 1)
                    if k % C == C - 1:
                        split_chunk(None, dve, K0 + 3 + k // C)
                if g > 0:
                    dve.wait_ge(v_free, g)
                for n in range(TT):
                    dve.wait_ge(m_full[n], g * MU + 4)
                    dve.tensor_tensor(vo[:, n, :, 0:HD], m[n][:, :].rearrange("p (h d) -> p h d", h=H),
                                      rows[:, 1, :].rearrange("p (h d) -> p h d", h=H), ALU.add).then_inc(m_free[n], 1)
                for n in range(TT):
                    dve.wait_ge(m_free[n], g * MU + 5)
                dve.sem_inc(kv_done, 1)
                for n in range(TT):
                    dve.wait_ge(m_full[n], g * MU + 5)
                    dve.tensor_tensor(acc[:, n, :], m[n][:, :], acc[:, n, :], ALU.add).then_inc(m_free[n], 1)
                split_chunk(None, dve, K0 + 5)
                sample(-1)
                for e in range(E0):
                    for n in range(TT):
                        dve.wait_ge(m_full[n], g * MU + (6 + e))
                        dve.wait_ge(m_free[n], g * MU + (6 + e))
                        dve.scalar_tensor_tensor(out=acc[:, n, :], in0=m[n][:, :], scalar=comb[:, n, e:e + 1],
                                                 in1=acc[:, n, :], op0=ALU.mult, op1=ALU.add).then_inc(m_free[n], 1)
                    if e < E0 - 1:
                        split_chunk(None, dve, K0 + 6 + e)
                    sample(e)
                for n in range(TT):
                    dve.wait_ge(m_free[n], g * MU + (MU + 1))
                dve.sem_inc(out_done, 1)
                steps.end()

        @block.gpsimd
        def _(pool):
            if smp:
                smp.gather(pool)


def sample_positions(nc, x_part, attn, mask, wqT, bq, woffT, boff, ident, x2, qp_dram, idx_dram, wt_dram, batch):
    F = TT * NS
    NG = S // G
    A = NG * F
    G0 = batch * NG
    with ExitStack() as ctx:
        t = Tools(nc, ctx, f"pos{batch}")
        w_q, w_off = t.sb("w_q", [P, C, D]), t.sb("w_off", [P, C, NS])
        bq_r, boff_r = t.sb("bq_r", [P, D]), t.sb("boff_r", [P, NS])
        mk = t.sb("mk", [P, T], I32)
        mkf = t.sb("mkf", [P, T])
        length, neg_length, inv_length = (t.sb(n, [P, 1]) for n in ("length", "neg_length", "inv_length"))
        pos_i, head_i = t.sb("pos_i", [P, NG, F], I32), t.sb("head_i", [P, A], I32)
        pos, head = t.sb("pos", [P, A]), t.sb("head", [P, A])
        xas, xbs = ([t.sb(f"{n}{g}", [P, TT, D]) for g in range(NG)] for n in ("xa", "xb"))
        lns, xT, qps = [t.sb(f"ln{g}", [P, TT, D]) for g in range(NG)], t.sb("xT", [P, C, G]), [t.sb(f"qp{g}", [P, TT, D]) for g in range(NG)]
        stats, mv, rstd = t.sb("stats", [P, TT, 6]), t.sb("mv", [P, TT, 2]), t.sb("rstd", [P, 4, TT])
        at, whole, frac, flag = (t.sb(n, [P, A]) for n in ("at", "whole", "frac", "flag"))
        whole_i = t.sb("whole_i", [P, A], I32)
        wt = t.sb("wt", [P, A, 2])
        idx = t.sb("idx", [P, A], I32)
        tb = [t.ps(f"tb{i}", [P, G]) for i in range(4)]
        m = [t.ps(f"m{i}", [P, G]) for i in range(4)]
        w_in, x_in, made = t.sem("w_in"), t.sems("x_in", NG), t.sem("made")
        mask_in, dsem, bsem = t.sem("mask_in"), t.sem("dve_steps"), t.sem("batch_steps")
        t_full, t_out = t.sems("t_full", 4), t.sems("t_out", 4)
        m_full, m_free = t.sems("m_full", 4), t.sems("m_free", 4)
        ln_done, qp_done, x2_done, idx_done, xT_free, stored = (
            t.sem(n) for n in ("ln_done", "qp_done", "x2_done", "idx_done", "xT_free", "stored"))
        TU = [3, 2, 2, 2]
        passed = t.sems("passed", 4)
        block = t.block()

        @block.sync
        def _(sp):
            xs = x_part.rearrange("(n p) d -> p n d", p=P)
            as_ = attn.rearrange("(n p) d -> p n d", p=P)

            def load(g):
                n = (G0 + g) * TT
                sp.dma_start(xas[g][:, :, :], xs[:, n:n + TT, :]).then_inc(x_in[g], 16)
                sp.dma_start(xbs[g][:, :, :], as_[:, n:n + TT, :]).then_inc(x_in[g], 16)

            sp.dma_start(mk[:, :], mask[batch:batch + 1, :].partition_broadcast(P).rearrange("p a t -> p (a t)")).then_inc(mask_in, 16)
            load(0)
            sp.dma_start(w_q[:, :, :], wqT.rearrange("(c p) n -> p c n", p=P)).then_inc(w_in, 16)
            sp.dma_start(w_off[:, :, :], woffT.rearrange("(c p) n -> p c n", p=P)).then_inc(w_in, 16)
            sp.dma_start(bq_r[:, :], row_of(bq, D)).then_inc(w_in, 16)
            sp.dma_start(boff_r[:, :], row_of(boff, NS)).then_inc(w_in, 16)
            for g in range(1, NG):
                load(g)

        @block.gpsimd
        def _(pool):
            for g in range(NG):
                pool.iota(pos_i[:, g, :], [[P, TT], [0, H], [1, NK5]], base=g * G + (-NK5 // 2),
                          channel_multiplier=1).then_inc(made, 1)
            pool.iota(head_i[:, :], [[0, NG * TT], [1, H], [0, NK5]], base=0, channel_multiplier=0).then_inc(made, 1)
            xd = x2.rearrange("(n p) d -> p n d", p=P)
            qd = qp_dram.rearrange("(n p) d -> p n d", p=P)
            idd = idx_dram.rearrange("(n p) d -> p n d", p=P)
            wd = wt_dram.rearrange("(n p) d -> p n d", p=P)
            for g in range(NG):
                n = (G0 + g) * TT
                pool.wait_ge(x2_done, g + 1)
                pool.dma_start(xd[:, n:n + TT, :], xas[g][:, :, :]).then_inc(stored, 16)
                pool.wait_ge(qp_done, g + 1)
                pool.dma_start(qd[:, n:n + TT, :], qps[g][:, :, :]).then_inc(stored, 16)
            n, N = G0 * TT, NG * TT
            pool.wait_ge(idx_done, 1)
            pool.dma_start(idd[:, n:n + N, :], idx[:, :].rearrange("p (n s) -> p n s", n=N)).then_inc(stored, 16)
            pool.dma_start(wd[:, n:n + N, :], wt[:, :, :].rearrange("p (n s) a -> p n (s a)", n=N)).then_inc(stored, 16)
            pool.wait_ge(stored, 16 * (2 * NG + 2))

        @block.tensor
        def _(pe):
            for k in range(4):
                pe.sem_inc(m_free[k], 1)
                pe.sem_inc(t_out[k], 1)
            pe.wait_ge(ln_done, 1)
            pe.wait_ge(w_in, 64)
            for g in range(NG):
                ln, qp = lns[g], qps[g]

                def turn(src, use):
                    for c in range(C):
                        pe.wait_ge(t_out[c], g * TU[c] + (use + 1))
                        for n in range(TT):
                            mm = pe.transpose(tb[c][:, n * P:(n + 1) * P], src[:, n, c * P:(c + 1) * P], ident[:, :])
                        mm.then_inc(t_full[c], 1)
                    for c in range(C):
                        pe.wait_ge(t_out[c], g * TU[c] + (use + 2))

                pe.wait_ge(ln_done, g + 1)
                turn(ln, 0)
                for n in range(TT):
                    pe.wait_ge(m_free[n], g + 1)
                    for c in range(C):
                        mm = pe.matmul(m[n][:, :], xT[:, c, n * P:(n + 1) * P], w_q[:, c, :], start=(c == 0), stop=(c == C - 1))
                    mm.then_inc(m_full[n], 1)
                pe.wait_ge(qp_done, g + 1)
                turn(qp, 1)
                for n in range(TT):
                    for c in range(C):
                        mm = pe.matmul(tb[0][:, n * NS:(n + 1) * NS], xT[:, c, n * P:(n + 1) * P], w_off[:, c, :],
                                       start=(c == 0), stop=(c == C - 1))
                mm.then_inc(t_full[0], 1)

        @block.scalar
        def _(act):
            act.sem_inc(xT_free, 1)
            with act.Fori(0, NG) as g:
                act.wait_ge(xT_free, g + 1)
                for use in range(2):
                    if use == 1:
                        act.wait_ge(m_full[3], g + 1)
                    for c in range(C):
                        act.wait_ge(t_full[c], g * TU[c] + (use + 1))
                        act.copy(xT[:, c, :], tb[c][:, :]).then_inc(t_out[c], 1)

        @block.vector
        def _(dve):
            per_batch = Steps(dve, bsem, 5)
            steps = Steps(dve, dsem, 84)
            steps.begin(0)
            go = lambda ins: (steps.did(ins), steps.settle())
            for g in range(NG):
                xa, xb = xas[g], xbs[g]
                dve.wait_ge(x_in[g], 32)
                for n in range(TT):
                    steps.did(dve.tensor_tensor(xa[:, n, :], xa[:, n, :], xb[:, n, :], ALU.add))
                steps.settle()
                dve.sem_inc(x2_done, 1)
                layer_norm(steps, dve, passed[3], xa, lns[g], stats, mv, rstd)
                dve.sem_inc(ln_done, 1)
            dve.wait_ge(made, NG + 1)
            dve.tensor_copy(pos[:, :], pos_i[:, :, :].rearrange("p g f -> p (g f)")).then_inc(made, 1)
            dve.tensor_scalar(head[:, :], head_i[:, :], float(ROWS * PAIR), float(2 * PAIR), ALU.mult,
                              ALU.add).then_inc(made, 1)
            dve.wait_ge(made, NG + 3)
            per_batch.begin(0)
            dve.wait_ge(mask_in, 16)
            per_batch.did(dve.tensor_copy(mkf[:, :], mk[:, :]))
            per_batch.settle()
            per_batch.did(dve.tensor_reduce(length[:, :], mkf[:, :], X, ALU.add))
            per_batch.settle()
            per_batch.did(dve.tensor_scalar(neg_length[:, :], length[:, :], float(T - 1), None, ALU.subtract))
            per_batch.settle()
            per_batch.did(dve.tensor_scalar(length[:, :], neg_length[:, :], -1.0, None, ALU.mult))
            per_batch.settle()
            per_batch.did(dve.reciprocal(inv_length[:, :], length[:, :]))
            per_batch.settle()
            per_batch.end()
            dve.wait_ge(w_in, 64)
            for g in range(NG):
                qp = qps[g]
                for n in range(TT):
                    dve.wait_ge(m_full[n], g + 1)
                    dve.tensor_tensor(qp[:, n, :], m[n][:, :], bq_r[:, :], ALU.add).then_inc(m_free[n], 1)
                for n in range(TT):
                    dve.wait_ge(m_free[n], g + 2)
                dve.sem_inc(qp_done, 1)
                dve.wait_ge(t_full[0], g * TU[0] + 3)
                go(dve.tensor_tensor(at[:, g * F:(g + 1) * F].rearrange("p (n s) -> p n s", n=TT),
                                     tb[0][:, 0:F].rearrange("p (n s) -> p n s", n=TT),
                                     boff_r[:, :].unsqueeze(1).to_broadcast([P, TT, NS]), ALU.add))
                dve.sem_inc(t_out[0], 1)
                dve.sem_inc(xT_free, 1)
            go(dve.tensor_tensor(at[:, :], at[:, :], pos[:, :], ALU.add))

            def floor(src, dst):
                go(dve.tensor_copy(whole_i[:, :], src))
                go(dve.tensor_copy(dst, whole_i[:, :]))
                go(dve.tensor_tensor(flag[:, :], dst, src, ALU.is_gt))
                go(dve.tensor_tensor(dst, dst, flag[:, :], ALU.subtract))

            go(dve.tensor_scalar(frac[:, :], at[:, :], inv_length[:, 0:1], None, ALU.mult))
            floor(frac[:, :], whole[:, :])
            go(dve.scalar_tensor_tensor(out=at[:, :], in0=whole[:, :], scalar=neg_length[:, 0:1], in1=at[:, :],
                                        op0=ALU.mult, op1=ALU.add))
            go(dve.tensor_scalar(flag[:, :], at[:, :], inv_length[:, 0:1], 1.0, ALU.mult, ALU.is_ge))
            go(dve.scalar_tensor_tensor(out=at[:, :], in0=flag[:, :], scalar=neg_length[:, 0:1], in1=at[:, :],
                                        op0=ALU.mult, op1=ALU.add))
            go(dve.tensor_scalar(flag[:, :], at[:, :], inv_length[:, 0:1], 0.0, ALU.mult, ALU.is_lt))
            go(dve.scalar_tensor_tensor(out=at[:, :], in0=flag[:, :], scalar=length[:, 0:1], in1=at[:, :],
                                        op0=ALU.mult, op1=ALU.add))
            go(dve.tensor_scalar(at[:, :], at[:, :], 1.0 / (T - 1), 2.0, ALU.mult, ALU.mult))
            go(dve.tensor_scalar(at[:, :], at[:, :], -1.0, 1.0, ALU.add, ALU.add))
            go(dve.tensor_scalar(at[:, :], at[:, :], float(T), -1.0, ALU.mult, ALU.add))
            go(dve.tensor_scalar(at[:, :], at[:, :], 0.5, None, ALU.mult))
            floor(at[:, :], whole[:, :])
            go(dve.tensor_tensor(frac[:, :], at[:, :], whole[:, :], ALU.subtract))
            steps.did(dve.tensor_scalar(wt[:, :, 0], frac[:, :], -0.5, 0.5, ALU.mult, ALU.add))
            steps.did(dve.tensor_scalar(wt[:, :, 1], frac[:, :], 0.5, None, ALU.mult))
            go(dve.tensor_scalar(whole[:, :], whole[:, :], -2.0, float(T), ALU.max, ALU.min))
            go(dve.scalar_tensor_tensor(out=idx[:, :], in0=whole[:, :], scalar=float(PAIR), in1=head[:, :],
                                        op0=ALU.mult, op1=ALU.add))
            dve.sem_inc(idx_done, 1)
            steps.end()


def ffn_last(nc, x2, cx, woT, bo, w_enc, b_enc, w_s2c, b_s2c, wr, br, w1, b1, w2, b2, w_c2s, b_c2s,
             w_dec, b_dec, ln_g, ln_b, ident, ahead, out, samples):
    NG = B * S // G
    TILES = [3, 3, 2, 0]
    PLACES = {3: [[0], [1], [2], [3], [4], [5]], 2: [[0], [], [1], [], [2, 3], []], 0: [[]] * 6}
    HC = HID // P
    with ExitStack() as ctx:
        t = Tools(nc, ctx, "out")
        wo_s, we_s = t.sb("wo", [P, C, D]), t.sb("we", [P, C, HID])
        ws_s, wr_s = t.sb("ws", [P, HC, MM]), t.sb("wr", [MM, E1])
        w1_s, w2_s = t.sb("w1", [P, E1, EH], F32R), t.sb("w2", [P, E1, EH // P, MM])
        wc_s, wd_s = t.sb("wc", [P, HID], F32R), t.sb("wd", [P, HC, D])
        be_c, bs_c, b1_c, bc_c = t.sb("be", [P, HC]), t.sb("bs", [P, 1]), t.sb("b1", [P, E1, EH // P]), t.sb("bc", [P, HC])
        rows = t.sb("rows", [P, 5, D])
        br_r = t.sb("br_r", [P, E1])
        ca, acc, ln = t.sb("ca", [P, TT, D]), t.sb("acc", [P, TT, D]), t.sb("ln", [P, TT, D])
        xT, hT = t.sb("xT", [P, C, G]), t.sb("hT", [P, HC, G])
        contT = t.sb("contT", [MM, G])
        assert 2 * MM == P
        s_hi, s_lo = t.sb("s_hi", [P, G], F32R), t.sb("s_lo", [MM, G], F32R)
        he = [t.sb(f"he{i}", [P, EH // P, G]) for i in range(2)]
        y = ln[:, :, :].rearrange("p n (e d) -> p n e d", e=E1)
        eo = t.sb("eo", [P, TT, 2, MM])
        stats, mv, rstd = t.sb("stats", [P, TT, 6]), t.sb("mv", [P, TT, 2]), t.sb("rstd", [P, 4, TT])
        lg, ex, sel, rank = (t.sb(n, [P, TT, E1]) for n in ("lg", "ex", "sel", "rank"))
        gt, eq = (t.sb(n, [P, TT, E1, E1]) for n in ("gt", "eq"))
        red = t.sb("red", [P, TT, 1])
        tb = [t.ps(f"tb{i}", [P, G]) for i in range(4)]
        m = [t.ps(f"m{i}", [P, G]) for i in range(4)]
        wo_in, w_in, both_in, w_hi, w_lo, s_split, ca_in, acc_in, ca_used = (t.sem(n) for n in ("wo_in", "w_in", "both_in", "w_hi", "w_lo", "s_split", "ca_in", "acc_in", "ca_used"))
        t_full, t_out = t.sems("t_full", 4), t.sems("t_out", 4)
        m_full, m_free = t.sems("m_full", 4), t.sems("m_free", 4)
        dsem, ln_done, lg_done, ex_done, eo_done, out_done, stored, he_used, cont_done, eo_hi = (
            t.sem(n) for n in ("dve_steps", "ln_done", "lg_done", "ex_done", "eo_done", "out_done", "stored", "he_used", "cont_done", "eo_hi"))
        TU = [4, 4, 4, 3]
        MU = 1 + 2 + E1 + 2 + 1
        NW = 18
        passed = t.sems("passed", 4)
        smp = Samples(t, *samples)
        assert EH == G
        staged = [he[0][:, :, :], he[1][:, :, :], hT[:, 0:HID // G, :].rearrange("p a n -> p (a n)")]
        parts = [w1_s[:, 0:4, :], w1_s[:, 4:8, :], wc_s[:, :]]
        block = t.block()

        @block.sync
        def _(sp):
            xs = x2.rearrange("(n p) d -> p n d", p=P)
            cs = cx.rearrange("(n p) d -> p n d", p=P)
            od = out.rearrange("(n p) d -> p n d", p=P)

            def load_ca(g):
                for n in range(TT):
                    if g >= NG // B:
                        for u in range(2):
                            sp.wait_ge(smp.stored[u], 16 * (TT * (g - NG // B) + n + 1))
                    sp.dma_start(ca[:, n, :], cs[:, g * TT + n, :]).then_inc(ca_in, 16)

            load_ca(0)
            loads = [(wo_s[:, :, :], woT.rearrange("(c p) n -> p c n", p=P)), (rows[:, 0, :], row_of(bo, D)),
                     (we_s[:, :, :], w_enc.rearrange("(c p) n -> p c n", p=P)),
                     (ws_s[:, :, :], w_s2c.rearrange("(c p) n -> p c n", p=P)), (wr_s[:, :], wr),
                     (w2_s[:, :, :, :], w2.rearrange("e (k p) m -> p e k m", p=P)),
                     (wd_s[:, :, :], w_dec.rearrange("(c p) n -> p c n", p=P)),
                     (be_c[:, :], b_enc.rearrange("(c p) -> p c", p=P)), *((bs_c[r:r + MM, :], b_s2c.rearrange("(m a) -> m a", a=1)) for r in (0, MM)),
                     (b1_c[:, :, :], b1.rearrange("e (k p) -> p e k", p=P)), (bc_c[:, :], b_c2s.rearrange("(c p) -> p c", p=P)),
                     (rows[:, 1, :], row_of(b_dec, D)), (rows[:, 2, :], row_of(ln_g, D)),
                     (rows[:, 3, :], row_of(ln_b, D)), (rows[:, 4, :], row_of(b2, D)), (br_r[:, :], row_of(br, E1))]
            assert len(loads) == NW - 1
            for i, (dst, src) in enumerate(loads):
                sp.dma_start(dst, src, allow_slow_non_contiguous=True).then_inc(wo_in if i < 2 else w_in, 16)
                if i == 1:
                    sp.dma_start(acc[:, :, :], xs[:, 0:TT, :]).then_inc(acc_in, 16)
                    for r in (0, MM):
                        for dst, src in zip(staged, (w1[0:4].rearrange("e m h -> m e h"), w1[4:8].rearrange("e m h -> m e h"),
                                                     w_c2s)):
                            sp.dma_start(dst[r:r + MM], src).then_inc(both_in, 16)

            for g in range(NG):
                if g > 0:
                    sp.dma_start(acc[:, :, :], xs[:, g * TT:(g + 1) * TT, :]).then_inc(acc_in, 16)
                if g + 1 < NG:
                    sp.wait_ge(ca_used, g + 1)
                    load_ca(g + 1)
                sp.wait_ge(out_done, g + 1)
                sp.dma_start(od[:, g * TT:(g + 1) * TT, :], acc[:, :, :]).then_inc(stored, 16)
                sp.wait_ge(stored, 16 * (g + 1))

        @block.tensor
        def _(pe):
            for k in range(4):
                pe.sem_inc(m_free[k], 1)
                pe.sem_inc(t_out[k], 1)
            pe.wait_ge(wo_in, 32)
            with pe.Fori(0, NG) as g:

                def turn(src, use):
                    for c in range(C):
                        pe.wait_ge(t_out[c], g * TU[c] + (use + 1))
                        for n in range(TT):
                            mm = pe.transpose(tb[c][:, n * P:(n + 1) * P], src[:, n, c * P:(c + 1) * P], ident[:, :])
                        mm.then_inc(t_full[c], 1)
                    for c in range(C):
                        pe.wait_ge(t_out[c], g * TU[c] + (use + 2))

                def tile(row, o, n, left, right):
                    pe.wait_ge(m_free[o], g * MU + (row + 1))
                    for c in range(n):
                        mm = pe.matmul(m[o][:, :], left(c), right(c), start=(c == 0), stop=(c == n - 1))
                    mm.then_inc(m_full[o], 1)

                def narrow(row, o, w):
                    pe.wait_ge(m_free[o], g * MU + (row + 1))
                    pe.matmul(m[o][:, :], w, s_hi[:, :], start=True, stop=False)
                    pe.matmul(m[o][:, :], w[0:MM, :], s_lo[:, :], start=False, stop=True).then_inc(m_full[o], 1)

                def y_of(e):
                    for k in range(4):
                        pe.wait_ge(m_free[k], g * MU + (3 + e + 2))
                    for n in range(TT):
                        if e == 0:
                            pe.wait_ge(t_out[n], g * TU[n] + [4, 4, 3, 3][n])
                        for k in range(EH // P):
                            mm = pe.matmul(tb[n][:, e * MM:(e + 1) * MM], he[e % 2][:, k, n * P:(n + 1) * P],
                                           w2_s[:, e, k, :], start=(k == 0), stop=(k == EH // P - 1))
                        if e == E1 - 1:
                            mm.then_inc(t_full[n], 1)
                    if e < E1 - 1:
                        mm.then_inc(he_used, 1)

                pe.wait_ge(ca_in, 16 * TT * g + 16 * TT)
                turn(ca, 0)
                pe.sem_inc(ca_used, 1)
                for o in range(4):
                    tile(0, o, C, lambda c: xT[:, c, o * P:(o + 1) * P], lambda c: wo_s[:, c, :])
                pe.wait_ge(ln_done, g + 1)
                turn(ln, 1)
                pe.wait_ge(w_lo, len(parts))
                pe.wait_ge(w_in, 16 * (NW - 3))
                for r in range(2):
                    for o in range(4):
                        k = (4 * r + o) * P
                        tile(1 + r, o, C, lambda c: we_s[:, c, k:k + P], lambda c: xT[:, c, :])
                for o in range(4):
                    pe.wait_ge(m_free[o], g * MU + 4)
                for k in range(HC):
                    for r in (0, MM):
                        mm = pe.matmul(tb[1][r:r + MM, :], ws_s[:, k, :], hT[:, k, :], start=(k == 0), stop=(k == HC - 1),
                                       skip_group_check=True)
                mm.then_inc(t_full[1], 1)
                pe.wait_ge(t_out[1], g * TU[1] + 4)
                for n in range(TT):
                    mm = pe.matmul(tb[0][:, n * E1:(n + 1) * E1], contT[:, n * P:(n + 1) * P], wr_s[:, :], start=True, stop=True)
                mm.then_inc(t_full[0], 1)
                pe.wait_ge(s_split, 2 * g + 1)
                for e in range(E1):
                    for o in range(4):
                        narrow(3 + e, o, w1_s[:, e, o * P:(o + 1) * P])
                    if e > 0:
                        y_of(e - 1)
                y_of(E1 - 1)
                pe.wait_ge(eo_done, g + 1)
                pe.wait_ge(t_out[2], g * TU[2] + 4)
                pe.sem_inc(passed[2], 1)
                for n in range(TT):
                    mm = pe.transpose(tb[2][:, n * P:(n + 1) * P], eo[:, n, :, :].rearrange("p a m -> p (a m)"), ident[:, :])
                mm.then_inc(t_full[2], 1)
                pe.wait_ge(s_split, 2 * g + 2)
                for r in range(2):
                    for o in range(4):
                        k = (4 * r + o) * P
                        narrow(3 + E1 + r, o, wc_s[:, k:k + P])
                for o in range(4):
                    pe.wait_ge(m_free[o], g * MU + (6 + E1))
                for o in range(4):
                    tile(5 + E1, o, HC, lambda c: hT[:, c, o * P:(o + 1) * P], lambda c: wd_s[:, c, :])

        @block.scalar
        def _(act):
            def turned(g, use):
                for c in range(C):
                    act.wait_ge(t_full[c], g * TU[c] + (use + 1))
                    act.copy(xT[:, c, :], tb[c][:, :]).then_inc(t_out[c], 1)

            smp.load_first(act)
            turned(0, 0)
            act.wait_ge(both_in, 16 * 2 * len(parts))
            for src, dst in zip(staged, parts):
                act.copy(dst, src).then_inc(w_hi, 1)

            def group(g, before, tiles):

                def sample(place):
                    for k in PLACES[tiles][place]:
                        smp.weights(act, before + k // 2, k % 2)

                def evac(row, o, dst, func, bias):
                    act.wait_ge(m_full[o], g * MU + (row + 1))
                    act.activation(dst, m[o][:, :], func, bias=bias).then_inc(m_free[o], 1)

                act.wait_ge(m_full[3], g * MU + 1)
                turned(g, 1)
                act.wait_ge(w_in, 16 * (NW - 3))
                act.wait_ge(w_lo, len(parts))
                for r in range(2):
                    for o in range(4):
                        k = 4 * r + o
                        evac(1 + r, o, hT[:, k, :], ACT.Sigmoid, be_c[:, k:k + 1])
                    if r == 0:
                        sample(0)
                act.wait_ge(t_full[1], g * TU[1] + 3)
                act.activation(contT[:, :], tb[1][0:MM, :], ACT.Identity, bias=bs_c[0:MM, 0:1]).then_inc(cont_done, 1)
                act.activation(s_hi[:, :], tb[1][:, :], ACT.Identity, bias=bs_c[:, 0:1]).then_inc(t_out[1], 1)
                for e in range(E1):
                    if e >= 2:
                        act.wait_ge(he_used, g * (E1 - 1) + (e - 1))
                    for o in range(4):
                        evac(3 + e, o, he[e % 2][:, o, :], ACT.Relu, b1_c[:, e, o:o + 1])
                    if e == 0:
                        act.wait_ge(lg_done, g + 1)
                        act.activation(ex[:, :, :], lg[:, :, :], ACT.Exp).then_inc(ex_done, 1)
                    if e in (1, 3, 6):
                        sample((1, 3, 6).index(e) + 1)
                act.wait_ge(t_full[2], g * TU[2] + 4)
                act.copy(s_hi[:, :], tb[2][:, :]).then_inc(eo_hi, 1)
                for r in range(2):
                    for o in range(4):
                        k = 4 * r + o
                        evac(3 + E1 + r, o, hT[:, k, :], ACT.Sigmoid, bc_c[:, k:k + 1])
                sample(4)
                sample(5)
                if not (isinstance(g, int) and g == NG - 1):
                    turned(g + 1, 0)

            with act.Fori(0, 2) as g:
                group(g, TILES[0] * g, TILES[0])
            for g in range(2, NG):
                group(g, sum(TILES[:g]), TILES[g])

        @block.vector
        def _(dve):
            steps = Steps(dve, dsem, 88)
            for i, (src, dst) in enumerate(zip(staged, parts)):
                dve.wait_ge(w_hi, i + 1)
                dve.tensor_tensor(dst[MM:P], src[MM:P], dst[MM:P].bitcast(F32), ALU.subtract).then_inc(w_lo, 1)
            dve.wait_ge(wo_in, 32)

            def group(g, before, tiles):
                def sample(place):
                    for k in PLACES[tiles][place]:
                        smp.scores(dve, before + k // 2, k % 2)
                        smp.output(dve, before + k // 2, k % 2)

                steps.begin(g)
                go = lambda ins: (steps.did(ins), steps.settle())
                dve.wait_ge(acc_in, 16 * g + 16)
                for n in range(TT):
                    steps.did(dve.tensor_tensor(acc[:, n, :], acc[:, n, :], rows[:, 0, :], ALU.add))
                steps.settle()
                for n in range(TT):
                    dve.wait_ge(m_full[n], g * MU + 1)
                    dve.tensor_tensor(acc[:, n, :], m[n][:, :], acc[:, n, :], ALU.add).then_inc(m_free[n], 1)
                for n in range(TT):
                    dve.wait_ge(m_free[n], g * MU + 2)
                layer_norm(steps, dve, passed[3], acc, ln, stats, mv, rstd)
                dve.sem_inc(ln_done, 1)
                sample(0)
                dve.wait_ge(w_in, 16 * (NW - 3))
                for n in range(TT):
                    steps.did(dve.tensor_tensor(acc[:, n, :], acc[:, n, :], rows[:, 3, :], ALU.add))
                steps.settle()
                dve.wait_ge(cont_done, g + 1)
                dve.wait_ge(t_out[1], g * TU[1] + 4)
                dve.tensor_tensor(s_lo[:, :], contT[:, :], s_hi[0:MM, :].bitcast(F32), ALU.subtract).then_inc(s_split, 1)
                dve.wait_ge(t_full[0], g * TU[0] + 3)
                logits = tb[0][:, 0:TT * E1].rearrange("p (n e) -> p n e", e=E1)
                go(dve.tensor_tensor(lg[:, :, :], logits, br_r[:, :].unsqueeze(1).to_broadcast([P, TT, E1]), ALU.add))
                dve.sem_inc(t_out[0], 1)
                go(dve.tensor_reduce(red[:, :, :], lg[:, :, :], X, ALU.max))
                go(dve.tensor_tensor(lg[:, :, :], lg[:, :, :], red[:, :, :].to_broadcast([P, TT, E1]), ALU.subtract))
                dve.sem_inc(lg_done, 1)
                dve.wait_ge(ex_done, g + 1)
                go(dve.tensor_reduce(red[:, :, :], ex[:, :, :], X, ALU.add))
                go(dve.reciprocal(red[:, :, :], red[:, :, :]))
                go(dve.tensor_tensor(ex[:, :, :], ex[:, :, :], red[:, :, :].to_broadcast([P, TT, E1]), ALU.mult))
                top_two(steps, dve, ex[:, :, :], ahead[:, :, :], gt[:, :, :, :], eq[:, :, :, :], rank[:, :, :], sel[:, :, :])
                go(dve.tensor_tensor(ex[:, :, :], ex[:, :, :], sel[:, :, :], ALU.mult))
                go(dve.tensor_reduce(red[:, :, :], ex[:, :, :], X, ALU.add))
                go(dve.reciprocal(red[:, :, :], red[:, :, :]))
                go(dve.tensor_tensor(ex[:, :, :], ex[:, :, :], red[:, :, :].to_broadcast([P, TT, E1]), ALU.mult))
                sample(1)
                sample(2)
                sample(3)
                for n in range(TT):
                    dve.wait_ge(t_full[n], g * TU[n] + [4, 4, 3, 3][n])
                    dve.tensor_tensor(y[:, n, :, :].rearrange("p e d -> p (e d)"), tb[n][:, :], rows[:, 4, :],
                                      ALU.add).then_inc(t_out[n], 1)
                for n in range(TT):
                    dve.wait_ge(t_out[n], g * TU[n] + [5, 5, 4, 4][n])
                    steps.did(dve.tensor_tensor(y[:, n, :, :], y[:, n, :, :],
                                                ex[:, n, :].unsqueeze(2).to_broadcast([P, E1, MM]), ALU.mult))
                steps.settle()
                for n in range(TT):
                    steps.did(dve.tensor_reduce(eo[:, n, 0, :], y[:, n, :, :].rearrange("p e d -> p d e"), X, ALU.add))
                steps.settle()
                go(dve.tensor_copy(eo[:, :, 1, :], eo[:, :, 0, :]))
                dve.sem_inc(eo_done, 1)
                dve.wait_ge(eo_hi, g + 1)
                go(dve.tensor_tensor(s_lo[:, :], tb[2][0:MM, :], s_hi[0:MM, :].bitcast(F32), ALU.subtract))
                dve.sem_inc(s_split, 1)
                dve.sem_inc(t_out[2], 1)
                sample(4)
                for n in range(TT):
                    dve.wait_ge(m_full[n], g * MU + MU)
                    dve.tensor_tensor(ln[:, n, :], m[n][:, :], rows[:, 1, :], ALU.add).then_inc(m_free[n], 1)
                for n in range(TT):
                    dve.wait_ge(m_free[n], g * MU + (MU + 1))
                layer_norm(steps, dve, passed[3], ln, None, stats, mv, rstd)
                for n in range(TT):
                    steps.did(dve.scalar_tensor_tensor(out=ln[:, n, :], in0=ln[:, n, :], scalar=mv[:, n, 0:1],
                                                       in1=rows[:, 2, :], op0=ALU.subtract, op1=ALU.mult))
                steps.settle()
                for n in range(TT):
                    steps.did(dve.scalar_tensor_tensor(out=acc[:, n, :], in0=ln[:, n, :], scalar=rstd[:, 2, n:n + 1],
                                                       in1=acc[:, n, :], op0=ALU.mult, op1=ALU.add))
                steps.settle()
                dve.sem_inc(out_done, 1)
                steps.end()
                sample(5)

            with dve.Fori(0, 2) as g:
                group(g, TILES[0] * g, TILES[0])
            for g in range(2, NG):
                group(g, sum(TILES[:g]), TILES[g])

        @block.gpsimd
        def _(pool):
            smp.gather(pool)


def program(nc, a, out):
    scratch = lambda name, shape, dt=F32: nc.dram_tensor(name, shape, dt).ap()
    k0h, k0l = (scratch(f"k0_{n}", [B * T // G * D, G], F32R) for n in ("hi", "lo"))
    q0h, q0l, q1h, q1l, k1h, k1l = (scratch(n, [B * S // G * D, G], F32R)
                                    for n in ("q0_hi", "q0_lo", "q1_hi", "q1_lo", "k1_hi", "k1_lo"))
    v0, v1 = scratch("v0", [B * T, H * V1]), scratch("v1", [B * S, H * V1])
    tables = [scratch(f"table{b}", [H * ROWS * PAIR]) for b in range(B)]
    att0, att1, x_part, x2, qp, cx = (scratch(n, [B * S, D]) for n in ("att0", "att1", "x_part", "x2", "qp", "cx"))
    idx, wt = scratch("idx", [B * S, NS], I32), scratch("wt", [B * S, NS * 2])
    with ExitStack() as ctx:
        ident = ctx.enter_context(nc.sbuf_tensor("ident", [P, P], F32))
        identb = ctx.enter_context(nc.sbuf_tensor("identb", [P, P], BF16))
        ahead = ctx.enter_context(nc.sbuf_tensor("ahead", [P, E0, E0], F32))
        x = a["x"].rearrange("b s d -> (b s) d")
        constants(nc, ident, identb, ahead)
        project_context(nc, a["ctxT"], a["L0_xattn_WkT"], a["L0_xattn_bk"], a["L0_xattn_WvT"], a["L0_xattn_bv"],
                        a["L1_xattn_WkT"], a["L1_xattn_bk"], a["L1_xattn_WvT"], a["L1_xattn_bv"], k0h, k0l, v0, tables)
        project_query(nc, x, a["L0_xattn_WqT"], a["L0_xattn_bq"], ident, q0h, q0l)
        NT = S // P
        for b in range(B):
            along = lambda batch, first, tiles: (tables[batch], qp, idx, wt, cx, batch * NT + first, tiles)
            cross_along, moe_along, self_along = ((along(b - 1, 0, 4), along(b - 1, 4, 3), along(b - 1, 7, 1))
                                                  if b > 0 else (None, None, None))
            attention(nc, f"cross{b}", T, q0h, q0l, k0h, k0l, v0, ident, identb, att0, [b], cross_along)
            ffn_moe(nc, x, att0, a["L0_xattn_WoT"], a["L0_xattn_bo"], a["L0_ffn_W_qkv"], a["L0_ffn_b_qkv"],
                    a["L0_ffn_W_gate"], a["L0_ffn_b_gate"], a["L0_ffn_W_experts"], a["L0_ffn_b_experts"], ident, ahead,
                    q1h, q1l, k1h, k1l, v1, x_part, b, moe_along)
            attention(nc, f"self{b}", S, q1h, q1l, k1h, k1l, v1, ident, identb, att1, [b], self_along)
            sample_positions(nc, x_part, att1, a["mask_BxS2_if0"], a["L1_xattn_WqT"], a["L1_xattn_bq"],
                             a["L1_xattn_WoffT"], a["L1_xattn_boff"], ident, x2, qp, idx, wt, b)
        ffn_last(nc, x2, cx, a["L1_xattn_WoT"], a["L1_xattn_bo"], a["L1_ffn_W_enc"], a["L1_ffn_b_enc"],
                 a["L1_ffn_W_s2c"], a["L1_ffn_b_s2c"], a["L1_ffn_Wr"], a["L1_ffn_br"], a["L1_ffn_W1"],
                 a["L1_ffn_b1"], a["L1_ffn_W2"], a["L1_ffn_b2"].rearrange("e m -> (e m)"), a["L1_ffn_W_c2s"],
                 a["L1_ffn_b_c2s"], a["L1_ffn_W_dec"], a["L1_ffn_b_dec"], a["L1_ffn_ln_g"], a["L1_ffn_ln_b"],
                 ident, ahead, out.rearrange("b s d -> (b s) d"), along(B - 1, 0, NT))


_TURNED = ["L0_xattn_Wq", "L0_xattn_Wk", "L0_xattn_Wv", "L0_xattn_Wo", "L1_xattn_Wq", "L1_xattn_Wk", "L1_xattn_Wv",
           "L1_xattn_Woff", "L1_xattn_Wo"]


def kernel(**inputs):
    import numpy as _np
    import concourse.bacc as _bacc
    from concourse import mybir as _mybir
    from concourse.bass_utils import run_bass_kernel_spmd as _run

    nc = _bacc.Bacc("TRN2", target_bir_lowering=False, num_devices=1)
    arrays, aps = {}, {}
    for name, value in inputs.items():
        v = _np.asarray(value)
        if name in _TURNED:
            name, v = name + "T", v.T
        elif name == "ctx_1024":
            name, v = "ctxT", v.reshape(B * T, D).T
        v = _np.ascontiguousarray(v)
        arrays[f"in_{name}"] = v
        aps[name] = nc.dram_tensor(f"in_{name}", v.shape, _mybir.dt.from_np(v.dtype), kind="ExternalInput").ap()
    out = nc.dram_tensor("out_0", (B, S, D), F32, kind="ExternalOutput").ap()
    program(nc, aps, out)
    r = _run(nc, [arrays], core_ids=[0])
    return r.results[0]["out_0"]
```
